# Optimizing a Trainium2 kernel written in Bass

```python
import numpy as np
import jax
import jax.numpy as jnp

def _softmax(x, axis=-1):
    return jax.nn.softmax(x, axis=axis)

def _gelu(x):
    return jax.nn.gelu(x, approximate=True)

def _silu(x):
    return jax.nn.silu(x)

def _sigmoid(x):
    return jax.nn.sigmoid(x)

def _layernorm(x, axis=-1, eps=1e-05):
    m = jnp.mean(x, axis=axis, keepdims=True)
    v = jnp.var(x, axis=axis, keepdims=True)
    return (x - m) / jnp.sqrt(v + eps)

def _scatter_add(tgt, idx, src, axis=0):
    return tgt.at[idx].add(src)

def _segment_sum(src, seg, n):
    return jax.ops.segment_sum(src, seg, n)
kernel_name = 'mk_flamingo_gated_d1_seqx_r4_d9bd2f'

def setup_inputs(seed: int=0):
    np.random.seed(seed)
    _w = jnp.asarray

    def _rec_inputs():
        import jax
        import jax.numpy as jnp
        _rk = jax.random.key(seed)
        x = -7.109e-05 + 0.9999 * jax.random.normal(jax.random.fold_in(_rk, 1), (4, 1024, 256), jnp.float32)
        _lenS = 1024 - jax.random.randint(jax.random.fold_in(_rk, 7), (4,), 0, max(1, 1024 // 4) + 1, jnp.int32)
        _lenS2 = 154 - jax.random.randint(jax.random.fold_in(_rk, 8), (4,), 0, max(1, 154 // 4) + 1, jnp.int32)
        _ctx_768P = jax.random.normal(jax.random.fold_in(_rk, 11), (4, 16, 192), jnp.float32)
        _ctx_768c = jax.random.dirichlet(jax.random.fold_in(_rk, 511), 0.3 * jnp.ones((16,), jnp.float32), (4, 154))
        _ctx_768t = jnp.einsum('bsk,bkd->bsd', _ctx_768c, _ctx_768P)
        _ctx_768t = _ctx_768t * jax.lax.rsqrt(jnp.mean(jnp.square(_ctx_768t)) + 1e-12) * 0.953939
        ctx_768 = 0.000486113 + 1.00014 * (_ctx_768t + 0.3 * jax.random.normal(jax.random.fold_in(_rk, 611), (4, 154, 192), jnp.float32))
        _g = jax.random.normal(jax.random.fold_in(_rk, 9001), (2, 1), jnp.float32)
        _g = jnp.sign(_g) * jnp.maximum(jnp.abs(_g), 1.0) + (_g == 0) * 1.0
        g_xattn = _g[0]
        g_ffn = _g[1]
        return (x, ctx_768, g_xattn, g_ffn)
    x, ctx_768, g_xattn, g_ffn = _rec_inputs()

    def _L0_xattn_setup():
        import jax, jax.numpy as jnp
        import numpy as np
        HEADS = 16
        DIM_HEAD = 64
        SCALE = DIM_HEAD ** (-0.5)
        key = jax.random.key(seed)
        ks = jax.random.split(key, 7)
        B, Nq, Dq = (16, 1024, 256)
        Nc, Dc = (77, 192)
        inner = HEADS * DIM_HEAD
        return {'x': jax.random.normal(ks[0], (B, Nq, Dq), jnp.float32), 'context': jax.random.normal(ks[1], (B, Nc, Dc), jnp.float32), 'Wq': jax.random.normal(ks[2], (Dq, inner), jnp.float32) * Dq ** (-0.5), 'Wk': jax.random.normal(ks[3], (Dc, inner), jnp.float32) * Dc ** (-0.5), 'Wv': jax.random.normal(ks[4], (Dc, inner), jnp.float32) * Dc ** (-0.5), 'Wo': jax.random.normal(ks[5], (inner, Dq), jnp.float32) * inner ** (-0.5), 'bo': jnp.zeros((Dq,), jnp.float32)}
    _L0_xattn_all = _L0_xattn_setup()
    _L0_xattn_in = {k: v for k, v in _L0_xattn_all.items() if k in ('Wq', 'Wk', 'Wv', 'Wo', 'bo')}
    del _L0_xattn_all

    def _L0_ffn_setup():
        import jax, jax.numpy as jnp
        import numpy as np
        B, T, C, H, E = (1, 64, 256, 512, 8)
        STD = 0.02
        key = jax.random.key(seed)
        ks = jax.random.split(key, 8)
        f32 = jnp.float32
        return {'x': jax.random.normal(ks[0], (B, T, C), f32), 'up': jax.random.normal(ks[1], (E, H, C), f32) * STD, 'gate': jax.random.normal(ks[2], (E, H, C), f32) * STD, 'down': jax.random.normal(ks[3], (E, C, H), f32) * STD, 'router': jax.random.normal(ks[4], (E, C), f32) * STD, 'w_up_s': jax.random.normal(ks[5], (H, C), f32) * STD, 'w_gate_s': jax.random.normal(ks[6], (H, C), f32) * STD, 'w_down_s': jax.random.normal(ks[7], (C, H), f32) * STD}
    _L0_ffn_all = _L0_ffn_setup()
    _L0_ffn_in = {k: v for k, v in _L0_ffn_all.items() if k in ('up', 'gate', 'down', 'router', 'w_up_s', 'w_gate_s', 'w_down_s')}
    del _L0_ffn_all
    return {'x': x, 'ctx_768': ctx_768, 'g_xattn': g_xattn, 'g_ffn': g_ffn, 'L0_xattn_Wq': _L0_xattn_in['Wq'], 'L0_xattn_Wk': _L0_xattn_in['Wk'], 'L0_xattn_Wv': _L0_xattn_in['Wv'], 'L0_xattn_Wo': _L0_xattn_in['Wo'], 'L0_xattn_bo': _L0_xattn_in['bo'], 'L0_ffn_up': _L0_ffn_in['up'], 'L0_ffn_gate': _L0_ffn_in['gate'], 'L0_ffn_down': _L0_ffn_in['down'], 'L0_ffn_router': _L0_ffn_in['router'], 'L0_ffn_w_up_s': _L0_ffn_in['w_up_s'], 'L0_ffn_w_gate_s': _L0_ffn_in['w_gate_s'], 'L0_ffn_w_down_s': _L0_ffn_in['w_down_s']}

def reference(x, ctx_768, g_xattn, g_ffn, L0_xattn_Wq, L0_xattn_Wk, L0_xattn_Wv, L0_xattn_Wo, L0_xattn_bo, L0_ffn_up, L0_ffn_gate, L0_ffn_down, L0_ffn_router, L0_ffn_w_up_s, L0_ffn_w_gate_s, L0_ffn_w_down_s):
    import jax
    import jax.numpy as jnp

    def _L0_xattn_ref(x, context, Wq, Wk, Wv, Wo, bo):
        import jax, jax.numpy as jnp
        import numpy as np
        HEADS = 16
        DIM_HEAD = 64
        SCALE = DIM_HEAD ** (-0.5)
        B, Nq, _ = x.shape
        Nc = context.shape[1]
        q = (x @ Wq).reshape(B, Nq, HEADS, DIM_HEAD).transpose(0, 2, 1, 3)
        k = (context @ Wk).reshape(B, Nc, HEADS, DIM_HEAD).transpose(0, 2, 1, 3)
        v = (context @ Wv).reshape(B, Nc, HEADS, DIM_HEAD).transpose(0, 2, 1, 3)
        sim = jnp.einsum('bhid,bhjd->bhij', q, k) * SCALE
        attn = jax.nn.softmax(sim, axis=-1)
        out = jnp.einsum('bhij,bhjd->bhid', attn, v)
        out = out.transpose(0, 2, 1, 3).reshape(B, Nq, HEADS * DIM_HEAD)
        return out @ Wo + bo

    def _L0_ffn_ref(x, up, gate, down, router, w_up_s, w_gate_s, w_down_s):
        import jax, jax.numpy as jnp
        import numpy as np
        B, T, C, H, E = (1, 64, 256, 512, 8)
        STD = 0.02
        b, t, c = x.shape
        x_ = x.reshape(b * t, c)
        logits = x_ @ router.T
        idx = jnp.argmax(logits, axis=-1)
        onehot = jax.nn.one_hot(idx, router.shape[0], dtype=x.dtype)
        u = jnp.einsum('bc,ehc->ebh', x_, up)
        g = jnp.einsum('bc,ehc->ebh', x_, gate)
        h = jax.nn.silu(g) * u
        ye = jnp.einsum('ebh,ech->ebc', h, down)
        y = jnp.einsum('ebc,be->bc', ye, onehot)
        ys = jax.nn.silu(x_ @ w_gate_s.T) * (x_ @ w_up_s.T) @ w_down_s.T
        return (y + ys).reshape(b, t, c)
    x = x + jnp.tanh(g_xattn[0]) * _L0_xattn_ref(_layernorm(x, axis=-1), ctx_768, L0_xattn_Wq, L0_xattn_Wk, L0_xattn_Wv, L0_xattn_Wo, L0_xattn_bo)
    x = x + jnp.tanh(g_ffn[0]) * _L0_ffn_ref(_layernorm(x, axis=-1), L0_ffn_up, L0_ffn_gate, L0_ffn_down, L0_ffn_router, L0_ffn_w_up_s, L0_ffn_w_gate_s, L0_ffn_w_down_s)
    return x

_drawn_inputs = setup_inputs


def setup_inputs(seed=0):
    import zlib

    import numpy as np

    out = dict(_drawn_inputs(seed))
    spreads = {'L0_xattn_bo': (0.0, 0.1)}
    factors = {'L0_ffn_up': 2.686,
     'L0_ffn_gate': 2.675,
     'L0_ffn_router': 2.84,
     'L0_ffn_w_up_s': 2.675,
     'L0_ffn_w_gate_s': 2.693,
     'L0_ffn_w_down_s': 2.67}
    for name, (base, spread) in spreads.items():
        noise = np.random.default_rng([zlib.crc32(name.encode()), seed]).standard_normal(out[name].shape)
        drawn = base * np.exp(spread * noise) if base else spread * noise
        out[name] = jnp.asarray(drawn.astype(out[name].dtype))
    for name, factor in factors.items():
        out[name] = (out[name] * factor).astype(out[name].dtype)
    return out
```

```python
from contextlib import ExitStack

import concourse.bass as bass
from concourse import mybir

P = 128
ALU = mybir.AluOpType
ACT = mybir.ActivationFunctionType
F32 = mybir.dt.float32
F32R = mybir.dt.float32r
I32 = mybir.dt.int32
BF16 = mybir.dt.bfloat16
AX_X = mybir.AxisListType.X

EPS = 1e-5
TILES = 4
BLK = TILES * P


def attention(nc, x, ctxT, g_xattn, Wq, Wk, Wv, Wo, bo, x1_dram, xn2_dram):
    B, Nq, D = x.shape
    DC, KEYS = ctxT.shape[1:]
    INNER = Wq.shape[1]
    PAIRS = INNER // P
    DH = P // 2
    SCALE = float(DH) ** -0.5
    NC = D // P
    KP = DC // 2
    PK = 2 * KEYS
    NB = B * Nq // BLK
    KA = (PK - P) // 2
    CH = [(0, KA), (KA, P), (KA + P, KA)]
    MID = KEYS - KA
    assert MID == DH and PAIRS == 8 and NC == 2 and Nq == 2 * BLK

    with ExitStack() as ctx:
        def sb(name, shape, dt=F32):
            return ctx.enter_context(nc.sbuf_tensor(name, shape, dt))

        def sem(name):
            return ctx.enter_context(nc.semaphore(name))

        wq = [sb(f"wq_{s}", [P, NC, INNER], F32R) for s in ("hi", "lo")]
        wk = [sb(f"wk_{s}", [KP, 2, INNER], F32R) for s in ("hi", "lo")]
        wv = [sb(f"wv_{s}", [KP, 2, INNER], F32R) for s in ("hi", "lo")]
        wo = [sb(f"wo_{s}", [P, PAIRS, D], F32R) for s in ("hi", "lo")]
        cx = [sb(f"cx_{s}", [KP, 2, KEYS + P], F32R) for s in ("hi", "lo")]
        cx_raw = sb("cx_raw", [KP, 2, KEYS + P])
        kst = [sb(f"kst_{s}", [P, PAIRS, PK], F32R) for s in ("hi", "lo")]
        VW = 3 * DH + P
        vst = [sb(f"vst_{s}", [P, PAIRS, VW], F32R) for s in ("hi", "lo")]
        qT = [sb(f"qT_{s}", [P, 4, BLK], F32R) for s in ("hi", "lo")]
        prob = sb("prob", [P, 3, TILES, PK])
        pT = [sb(f"pT_{s}", [P, 3, BLK], F32R) for s in ("hi", "lo")]
        oT = [sb(f"oT_{s}", [P, PAIRS, BLK], F32R) for s in ("hi", "lo")]
        xw = sb("xw", [P, 3, TILES, D])
        xn = xw[:, 2]
        xT = [sb(f"xT_{s}", [P, NC, BLK], F32R) for s in ("hi", "lo")]
        ident = sb("ident", [P, P])
        tbo = sb("tbo", [P, D])
        gate = sb("gate", [P, 1])
        tg = sb("tg", [P, 1])
        nmax = sb("nmax", [P, 3, TILES, 2])
        den = sb("den", [P, 3, TILES, 2])
        rden = sb("rden", [P, 3, TILES, 2])
        st = [sb(f"st{i}", [P, TILES, 6]) for i in range(2)]
        mv = [sb(f"mv{i}", [P, TILES, 2]) for i in range(2)]
        sc = [sb(f"sc{i}", [P, 5, TILES]) for i in range(2)]

        ps = ctx.enter_context(nc.psum_tensor("ps", [P, 8, 512], F32))
        BT, BQ, BV = 4, 6, 7

        V_PARTS = [(slice(0, KA), slice(0, DH), BQ), (slice(0, DH), slice(3 * DH, 4 * DH), BV),
                   (slice(DH, P), slice(4 * DH, 5 * DH), BT), (slice(0, KA), slice(2 * DH, 3 * DH), BT + 1)]

        stage = [prob[:, :].rearrange("p a t k -> p (a t k)")[:, 0:2048],
                 xw[:, 1:3].rearrange("p a t c -> p (a t c)")]
        w_in = [sem(f"w{i}_in") for i in range(4)]
        ident0 = sem("ident0"); ident_done = sem("ident_done"); zeroed = sem("zeroed")
        w_hi = sem("w_hi"); w_lo = sem("w_lo")
        gate_in = sem("gate_in"); tg_done = sem("tg_done"); tbo_done = sem("tbo_done")
        cx_in = sem("cx_in"); cx_hi = sem("cx_hi"); cx_lo = sem("cx_lo")
        kv_done = sem("kv_done"); kv_hi = sem("kv_hi"); kv_lo = sem("kv_lo")
        x_in = sem("x_in"); ln1 = sem("ln1"); xn_done = sem("xn_done"); xb_done = sem("xb_done")
        xt_done = sem("xt_done"); xt_hi = sem("xt_hi"); xt_lo = sem("xt_lo")
        q_done = sem("q_done"); q_hi = sem("q_hi"); q_lo = sem("q_lo")
        s_done = sem("s_done"); max_done = sem("max_done"); exp_done = sem("exp_done")
        rden_done = sem("rden_done"); p_done = sem("p_done")
        t_done = sem("t_done"); pt_hi = sem("pt_hi"); pt_lo = sem("pt_lo")
        pv_done = sem("pv_done"); o_hi = sem("o_hi"); o_lo = sem("o_lo")
        wo_done = sem("wo_done"); x1_done = sem("x1_done"); ln2 = sem("ln2"); xn2_done = sem("xn2_done")
        x1_out = sem("x1_out"); xn2_out = sem("xn2_out")
        chain = sem("chain"); pool_go = sem("pool_go"); dve_go = sem("dve_go")

        xb = x.rearrange("b (k t p) c -> (b k) p t c", t=TILES, p=P)
        x1b = x1_dram.rearrange("(n t p) c -> n p t c", t=TILES, p=P)
        xn2b = xn2_dram.rearrange("(n t p) c -> n p t c", t=TILES, p=P)
        cxb = ctxT.rearrange("b (k p) s -> b p k s", p=KP)

        block = ctx.enter_context(nc.Block())

        @block.sync
        def _(sp):
            def load_ctx(b):
                sp.wait_ge(cx_lo, b)
                sp.dma_start(cx_raw[:, :, 0:KEYS], cxb[b]).then_inc(cx_in, 16)
                sp.dma_start(cx_raw[:, :, KEYS:KEYS + MID], cxb[b, :, :, KA:KEYS]).then_inc(cx_in, 16)
                sp.dma_start(cx_raw[:, :, KEYS + MID:KEYS + P], cxb[b, :, :, 0:MID]).then_inc(cx_in, 16)

            cx_first = cxb[0]
            for i, (w, p) in enumerate(((Wk, KP), (Wv, KP))):
                sp.dma_start(stage[i][0:p].rearrange("p (k n) -> p k n", k=2),
                             w.rearrange("(k p) n -> p k n", p=p)).then_inc(w_in[i], 16)
            sp.dma_start(gate[:, :], g_xattn.rearrange("(a b) -> a b", a=1).broadcast_to([P, 1])).then_inc(gate_in, 16)
            sp.dma_start(tbo[:, :], bo.rearrange("(a b) -> a b", a=1).broadcast_to([P, D])).then_inc(gate_in, 16)
            sp.dma_start(cx_raw[:, :, 0:KEYS], cx_first).then_inc(cx_in, 16)
            sp.dma_start(cx_raw[:, :, KEYS:KEYS + MID], cx_first[:, :, KA:KEYS]).then_inc(cx_in, 16)
            sp.dma_start(cx_raw[:, :, KEYS + MID:KEYS + P], cx_first[:, :, 0:MID]).then_inc(cx_in, 16)
            sp.dma_start(xw[:, 0], xb[0]).then_inc(x_in, 16)
            for i, (w, m) in ((2, (Wq, NC)), (3, (Wo, PAIRS))):
                sp.wait_ge(w_lo, i - 1)
                sp.dma_start(stage[i % 2].rearrange("p (k n) -> p k n", k=m),
                             w.rearrange("(k p) n -> p k n", p=P)).then_inc(w_in[i], 16)
            sp.wait_ge(w_lo, 4)

            def block_io(n, k, more):
                if more:
                    sp.wait_ge(x1_out, 16 * n + 1)
                    sp.dma_start(xw[:, 1 - k], xb[n + 1]).then_inc(x_in, 16)
                sp.wait_ge(x1_done, 4 * n + 8)
                sp.dma_start(x1b[n], xw[:, k]).then_inc(x1_out, 16)
                sp.wait_ge(xn2_done, n + 2)
                sp.dma_start(xn2b[n], xn).then_inc(xn2_out, 16)

            sp.sem_inc(x1_out, 1)
            with sp.Fori(0, B - 1) as b:
                block_io(2 * b, 0, True)
                load_ctx(b + 1)
                block_io(2 * b + 1, 1, True)
            block_io(NB - 2, 0, True)
            block_io(NB - 1, 1, False)
            sp.wait_ge(x1_out, 16 * NB + 1)
            sp.wait_ge(xn2_out, 16 * NB + 1)

        @block.gpsimd
        def _(pool):
            pool.memset(ident[:, :], 0.0).then_inc(ident0, 1)
            pool.wait_ge(ident0, 1)
            pool.affine_select(out=ident[:, :], in_=ident[:, :], compare_op=ALU.not_equal, fill=1.0,
                               base=0, pattern=[[-1, P]], channel_multiplier=1).then_inc(ident_done, 1)
            for s in range(2):
                pool.memset(kst[s][:, :, :].bitcast(F32), 0.0).then_inc(zeroed, 1)
                pool.memset(vst[s][:, :, :].bitcast(F32), 0.0).then_inc(zeroed, 1)
            pool.wait_ge(tbo_done, 1)

            def apply_ln1(n, k, stored):
                pool.wait_ge(ln1, n + 1)
                if stored:
                    pool.wait_ge(xn2_out, 16 * stored[0] + 1)
                pool.sem_inc(pool_go, 1)
                for t in range(TILES):
                    pool.tensor_scalar(xn[:, t, :], xw[:, k, t, :], sc[0][:, 3, t:t + 1], sc[0][:, 4, t:t + 1],
                                       ALU.mult, ALU.add).then_inc(xn_done, 1)
                pool.wait_ge(xn_done, 4 * n + 5)
                pool.tensor_tensor(xw[:, k], xw[:, k], tbo[:, :].unsqueeze(1).broadcast_to([P, TILES, D]),
                                   ALU.add).then_inc(xb_done, 1)

            def apply_ln2(n, k, last):
                pool.wait_ge(ln2, n + 1)
                pool.wait_ge(xn2_out, 16 * n + 1)
                pool.wait_ge(xt_done, 2 * n + (2 if last else 4))
                pool.sem_inc(pool_go, 1)
                for t in range(TILES):
                    i = pool.tensor_scalar(xn[:, t, :], xw[:, k, t, :], sc[1][:, 3, t:t + 1], sc[1][:, 4, t:t + 1],
                                           ALU.mult, ALU.add)
                i.then_inc(xn2_done, 1)

            def normalise(n, p):
                pool.wait_ge(rden_done, 8 * n + p + 1)
                pool.tensor_tensor(prob[:, p % 3].rearrange("p t (h k) -> p (t h) k", h=2),
                                   prob[:, p % 3].rearrange("p t (h k) -> p (t h) k", h=2),
                                   rden[:, p % 3].rearrange("p t h -> p (t h)").unsqueeze(2)
                                   .broadcast_to([P, 2 * TILES, KEYS]), ALU.mult).then_inc(p_done, 1)

            pool.sem_inc(xn2_out, 1)
            pool.sem_inc(xn_done, 1)
            pool.sem_inc(xn2_done, 1)
            pool.wait_ge(w_lo, 4)
            apply_ln1(0, 0, None)

            def blk(n, k, last):
                for p in range(PAIRS):
                    normalise(n, p)
                    if p == 6 and not last:
                        apply_ln1(n + 1, 1 - k, [n])
                apply_ln2(n, k, last)

            with pool.Fori(0, B - 1) as b:
                blk(2 * b, 0, False)
                blk(2 * b + 1, 1, False)
            blk(NB - 2, 0, False)
            blk(NB - 1, 1, True)

        @block.scalar
        def _(act):
            act.sem_inc(exp_done, 4)
            act.wait_ge(gate_in, 32)
            act.activation(tg[:, :], gate[:, :], ACT.Tanh).then_inc(tg_done, 1)
            for i, (w, p) in enumerate(((wk, KP), (wv, KP), (wq, P), (wo, P))):
                act.wait_ge(w_in[i], 16)
                act.copy(w[0][:, :, :].rearrange("p k n -> p (k n)"), stage[i % 2][0:p]).then_inc(w_hi, 1)

            def xt_high(n, c):
                act.wait_ge(xt_done, 2 * n + c + 1)
                act.copy(xT[0][:, c, :], ps[:, BQ, :]).then_inc(xt_hi, 1)

            def q_high(n, p):
                act.wait_ge(q_done, 8 * n + p + 1)
                act.copy(qT[0][:, p % 4, :], ps[:, BQ, :]).then_inc(q_hi, 1)

            def exps(n, p, t):
                act.wait_ge(max_done, 4 * (8 * n + p) + t + 1)
                if t == 0:
                    act.wait_ge(t_done, 3 * (8 * n + max(p - 2, 0)) + 4)
                for h in range(2):
                    i = act.activation(prob[:, p % 3, t, h * KEYS:(h + 1) * KEYS], ps[:, t, h * KEYS:(h + 1) * KEYS],
                                       ACT.Exp, bias=nmax[:, p % 3, t, h:h + 1],
                                       accum_out=den[:, p % 3, t, h:h + 1])
                i.then_inc(exp_done, 1)

            def pt_high(n, p, c):
                act.wait_ge(t_done, 3 * (8 * n + p) + c + 5)
                act.copy(pT[0][0:CH[c][1], c, :], ps[0:CH[c][1], BT + (3 * p + c) % 2, :]).then_inc(pt_hi, 1)

            def o_high(n, p):
                act.wait_ge(pv_done, 8 * n + p + 1)
                act.copy(oT[0][:, p, :], ps[:, BV, :]).then_inc(o_hi, 1)

            def kv_high(b):
                act.wait_ge(kv_done, 8 * b + 1)
                act.wait_ge(cx_in, 48 * b + 48)
                act.copy(cx[0][:, :, :], cx_raw[:, :, :]).then_inc(cx_hi, 1)
                for j in range(4):
                    act.wait_ge(kv_done, 8 * b + j + 2)
                    for h in range(2):
                        r = slice(h * DH, (h + 1) * DH)
                        i = act.activation(kst[0][r, 2 * j:2 * j + 2, h * KEYS:(h + 1) * KEYS],
                                           ps[r, BT + j % 2, 0:PK].rearrange("p (a k) -> p a k", a=2),
                                           ACT.Copy, scale=SCALE)
                    i.then_inc(kv_hi, 1)
                for j, (r, c, bank) in enumerate(V_PARTS):
                    act.wait_ge(kv_done, 8 * b + j + 6)
                    act.copy(vst[0][r, :, c], ps[r, bank, :].rearrange("p (a d) -> p a d", d=DH)).then_inc(kv_hi, 1)

            act.wait_ge(zeroed, 4)
            act.wait_ge(tg_done, 1)
            for c in range(NC):
                xt_high(0, c)
            for p in range(2):
                q_high(0, p)

            def blk(n, b, k, last):
                if k == 0:
                    kv_high(b)
                exps(n, 0, 0)
                exps(n, 0, 1)
                q_high(n, 2)
                exps(n, 0, 2)
                exps(n, 0, 3)
                q_high(n, 3)
                for t in range(TILES):
                    exps(n, 1, t)
                for p in range(PAIRS):
                    ex = p + 2 < PAIRS
                    pt_high(n, p, 0)
                    if ex:
                        exps(n, p + 2, 0)
                    pt_high(n, p, 1)
                    if ex:
                        exps(n, p + 2, 1)
                        exps(n, p + 2, 2)
                    pt_high(n, p, 2)
                    if ex:
                        exps(n, p + 2, 3)
                    if p + 4 < PAIRS:
                        q_high(n, p + 4)
                    if p >= 6 and not last:
                        xt_high(n + 1, p - 6)
                    o_high(n, p)
                if not last:
                    for p in range(2):
                        q_high(n + 1, p)

            with act.Fori(0, B - 1) as b:
                blk(2 * b, b, 0, False)
                blk(2 * b + 1, b, 1, False)
            blk(NB - 2, B - 1, 0, False)
            blk(NB - 1, B - 1, 1, True)

        @block.vector
        def _(dve):


            def low(out, src, hi, done):
                dve.tensor_tensor(out, src, hi.bitcast(F32), ALU.subtract).then_inc(done, 1)

            dve.sem_inc(x1_done, 4)
            dve.sem_inc(o_lo, 1)
            dve.wait_ge(tg_done, 1)
            dve.tensor_scalar(tbo[:, :], tbo[:, :], tg[:, 0:1], None, ALU.mult).then_inc(tbo_done, 1)
            for i, (w, p) in enumerate(((wk, KP), (wv, KP), (wq, P), (wo, P))):
                dve.wait_ge(w_hi, i + 1)
                low(w[1][:, :, :].rearrange("p k n -> p (k n)"), stage[i % 2][0:p],
                    w[0][:, :, :].rearrange("p k n -> p (k n)"), w_lo)

            NEWTON = 3
            STAT = 4 + 3 * NEWTON

            def rstd(which, base, done):
                v, m, s = mv[which][:, :, 1], mv[which][:, :, 0], sc[which]
                dve.wait_ge(chain, base)
                dve.tensor_scalar(s[:, 0, :], v, EPS, None, ALU.add).then_inc(chain, 1)
                dve.wait_ge(chain, base + 1)
                dve.tensor_scalar(s[:, 1, :].bitcast(I32), s[:, 0, :].bitcast(I32), -0.5, float(0x5f3759df),
                                  ALU.mult, ALU.add).then_inc(chain, 1)
                for i in range(NEWTON):
                    out = s[:, 1 if i < NEWTON - 1 else 3, :]
                    dve.wait_ge(chain, base + 3 * i + 2)
                    dve.tensor_tensor(s[:, 2, :], s[:, 1, :], s[:, 1, :], ALU.mult).then_inc(chain, 1)
                    dve.wait_ge(chain, base + 3 * i + 3)
                    dve.scalar_tensor_tensor(s[:, 2, :], s[:, 2, :], -0.5, s[:, 0, :], ALU.mult, ALU.mult)\
                       .then_inc(chain, 1)
                    dve.wait_ge(chain, base + 3 * i + 4)
                    dve.scalar_tensor_tensor(out, s[:, 2, :], 1.5, s[:, 1, :], ALU.add, ALU.mult).then_inc(chain, 1)
                dve.wait_ge(chain, base + 3 * NEWTON + 2)
                dve.scalar_tensor_tensor(s[:, 4, :], m, -1.0, s[:, 3, :], ALU.mult, ALU.mult).then_inc(done, 1)

            def stats1(n, k):
                dve.wait_ge(x_in, 16 * n + 16)
                dve.wait_ge(xn_done, 4 * n + 1)
                for t in range(TILES):
                    i = dve.bn_stats(st[0][:, t, :], xw[:, k, t, :])
                i.then_inc(chain, 1)
                dve.wait_ge(chain, 2 * STAT * n + 1)
                dve.sem_inc(dve_go, 1)
                for t in range(TILES):
                    i = dve.bn_aggr(mv[0][:, t, :], st[0][:, t, :])
                i.then_inc(chain, 1)
                rstd(0, 2 * STAT * n + 2, ln1)

            def q_low(n, p):
                dve.wait_ge(q_hi, 8 * n + p + 1)
                low(qT[1][:, p % 4, :], ps[:, BQ, :], qT[0][:, p % 4, :], q_lo)

            def xt_low(n, c):
                dve.wait_ge(xt_hi, 2 * n + c + 1)
                low(xT[1][:, c, :], ps[:, BQ, :], xT[0][:, c, :], xt_lo)

            def maxima(n, p, t):
                dve.wait_ge(s_done, 4 * (8 * n + p) + t + 1)
                dve.tensor_reduce(nmax[:, p % 3, t, :], ps[:, t, 0:PK].rearrange("p (h k) -> p h k", h=2),
                                  AX_X, ALU.max, negate=True).then_inc(max_done, 1)

            def recip(n, p):
                dve.wait_ge(exp_done, 4 * (8 * n + p) + 8)
                dve.reciprocal(rden[:, p % 3], den[:, p % 3]).then_inc(rden_done, 1)

            def pt_low(n, p, c):
                dve.wait_ge(pt_hi, 3 * (8 * n + p) + c + 1)
                r = slice(0, CH[c][1])
                low(pT[1][r, c, :], ps[r, BT + (3 * p + c) % 2, :], pT[0][r, c, :], pt_lo)

            def o_low(n, p):
                dve.wait_ge(o_hi, 8 * n + p + 1)
                low(oT[1][:, p, :], ps[:, BV, :], oT[0][:, p, :], o_lo)

            def kv_low(b):
                dve.wait_ge(cx_hi, b + 1)
                low(cx[1][:, :, :], cx_raw[:, :, :], cx[0][:, :, :], cx_lo)
                for j in range(4):
                    dve.wait_ge(kv_hi, 8 * b + j + 1)
                    for h in range(2):
                        r = slice(h * DH, (h + 1) * DH)
                        part = kst[0][r, 2 * j:2 * j + 2, h * KEYS:(h + 1) * KEYS]
                        i = dve.scalar_tensor_tensor(kst[1][r, 2 * j:2 * j + 2, h * KEYS:(h + 1) * KEYS],
                                                     ps[r, BT + j % 2, 0:PK].rearrange("p (a k) -> p a k", a=2),
                                                     SCALE, part.bitcast(F32), ALU.mult, ALU.subtract)
                    i.then_inc(kv_lo, 1)
                for j, (r, c, bank) in enumerate(V_PARTS):
                    dve.wait_ge(kv_hi, 8 * b + j + 5)
                    low(vst[1][r, :, c], ps[r, bank, :].rearrange("p (a d) -> p a d", d=DH), vst[0][r, :, c], kv_lo)

            def residual(n, k):
                dve.wait_ge(xb_done, n + 1)
                for t in range(TILES):
                    dve.wait_ge(wo_done, 4 * n + t + 1)
                    dve.scalar_tensor_tensor(xw[:, k, t, :], ps[:, t, 0:D], tg[:, 0:1], xw[:, k, t, :],
                                             ALU.mult, ALU.add).then_inc(x1_done, 1)
                dve.wait_ge(xn2_done, n + 1)
                dve.wait_ge(x1_done, 4 * n + 8)
                for t in range(TILES):
                    i = dve.bn_stats(st[1][:, t, :], xw[:, k, t, :])
                i.then_inc(chain, 1)
                dve.wait_ge(chain, 2 * STAT * n + 3 * STAT + 1)
                dve.sem_inc(dve_go, 1)
                for t in range(TILES):
                    i = dve.bn_aggr(mv[1][:, t, :], st[1][:, t, :])
                i.then_inc(chain, 1)
                rstd(1, 2 * STAT * n + 3 * STAT + 2, ln2)

            stats1(0, 0)
            dve.sem_inc(chain, STAT)
            dve.wait_ge(zeroed, 4)
            for c in range(NC):
                xt_low(0, c)
            for p in range(2):
                q_low(0, p)

            def blk(n, b, k, last):
                if k == 0:
                    kv_low(b)
                for t in range(TILES):
                    maxima(n, 0, t)
                q_low(n, 2)
                recip(n, 0)
                q_low(n, 3)
                for t in range(TILES):
                    maxima(n, 1, t)
                recip(n, 1)
                for p in range(PAIRS):
                    ex = p + 2 < PAIRS
                    if ex:
                        maxima(n, p + 2, 0)
                    pt_low(n, p, 0)
                    if ex:
                        maxima(n, p + 2, 1)
                    pt_low(n, p, 1)
                    if ex:
                        maxima(n, p + 2, 2)
                    pt_low(n, p, 2)
                    if ex:
                        maxima(n, p + 2, 3)
                    if p + 4 < PAIRS:
                        q_low(n, p + 4)
                    if ex:
                        recip(n, p + 2)
                    if p == 5 and not last:
                        stats1(n + 1, 1 - k)
                    if p >= 6 and not last:
                        xt_low(n + 1, p - 6)
                    o_low(n, p)
                if not last:
                    for p in range(2):
                        q_low(n + 1, p)
                else:
                    dve.sem_inc(chain, STAT)
                residual(n, k)

            with dve.Fori(0, B - 1) as b:
                blk(2 * b, b, 0, False)
                blk(2 * b + 1, b, 1, False)
            blk(NB - 2, B - 1, 0, False)
            blk(NB - 1, B - 1, 1, True)

        @block.tensor
        def _(pe):
            def mm3(out, parts, first, last):
                n = 3 * len(parts)
                i = 0
                for a, b in parts:
                    for u, v in ((a[0], b[0]), (a[0], b[1]), (a[1], b[0])):
                        r = pe.matmul(out, u, v, start=first and i == 0, stop=last and i == n - 1)
                        i += 1
                return r

            def cut(pair, *key):
                return [w[key] for w in pair]

            ALLP = slice(None)

            def transposes(n, c):
                if c == 0:
                    pe.wait_ge(xn_done, 4 * n + 5)
                else:
                    pe.wait_ge(xt_lo, 2 * n + 1)
                for t in range(TILES):
                    i = pe.transpose(ps[:, BQ, t * P:(t + 1) * P], xn[:, t, c * P:(c + 1) * P], ident[:, :])
                i.then_inc(xt_done, 1)

            def project_q(n, p):
                mm3(ps[:, BQ, :], [(cut(wq, ALLP, c, slice(p * P, (p + 1) * P)), cut(xT, ALLP, c, ALLP))
                                   for c in range(NC)], True, True).then_inc(q_done, 1)

            def scores(n, p, t):
                pe.wait_ge(exp_done, 4 * (8 * n + p) + t + 1)
                mm3(ps[:, t, 0:PK], [(cut(qT, ALLP, p % 4, slice(t * P, (t + 1) * P)), cut(kst, ALLP, p, ALLP))],
                    True, True).then_inc(s_done, 1)

            def transpose_p(n, p, c):
                c0, m = CH[c]
                for t in range(TILES):
                    i = pe.transpose(ps[0:m, BT + (3 * p + c) % 2, t * P:(t + 1) * P],
                                     prob[:, p % 3, t, c0:c0 + m], ident[:, :])
                i.then_inc(t_done, 1)

            def values(n, p, c):
                m = CH[c][1]
                pe.wait_ge(pt_lo, 3 * (8 * n + p) + c + 1)
                cols = (slice(0, P), slice(3 * DH, 3 * DH + P), slice(DH, DH + P))[c]
                i = mm3(ps[:, BV, :], [(cut(vst, slice(0, m), p, cols), cut(pT, slice(0, m), c, ALLP))],
                        c == 0, c == 2)
                if c == 2:
                    i.then_inc(pv_done, 1)

            def out_proj(n, t, last):
                for p in range(PAIRS):
                    if t == 0 and p >= PAIRS - 2:
                        pe.wait_ge(o_lo, 8 * n + p + 2)
                    i = mm3(ps[:, t, 0:D], [(cut(oT, ALLP, p, slice(t * P, (t + 1) * P)), cut(wo, ALLP, p, ALLP))],
                            p == 0, p == PAIRS - 1)
                i.then_inc(wo_done, 1)

            def project_kv(n, b):
                pe.wait_ge(cx_lo, b + 1)
                for j in range(4):
                    if j >= 2:
                        pe.wait_ge(kv_lo, 8 * b + j - 1)
                    for a in range(2):
                        p = 2 * j + a
                        i = mm3(ps[:, BT + j % 2, a * KEYS:(a + 1) * KEYS],
                                [(cut(wk, ALLP, c, slice(p * P, (p + 1) * P)), cut(cx, ALLP, c, slice(0, KEYS)))
                                 for c in range(2)], True, True)
                    i.then_inc(kv_done, 1)
                keys = (slice(0, KA), slice(KEYS, KEYS + P), slice(KEYS, KEYS + P), slice(MID, KEYS))
                for j, (s, odd) in enumerate(zip(keys, (0, 0, 1, 1))):
                    m = s.stop - s.start
                    if j >= 2:
                        pe.wait_ge(kv_lo, 8 * b + j + 1)
                    rhs = [[w[:, c, :].rearrange("p (a two d) -> p two a d", two=2, d=DH)[:, odd] for w in wv]
                           for c in range(2)]
                    mm3(ps[0:m, V_PARTS[j][2], :].rearrange("p (a d) -> p a d", d=DH),
                        [(cut(cx, ALLP, c, s), rhs[c]) for c in range(2)], True, True).then_inc(kv_done, 1)

            pe.sem_inc(kv_done, 1)
            pe.sem_inc(t_done, 4)
            pe.wait_ge(ident_done, 1)
            transposes(0, 0)
            transposes(0, 1)
            pe.wait_ge(w_lo, 4)
            pe.wait_ge(xt_lo, 2)
            project_q(0, 0)
            pe.wait_ge(q_lo, 1)
            project_q(0, 1)

            def blk(n, b, k, last):
                if k == 0:
                    pe.wait_ge(q_lo, 8 * n + 2)
                    project_kv(n, b)
                    pe.wait_ge(kv_lo, 8 * b + 4)
                else:
                    pe.wait_ge(q_lo, 8 * n + 2)
                for t in range(TILES):
                    pe.wait_ge(x1_done, 4 * n + t + 1)
                    scores(n, 0, t)
                if k == 0:
                    pe.wait_ge(kv_lo, 8 * b + 8)
                project_q(n, 2)
                pe.wait_ge(q_lo, 8 * n + 3)
                project_q(n, 3)
                for t in range(TILES):
                    scores(n, 1, t)
                for p in range(PAIRS):
                    ex = p + 2 < PAIRS
                    if ex:
                        pe.wait_ge(q_lo, 8 * n + p + 3)
                        scores(n, p + 2, 0)
                    pe.wait_ge(p_done, 8 * n + p + 1)
                    transpose_p(n, p, 0)
                    if ex:
                        scores(n, p + 2, 1)
                    transpose_p(n, p, 1)
                    if ex:
                        scores(n, p + 2, 2)
                    pe.wait_ge(o_lo, 8 * n + p + 1)
                    values(n, p, 0)
                    transpose_p(n, p, 2)
                    if ex:
                        scores(n, p + 2, 3)
                    values(n, p, 1)
                    if p + 4 < PAIRS:
                        pe.wait_ge(q_lo, 8 * n + p + 4)
                        project_q(n, p + 4)
                    if p >= 6 and not last:
                        if p == 6:
                            pe.wait_ge(q_lo, 8 * n + 8)
                        transposes(n + 1, p - 6)
                    values(n, p, 2)
                if not last:
                    pe.wait_ge(xt_lo, 2 * n + 4)
                    project_q(n + 1, 0)
                out_proj(n, 0, last)
                if not last:
                    pe.wait_ge(q_lo, 8 * n + 9)
                    project_q(n + 1, 1)
                for t in range(1, TILES):
                    out_proj(n, t, last)

            with pe.Fori(0, B - 1) as b:
                blk(2 * b, b, 0, False)
                blk(2 * b + 1, b, 1, False)
            blk(NB - 2, B - 1, 0, False)
            blk(NB - 1, B - 1, 1, True)


def feed_forward(nc, comb, x1_dram, g_ffn, gateT, upT, downT, routerT, gate_sT, up_sT, down_sT, out):
    T, D2 = comb.shape
    D = D2 // 2
    E, _, H = gateT.shape
    NC, HC = D // P, H // P
    NT = T // P
    NB = T // BLK
    ST = NT + E - 1
    SC = ST + 3
    EW = 3 * H * NC
    OOB = float(2 * T)
    assert HC * D == NC * H and NC == 2 and NT * E <= 256 and SC % 2 == 0

    with ExitStack() as outer:
        W = outer.enter_context(nc.sbuf_tensor("W", [P, E * EW], F32))
        Wv = W[:, :].rearrange("p (e w) -> p e w", e=E)
        ident = outer.enter_context(nc.sbuf_tensor("ident2", [P, P], F32))
        tg = outer.enter_context(nc.sbuf_tensor("tg2", [P, 1], F32))
        slot_token = outer.enter_context(nc.sbuf_tensor("slot_token", [P, SC], I32))
        tile_expert = outer.enter_context(nc.sbuf_tensor("tile_expert", [P, SC], I32))
        shared_and_route(nc, comb, x1_dram, g_ffn, gateT, upT, downT, routerT, gate_sT, up_sT, down_sT,
                         Wv, ident, tg, slot_token, tile_expert, OOB)
        routed_experts(nc, comb, W, ident, tg, slot_token, tile_expert, out, E, EW, H, T, ST)


def shared_and_route(nc, comb, x1_dram, g_ffn, gateT, upT, downT, routerT, gate_sT, up_sT, down_sT,
                     Wv, ident, tg, slot_token, tile_expert, OOB):
    T, D = comb.shape[0], comb.shape[1] // 2
    E, _, H = gateT.shape
    NC, HC, NT, NB = D // P, H // P, T // P, T // BLK
    SC = slot_token.shape[1]
    with ExitStack() as ctx:
        def sb(name, shape, dt=F32):
            return ctx.enter_context(nc.sbuf_tensor(name, shape, dt))

        def sem(name):
            return ctx.enter_context(nc.semaphore(name))

        xT = sb("xT_all", [P, NC, T])
        wg = [sb(f"wg_{s}", [P, NC, H], F32R) for s in ("hi", "lo")]
        wu = [sb(f"wu_{s}", [P, NC, H], F32R) for s in ("hi", "lo")]
        wd = [sb(f"wd_{s}", [P, HC, D], F32R) for s in ("hi", "lo")]
        xs = [sb(f"xs_{s}", [P, 2, NC, BLK], F32R) for s in ("hi", "lo")]
        hT = [sb(f"hT_{s}", [P, HC, BLK], F32R) for s in ("hi", "lo")]
        work = sb("work", [P, 4096])
        xl = work[:, 0:2048].rearrange("p (a t c) -> p a t c", a=2, t=TILES)
        row1 = work[:, 0:2048].bitcast(BF16).rearrange("p (i r) -> p i r", i=NT)
        col1 = work[:, 2048:2048 + NT * SC // 2].bitcast(BF16).rearrange("p (i a) -> p i a", i=NT)
        colv = work[:, 2048 + NT * SC // 2:2048 + 3 * NT * SC // 2].bitcast(BF16).rearrange("p (i w) -> p i w", i=NT)
        base = work[:, 0:2048].rearrange("p (a t c) -> p a t c", a=2, t=TILES)
        sg = work[:, 2048:3072].rearrange("p (a c) -> p a c", a=2)
        hf = work[:, 3072:4096].rearrange("p (a c) -> p a c", a=2)
        stage = Wv[:, E - 1, :]
        rT = sb("rT", [P, NC, E])
        rTs = [sb(f"rT_{s}", [P, NC, E], F32R) for s in ("hi", "lo")]
        gate = sb("gate2", [P, 1])
        before = sb("before", [P, P], BF16)
        ones = sb("ones", [P, P], BF16)
        count = sb("count", [P, P])
        upto = sb("upto", [P, E, E])
        token1 = sb("token1", [P, 1])
        desc = sb("desc", [P, E])
        c128 = sb("c128", [P, NT])
        top = sb("top", [P, NT])
        pick = sb("pick", [P, NT, E])
        onehot = sb("onehot", [P, NT + 1, E], BF16)
        many = sb("many", [P, E])
        cmp = work[:, 0:SC * E].rearrange("p (a e) -> p a e", e=E)
        cmpn = work[:, 512:512 + E * NT].rearrange("p (e i) -> p e i", e=E)
        tiles_of = sb("tiles_of", [P, E])
        prod = sb("prod", [P, E, E])
        end = sb("end", [P, E])
        first = sb("first", [P, E])
        slot = sb("slot", [P, NT])
        sloti = sb("sloti", [P, 3, NT], I32)
        slotf = sb("slotf", [P, 2, NT])
        tab = sb("tab", [P, 4, SC])
        et = sb("et", [P, SC])

        ps = ctx.enter_context(nc.psum_tensor("ps2", [P, 8, 512], F32))
        LOG, RANK, TAB = 6, 7, 5
        sh_in = sem("sh_in"); rt_in = sem("rt_in"); rt_lo = sem("rt_lo"); g_in = sem("g_in"); consts = sem("consts")
        sh_hi = sem("sh_hi"); sh_lo = sem("sh_lo"); w_in = sem("w_in")
        xl_in = [sem(f"xl_in{k}") for k in range(2)]; xt_ps = sem("xt_ps"); x_sum = sem("x_sum")
        logits = sem("logits"); onehot_done = sem("onehot_done"); rank_done = sem("rank_done")
        place_done = sem("place_done"); table_done = sem("table_done"); tg_done = sem("tg2_done")
        link_s = sem("link2"); xs_hi = sem("xs_hi"); xs_lo = sem("xs_lo")
        gu_done = sem("gu_done"); silu_done = sem("silu_done"); h_done = sem("h_done")
        h_hi = sem("h_hi"); h_lo = sem("h_lo"); y_done = sem("y_done"); base_done = sem("base_done")
        x1_in = [sem(f"x1_in{k}") for k in range(2)]; base_out = [sem(f"base_out{k}") for k in range(2)]; go = sem("go2"); routed = sem("routed")

        xn2b = comb[:, 0:D].rearrange("(n t p) c -> n p t c", t=TILES, p=P)
        baseb = comb[:, D:2 * D].rearrange("(n t p) c -> n p t c", t=TILES, p=P)
        x1b = x1_dram.rearrange("(n t p) c -> n p t c", t=TILES, p=P)
        block = ctx.enter_context(nc.Block())

        @block.sync
        def _(sp):
            sp.dma_start(rT[:, :, :], routerT.rearrange("(k p) e -> p k e", p=P)).then_inc(rt_in, 16)
            sp.dma_start(gate[:, :], g_ffn.rearrange("(a b) -> a b", a=1).broadcast_to([P, 1])).then_inc(g_in, 16)
            sp.dma_start(xl[:, 0], xn2b[0]).then_inc(xl_in[0], 16)
            sp.dma_start(xl[:, 1], xn2b[1]).then_inc(xl_in[1], 16)
            for j, w in enumerate((gate_sT, up_sT, down_sT)):
                sp.dma_start(stage[:, j * 1024:(j + 1) * 1024].rearrange("p (k n) -> p k n", n=w.shape[1]),
                             w.rearrange("(k p) n -> p k n", p=P)).then_inc(sh_in, 16)
            with sp.Fori(0, NB // 2 - 1) as i:
                for k in range(2):
                    sp.wait_ge(xt_ps, 4 * i + 2 * k + 2)
                    sp.dma_start(xl[:, k], xn2b[2 * i + k + 2]).then_inc(xl_in[k], 16)

            def base_io(i, k, more):
                sp.wait_ge(base_done, 8 * i + 4 * k + 8)
                sp.dma_start(baseb[2 * i + k], base[:, k]).then_inc(base_out[k], 16)
                if more:
                    sp.wait_ge(base_out[k], 16 * i + 16)
                    sp.dma_start(base[:, k], x1b[2 * i + k + 2]).then_inc(x1_in[k], 16)

            sp.wait_ge(table_done, 1)
            for k in range(2):
                sp.dma_start(base[:, k], x1b[k]).then_inc(x1_in[k], 16)
            with sp.Fori(0, NB // 2 - 1) as i:
                base_io(i, 0, True)
                base_io(i, 1, True)
            for k in range(2):
                base_io(NB // 2 - 1, k, False)
            for k in range(2):
                sp.wait_ge(base_out[k], 16 * (NB // 2))

        @block.gpsimd
        def _(pool):
            pool.sem_inc(x_sum, 2)
            pool.sem_inc(h_lo, 2)
            pool.memset(ident[:, :], 0.0).then_inc(go, 1)
            pool.memset(before[:, :], 1.0).then_inc(go, 1)
            pool.memset(upto[:, :, :], 1.0).then_inc(go, 1)
            pool.memset(ones[:, :], 1.0).then_inc(consts, 1)
            pool.memset(onehot[:, :, :], 0.0).then_inc(consts, 1)
            pool.iota(count[:, :], pattern=[[1, P]], base=0, channel_multiplier=0,
                      allow_small_or_imprecise_dtypes=True).then_inc(consts, 1)
            pool.iota(token1[:, :], pattern=[[0, 1]], base=1, channel_multiplier=1,
                      allow_small_or_imprecise_dtypes=True).then_inc(consts, 1)
            pool.wait_ge(go, 3)
            pool.affine_select(out=ident[:, :], in_=ident[:, :], compare_op=ALU.not_equal, fill=1.0,
                               base=0, pattern=[[-1, P]], channel_multiplier=1).then_inc(consts, 1)
            pool.affine_select(out=before[:, :], in_=before[:, :], compare_op=ALU.is_gt, fill=0.0,
                               base=0, pattern=[[1, P]], channel_multiplier=-1).then_inc(consts, 1)
            pool.affine_select(out=upto[:, :, :], in_=upto[:, :, :], compare_op=ALU.is_ge, fill=0.0,
                               base=0, pattern=[[1, E], [-1, E]], channel_multiplier=0).then_inc(consts, 1)
            def load_expert(e):
                for j, w in enumerate((gateT, upT)):
                    pool.dma_start(Wv[:, e, 0:2 * NC * H].rearrange("p (k j h) -> p k j h", k=NC, j=2)[:, :, j, :],
                                   w[e].rearrange("(k p) h -> p k h", p=P)).then_inc(w_in, 16)
                pool.dma_start(Wv[:, e, 2 * NC * H:3 * NC * H].rearrange("p (k c) -> p k c", k=HC),
                               downT[e].rearrange("(k p) c -> p k c", p=P)).then_inc(w_in, 16)

            for e in range(E - 1):
                load_expert(e)

            with pool.Fori(0, NB // 2) as i:
                for k in range(2):
                    pool.wait_ge(xs_lo, 4 * i + 2 * k + 2)
                    pool.tensor_tensor(xT[:, :, bass.ds(i * (2 * BLK) + k * BLK, BLK)], xs[0][:, k].bitcast(F32),
                                       xs[1][:, k].bitcast(F32), ALU.add).then_inc(x_sum, 1)

            pool.wait_ge(sh_lo, 3)
            load_expert(E - 1)

            def h_low(n, j):
                pool.wait_ge(h_hi, 4 * n + j + 1)
                pool.tensor_tensor(hT[1][:, j, :], hf[:, j % 2, :], hT[0][:, j, :].bitcast(F32),
                                   ALU.subtract).then_inc(h_lo, 1)

            with pool.Fori(0, NB) as n:
                for j in range(HC):
                    h_low(n, j)
            pool.wait_ge(w_in, 16 * 3 * E)

        @block.scalar
        def _(act):
            act.wait_ge(g_in, 16)
            act.activation(tg[:, :], gate[:, :], ACT.Tanh).then_inc(tg_done, 1)

            with act.Fori(0, NB // 2) as i:
                for k in range(2):
                    act.wait_ge(x_sum, 2 * i + k + 1)
                    for c in range(NC):
                        act.wait_ge(xt_ps, 4 * i + 2 * k + c + 1)
                        act.copy(xs[0][:, k, c, :], ps[:, 2 * k + c, :]).then_inc(xs_hi, 1)

            for j, w in enumerate((wg, wu, wd)):
                act.wait_ge(sh_in, 48)
                act.copy(w[0][:, :, :].rearrange("p k n -> p (k n)"), stage[:, j * 1024:(j + 1) * 1024])\
                   .then_inc(sh_hi, 1)

            def x_high(n, k):
                act.copy(xs[0][:, k], xT[:, :, bass.ds(n * BLK, BLK)]).then_inc(xs_hi, 1)

            def silu(n, j):
                act.wait_ge(gu_done, 4 * n + j + 1)
                act.activation(sg[:, j % 2, :], ps[:, 2 * (j % 2), :], ACT.Silu).then_inc(silu_done, 1)

            def high(n, j):
                act.wait_ge(h_done, 4 * n + j + 1)
                act.copy(hT[0][:, j, :], hf[:, j % 2, :]).then_inc(h_hi, 1)

            act.wait_ge(x_sum, NB + 2)
            act.wait_ge(logits, 1)
            x_high(0, 0)
            act.wait_ge(table_done, 1)
            for j in range(2):
                silu(0, j)
                high(0, j)

            def blk(n, k, last):
                silu(n, 2)
                high(n, 2)
                if not last:
                    x_high(n + 1, 1 - k)
                silu(n, 3)
                high(n, 3)
                if not last:
                    for j in range(2):
                        silu(n + 1, j)
                        high(n + 1, j)

            with act.Fori(0, NB // 2 - 1) as i:
                blk(2 * i, 0, False)
                blk(2 * i + 1, 1, False)
            blk(NB - 2, 0, False)
            blk(NB - 1, 1, True)

        @block.vector
        def _(dve):
            links = [0]

            def link(i):
                links[0] += 1
                i.then_inc(link_s, 1)
                dve.wait_ge(link_s, links[0])

            dve.sem_inc(base_done, 4)
            dve.wait_ge(rt_in, 16)
            link(dve.tensor_copy(rTs[0][:, :, :], rT[:, :, :]))
            dve.tensor_tensor(rTs[1][:, :, :], rT[:, :, :], rTs[0][:, :, :].bitcast(F32), ALU.subtract)\
               .then_inc(rt_lo, 1)
            with dve.Fori(0, NB // 2) as i:
                for k in range(2):
                    for c in range(NC):
                        dve.wait_ge(xs_hi, 4 * i + 2 * k + c + 1)
                        dve.tensor_tensor(xs[1][:, k, c, :], ps[:, 2 * k + c, :], xs[0][:, k, c, :].bitcast(F32),
                                          ALU.subtract).then_inc(xs_lo, 1)
            for j, w in enumerate((wg, wu, wd)):
                dve.wait_ge(sh_hi, j + 1)
                dve.tensor_tensor(w[1][:, :, :].rearrange("p k n -> p (k n)"), stage[:, j * 1024:(j + 1) * 1024],
                                  w[0][:, :, :].rearrange("p k n -> p (k n)").bitcast(F32),
                                  ALU.subtract).then_inc(sh_lo, 1)

            def x_low(n, k):
                dve.wait_ge(xs_hi, n + 2 * NB + 1)
                dve.tensor_tensor(xs[1][:, k], xT[:, :, bass.ds(n * BLK, BLK)], xs[0][:, k].bitcast(F32),
                                  ALU.subtract).then_inc(xs_lo, 1)

            x_low(0, 0)
            dve.wait_ge(consts, 7)
            link(dve.tensor_scalar(desc[:, :], count[:, 0:E], -1.0, float(E), ALU.mult, ALU.add))
            link(dve.tensor_scalar(c128[:, :], count[:, 0:NT], float(P), None, ALU.mult))
            dve.wait_ge(logits, 1)
            lg = ps[:, LOG, 0:NT * E].rearrange("p (i e) -> p i e", e=E)

            def bc(ap, axis, shape):
                return ap.unsqueeze(axis).broadcast_to(shape)

            link(dve.tensor_reduce(top[:, :], lg, AX_X, ALU.max))
            link(dve.tensor_tensor(pick[:, :, :], lg, bc(top[:, :], 2, [P, NT, E]), ALU.is_equal))
            link(dve.tensor_tensor(pick[:, :, :], pick[:, :, :], bc(desc[:, :], 1, [P, NT, E]), ALU.mult))
            link(dve.tensor_reduce(top[:, :], pick[:, :, :], AX_X, ALU.max))
            dve.tensor_tensor(onehot[:, 0:NT, :], pick[:, :, :], bc(top[:, :], 2, [P, NT, E]), ALU.is_equal)\
               .then_inc(onehot_done, 1)
            dve.wait_ge(rank_done, 1)
            rank = ps[:, RANK, 0:NT * E].rearrange("p (i e) -> p i e", e=E)
            link(dve.tensor_copy(many[:, :], ps[:, RANK, NT * E:NT * E + E]))
            link(dve.tensor_tensor(cmpn[:, :, :], bc(c128[:, :], 1, [P, E, NT]), bc(many[:, :], 2, [P, E, NT]),
                                   ALU.is_lt))
            link(dve.tensor_reduce(tiles_of[:, :], cmpn[:, :, :], AX_X, ALU.add))
            link(dve.tensor_tensor(prod[:, :, :], upto[:, :, :], bc(tiles_of[:, :], 1, [P, E, E]), ALU.mult))
            link(dve.tensor_reduce(end[:, :], prod[:, :, :], AX_X, ALU.add))
            link(dve.tensor_tensor(first[:, :], end[:, :], tiles_of[:, :], ALU.subtract))
            link(dve.tensor_tensor(cmp[:, :, :], bc(count[:, 0:SC], 2, [P, SC, E]), bc(end[:, :], 1, [P, SC, E]),
                                   ALU.is_ge))
            link(dve.tensor_reduce(et[:, :], cmp[:, :, :], AX_X, ALU.add))
            dve.tensor_scalar(tile_expert[:, :], et[:, :], float(E - 1), None, ALU.min).then_inc(routed, 1)
            link(dve.scalar_tensor_tensor(pick[:, :, :], bc(first[:, :], 1, [P, NT, E]), float(P), rank,
                                          ALU.mult, ALU.add))
            link(dve.tensor_tensor(pick[:, :, :], pick[:, :, :], onehot[:, 0:NT, :], ALU.mult))
            link(dve.tensor_reduce(slot[:, :], pick[:, :, :], AX_X, ALU.add))
            link(dve.tensor_copy(sloti[:, 0, :], slot[:, :]))
            link(dve.tensor_scalar(sloti[:, 1, :], sloti[:, 0, :], P - 1, None, ALU.bitwise_and))
            link(dve.tensor_scalar(sloti[:, 2, :], sloti[:, 0, :], 7, None, ALU.logical_shift_right))
            link(dve.tensor_copy(slotf[:, :, :], sloti[:, 1:3, :]))
            dve.tensor_tensor(row1, bc(count[:, :], 1, [P, NT, P]), bc(slotf[:, 0, :], 2, [P, NT, P]),
                              ALU.is_equal).then_inc(place_done, 1)
            link(dve.tensor_tensor(col1, bc(count[:, 0:SC], 1, [P, NT, SC]), bc(slotf[:, 1, :], 2, [P, NT, SC]),
                                   ALU.is_equal))
            dve.tensor_scalar(colv[:, :, 0:SC], col1, token1[:, 0:1], None, ALU.mult).then_inc(place_done, 1)
            dve.tensor_tensor(colv[:, :, SC:2 * SC], col1, bc(count[:, 0:NT], 2, [P, NT, SC]), ALU.mult)\
               .then_inc(place_done, 1)
            dve.wait_ge(table_done, 1)
            link(dve.tensor_copy(tab[:, 0, :], ps[:, TAB, 0:SC]))
            link(dve.scalar_tensor_tensor(tab[:, 1, :], ps[:, TAB, SC:2 * SC], float(P), tab[:, 0, :],
                                          ALU.mult, ALU.add))
            link(dve.tensor_scalar(tab[:, 2, :], tab[:, 0, :], 0.0, OOB, ALU.is_equal, ALU.mult))
            dve.scalar_tensor_tensor(slot_token[:, :], tab[:, 1, :], -1.0, tab[:, 2, :], ALU.add, ALU.add)\
               .then_inc(routed, 1)
            dve.wait_ge(routed, 2)

            def gated(n, j):
                dve.wait_ge(h_lo, 4 * n + j + 1)
                dve.wait_ge(silu_done, 4 * n + j + 1)
                dve.tensor_tensor(hf[:, j % 2, :], ps[:, 2 * (j % 2) + 1, :], sg[:, j % 2, :],
                                  ALU.mult).then_inc(h_done, 1)

            def add_base(n, i, k):
                dve.wait_ge(x1_in[k], 16 * i + 16)
                for t in range(TILES):
                    dve.wait_ge(y_done, 4 * n + t + 1)
                    dve.scalar_tensor_tensor(base[:, k, t, :], ps[:, 4 + t, 0:D], tg[:, 0:1], base[:, k, t, :],
                                             ALU.mult, ALU.add).then_inc(base_done, 1)

            dve.wait_ge(tg_done, 1)
            for j in range(2):
                gated(0, j)

            def blk(i, k, last):
                n = 2 * i + k
                gated(n, 2)
                if not last:
                    x_low(n + 1, 1 - k)
                gated(n, 3)
                if not last:
                    gated(n + 1, 0)
                add_base(n, i, k)
                if not last:
                    gated(n + 1, 1)

            with dve.Fori(0, NB // 2 - 1) as i:
                blk(i, 0, False)
                blk(i, 1, False)
            blk(NB // 2 - 1, 0, False)
            blk(NB // 2 - 1, 1, True)

        @block.tensor
        def _(pe):
            def mm3(out, parts, first, last):
                n = 3 * len(parts)
                i = 0
                for a, b in parts:
                    for u, v in ((a[0], b[0]), (a[0], b[1]), (a[1], b[0])):
                        r = pe.matmul(out, u, v, start=first and i == 0, stop=last and i == n - 1)
                        i += 1
                return r

            def transposes(i, k):
                pe.wait_ge(xl_in[k], 16 * i + 16)
                for c in range(NC):
                    for t in range(TILES):
                        r = pe.transpose(ps[:, 2 * k + c, t * P:(t + 1) * P], xl[:, k, t, c * P:(c + 1) * P],
                                         ident[:, :])
                    r.then_inc(xt_ps, 1)

            def block_logits(i, k):
                pe.wait_ge(xs_lo, 4 * i + 2 * k + 2)
                for t in range(TILES):
                    r = mm3(ps[:, LOG, bass.ds(i * (2 * TILES * E) + (k * TILES + t) * E, E)],
                            [([w[:, k, c, t * P:(t + 1) * P] for w in xs], [w[:, c, :] for w in rTs])
                             for c in range(NC)], True, True)
                return r

            def gate_up(n, k, j):
                if j == 0:
                    pe.wait_ge(xs_lo, 2 * NB + n + 1)
                for m, w in enumerate((wg, wu)):
                    r = mm3(ps[:, 2 * (j % 2) + m, :],
                            [([v[:, c, j * P:(j + 1) * P] for v in w], [v[:, k, c, :] for v in xs])
                             for c in range(NC)], True, True)
                r.then_inc(gu_done, 1)

            def down(n, j):
                pe.wait_ge(h_lo, 4 * n + j + 3)
                for t in range(TILES):
                    if j == 0:
                        pe.wait_ge(base_done, 4 * n + t + 1)
                    r = mm3(ps[:, 4 + t, 0:D], [([v[:, j, t * P:(t + 1) * P] for v in hT], [v[:, j, :] for v in wd])],
                            j == 0, j == HC - 1)
                    if j == HC - 1:
                        r.then_inc(y_done, 1)

            pe.wait_ge(consts, 7)
            pe.wait_ge(rt_lo, 1)
            transposes(0, 0)
            with pe.Fori(0, NB // 2 - 1) as i:
                transposes(i, 1)
                block_logits(i, 0)
                transposes(i + 1, 0)
                block_logits(i, 1)
            transposes(NB // 2 - 1, 1)
            block_logits(NB // 2 - 1, 0)
            block_logits(NB // 2 - 1, 1).then_inc(logits, 1)

            pe.wait_ge(sh_lo, 3)
            gate_up(0, 0, 0)
            pe.wait_ge(onehot_done, 1)
            pe.matmul(ps[:, RANK, 0:(NT + 1) * E], before[:, :], onehot[:, :, :].rearrange("p i e -> p (i e)"),
                      start=True, stop=False)
            for i in range(NT):
                r = pe.matmul(ps[:, RANK, (i + 1) * E:(NT + 1) * E].rearrange("p (i e) -> p i e", e=E), ones[:, :],
                              onehot[:, i, :].unsqueeze(1).broadcast_to([P, NT - i, E]),
                              start=False, stop=i == NT - 1)
            r.then_inc(rank_done, 1)
            gate_up(0, 0, 1)
            pe.wait_ge(place_done, 3)
            for i in range(NT):
                r = pe.matmul(ps[:, TAB, 0:2 * SC], row1[:, i, :], colv[:, i, :], start=i == 0, stop=i == NT - 1)
            r.then_inc(table_done, 1)

            def blk(n, k, last):
                down(n, 0)
                pe.wait_ge(h_done, 4 * n + 1)
                gate_up(n, k, 2)
                down(n, 1)
                pe.wait_ge(h_done, 4 * n + 2)
                gate_up(n, k, 3)
                down(n, 2)
                if not last:
                    pe.wait_ge(h_done, 4 * n + 3)
                    gate_up(n + 1, 1 - k, 0)
                down(n, 3)
                if not last:
                    pe.wait_ge(h_done, 4 * n + 4)
                    gate_up(n + 1, 1 - k, 1)

            with pe.Fori(0, NB // 2 - 1) as i:
                blk(2 * i, 0, False)
                blk(2 * i + 1, 1, False)
            blk(NB - 2, 0, False)
            blk(NB - 1, 1, True)


def routed_experts(nc, comb, W, ident, tg, slot_token, tile_expert, out, E, EW, H, T, ST):
    D = comb.shape[1] // 2
    NC, HC = D // P, H // P
    RING = LOOP = 4
    assert (ST - 3) % LOOP == 0
    with ExitStack() as ctx:
        def sb(name, shape, dt=F32):
            return ctx.enter_context(nc.sbuf_tensor(name, shape, dt))

        def sem(name):
            return ctx.enter_context(nc.semaphore(name))

        rows = [sb(f"rows{i}", [P, 2 * D]) for i in range(RING)]
        gidx = [sb(f"gidx{i}", [P, 1], I32) for i in range(2)]
        sidx = [sb(f"sidx{i}", [P, 1], I32) for i in range(2)]
        xT = sb("xT3", [P, 2, NC * P])
        sg = sb("sg3", [P, 2, H])
        h = sb("h3", [P, 2, H])
        hT = sb("hT3", [P, 2, HC * P])
        og = [sb(f"og{i}", [P, D]) for i in range(2)]
        ps = ctx.enter_context(nc.psum_tensor("ps3", [P, 8, 512], F32))
        XB, HB, YB = 4, 5, 6
        cleared = sem("cleared")
        g_idx = sem("g_idx"); s_idx = sem("s_idx"); issue = sem("issue")
        rows_in = [sem(f"rows_in{i}") for i in range(RING)]
        out_sent = [sem(f"out_sent{i}") for i in range(2)]
        xt_ps = sem("xt3_ps"); xt_sb = sem("xt3_sb"); gate_done = sem("gate3"); up_done = sem("up3"); silu_done = sem("silu3")
        h_done = sem("h3_done"); ht_ps = sem("ht3_ps"); ht_sb = sem("ht3_sb"); y_done = sem("y3")
        og_done = sem("og3")
        block = ctx.enter_context(nc.Block())

        def steps(eng, step):
            step(0, 1)
            step(0, 2)
            with eng.Fori(0, (ST - 3) // LOOP) as j:
                for r in range(3, 3 + LOOP):
                    step(j, r)

        @block.gpsimd
        def _(pool):
            last_token = pool.to_reg(T - 1)


            def gather(j, r):
                i = j * LOOP + r
                col = i if isinstance(i, int) else pool.snap(i)
                if r >= RING:
                    pool.wait_ge(og_done, i - 3)
                if r >= 2:
                    pool.wait_ge(rows_in[(r - 2) % RING], 16 * (j * (LOOP // RING) + (r - 2) // RING + 1))
                    pool.sem_inc(issue, 1)
                pool.tensor_copy(gidx[r % 2][:, :], slot_token[:, bass.ds(col, 1)]).then_inc(g_idx, 1)
                pool.wait_ge(g_idx, i + 1)
                pool.sem_inc(issue, 1)
                pool.indirect_dma_start(rows[r % RING][:, :], None, comb,
                                        bass.IndirectOffsetOnAxis(gidx[r % 2][:, 0:1], 0),
                                        bounds_check=last_token, oob_is_err=False).then_inc(rows_in[r % RING], 16)

            def scatter(j, r):
                i = j * LOOP + r
                col = i if isinstance(i, int) else pool.snap(i)
                if r >= 2:
                    pool.wait_ge(out_sent[r % 2], 16 * (j * (LOOP // 2) + r // 2))
                    pool.sem_inc(issue, 1)
                pool.tensor_copy(sidx[r % 2][:, :], slot_token[:, bass.ds(col, 1)]).then_inc(s_idx, 1)
                pool.wait_ge(s_idx, i + 1)
                pool.wait_ge(og_done, i + 1)
                pool.sem_inc(issue, 1)
                pool.indirect_dma_start(out, bass.IndirectOffsetOnAxis(sidx[r % 2][:, 0:1], 0), og[r % 2][:, :],
                                        None, bounds_check=last_token, oob_is_err=False)\
                    .then_inc(out_sent[r % 2], 16)

            for i in range(RING):
                pool.memset(rows[i][:, :], 0.0).then_inc(cleared, 1)
            pool.wait_ge(cleared, RING)
            for i in range(3):
                gather(0, i)

            def step(j, r):
                gather(j, r + 2)
                scatter(j, r - 1)

            steps(pool, step)
            scatter((ST - 3) // LOOP, 2)
            for k in range(2):
                pool.wait_ge(out_sent[k], 16 * ((ST + 1 - k) // 2))

        @block.scalar
        def _(act):
            def rows_out(j, r):
                act.wait_ge(xt_ps, j * LOOP + r + 1)
                act.copy(xT[:, r % 2, :], ps[:, XB, 0:NC * P]).then_inc(xt_sb, 1)

            def silu(j, r):
                i = j * LOOP + r
                act.wait_ge(gate_done, i + 1)
                if r >= 2:
                    act.wait_ge(h_done, i - 1)
                act.activation(sg[:, r % 2, :], ps[:, 2 * (r % 2), :], ACT.Silu).then_inc(silu_done, 1)

            def step(j, r):
                silu(j, r)
                rows_out(j, r + 1)

            rows_out(0, 0)
            step(0, 0)
            steps(act, step)

        @block.vector
        def _(dve):
            def step(j, r):
                i = j * LOOP + r - 1
                r = r - 1
                dve.wait_ge(silu_done, i + 1)
                dve.wait_ge(up_done, i + 1)
                dve.tensor_tensor(h[:, r % 2, :], ps[:, 2 * (r % 2) + 1, :], sg[:, r % 2, :], ALU.mult)\
                   .then_inc(h_done, 1)
                dve.wait_ge(ht_ps, i + 1)
                dve.tensor_copy(hT[:, r % 2, :], ps[:, HB, :]).then_inc(ht_sb, 1)
                if r >= 2:
                    dve.wait_ge(out_sent[r % 2], 16 * (j * (LOOP // 2) + r // 2))
                dve.wait_ge(y_done, i + 1)
                dve.scalar_tensor_tensor(og[r % 2][:, :], ps[:, YB + r % 2, 0:D], tg[:, 0:1],
                                         rows[r % RING][:, D:2 * D], ALU.mult, ALU.add).then_inc(og_done, 1)

            steps(dve, step)
            step((ST - 3) // LOOP, 3)

        @block.tensor
        def _(pe):
            def transposes(j, r):
                i = j * LOOP + r
                pe.wait_ge(rows_in[r % RING], 16 * (j * (LOOP // RING) + r // RING + 1))
                if r >= 1:
                    pe.wait_ge(xt_sb, i)
                for c in range(NC):
                    k = pe.transpose(ps[:, XB, c * P:(c + 1) * P], rows[r % RING][:, c * P:(c + 1) * P], ident[:, :])
                k.then_inc(xt_ps, 1)

            def expert_at(i):
                e = pe.value_load(tile_expert[0:1, bass.ds(i, 1)], min_val=0, max_val=E - 1)
                return pe.snap(e * EW)

            def product(j, r, m, at, done):
                for c in range(NC):
                    k = pe.matmul(ps[:, 2 * (r % 2) + m, :], xT[:, r % 2, c * P:(c + 1) * P],
                                  W[:, bass.ds(at + (2 * c + m) * H, H)], start=c == 0, stop=c == NC - 1)
                k.then_inc(done, 1)

            def h_transposes(j, r):
                i = j * LOOP + r
                pe.wait_ge(h_done, i + 1)
                if r >= 1:
                    pe.wait_ge(ht_sb, i)
                for c in range(HC):
                    k = pe.transpose(ps[:, HB, c * P:(c + 1) * P], h[:, r % 2, c * P:(c + 1) * P], ident[:, :])
                k.then_inc(ht_ps, 1)

            def down(j, r):
                i = j * LOOP + r
                at = expert_at(i)
                pe.wait_ge(ht_sb, i + 1)
                if r >= 2:
                    pe.wait_ge(og_done, i - 1)
                for c in range(HC):
                    k = pe.matmul(ps[:, YB + r % 2, 0:D], hT[:, r % 2, c * P:(c + 1) * P],
                                  W[:, bass.ds(at + 2 * NC * H + c * D, D)], start=c == 0, stop=c == HC - 1)
                k.then_inc(y_done, 1)

            def step(j, r):
                i = j * LOOP + r
                at = expert_at(i)
                pe.wait_ge(xt_sb, i + 1)
                if r >= 2:
                    pe.wait_ge(h_done, i - 1)
                product(j, r, 0, at, gate_done)
                transposes(j, r + 1)
                if r >= 1:
                    h_transposes(j, r - 1)
                product(j, r, 1, at, up_done)
                if r >= 1:
                    down(j, r - 1)

            transposes(0, 0)
            step(0, 0)
            steps(pe, step)
            h_transposes((ST - 3) // LOOP, 2)
            down((ST - 3) // LOOP, 2)


def program(nc, ins, out, tokens, dim):
    comb = nc.dram_tensor("comb_dram", (tokens, 2 * dim), F32).ap()
    x1 = nc.dram_tensor("x1_dram", (tokens, dim), F32).ap()
    attention(nc, ins['x'], ins['ctx_768'], ins['g_xattn'], ins['L0_xattn_Wq'], ins['L0_xattn_Wk'],
              ins['L0_xattn_Wv'], ins['L0_xattn_Wo'], ins['L0_xattn_bo'], x1, comb[:, 0:dim])
    feed_forward(nc, comb, x1, ins['g_ffn'], ins['L0_ffn_gate'], ins['L0_ffn_up'], ins['L0_ffn_down'],
                 ins['L0_ffn_router'], ins['L0_ffn_w_gate_s'], ins['L0_ffn_w_up_s'], ins['L0_ffn_w_down_s'], out)


_INS = {
    'x': None, 'ctx_768': (0, 2, 1), 'g_xattn': None, 'g_ffn': None,
    'L0_xattn_Wq': None, 'L0_xattn_Wk': None, 'L0_xattn_Wv': None, 'L0_xattn_Wo': None, 'L0_xattn_bo': None,
    'L0_ffn_up': (0, 2, 1), 'L0_ffn_gate': (0, 2, 1), 'L0_ffn_down': (0, 2, 1), 'L0_ffn_router': (1, 0),
    'L0_ffn_w_up_s': (1, 0), 'L0_ffn_w_gate_s': (1, 0), 'L0_ffn_w_down_s': (1, 0),
}


def kernel(**inputs):
    import numpy as _np
    import concourse.bacc as _bacc
    from concourse import mybir as _mybir
    from concourse.bass_utils import run_bass_kernel_spmd as _run

    nc = _bacc.Bacc("TRN2", target_bir_lowering=False, num_devices=1)
    arrays, args = {}, {}
    for name, order in _INS.items():
        a = _np.asarray(inputs[name])
        a = _np.ascontiguousarray(a if order is None else a.transpose(order))
        arrays[f"in_{name}_dram"] = a
        args[name] = nc.dram_tensor(f"in_{name}_dram", a.shape, _mybir.dt.from_np(a.dtype),
                                    kind="ExternalInput").ap()
    shape = inputs['x'].shape
    tokens, dim = shape[0] * shape[1], shape[2]
    out = nc.dram_tensor("out_0_dram", (tokens, dim), _mybir.dt.float32, kind="ExternalOutput").ap()
    program(nc, args, out, tokens, dim)
    r = _run(nc, [arrays], core_ids=[0])
    return r.results[0]["out_0_dram"].reshape(shape)
```

```python
from contextlib import ExitStack

import concourse.bass as bass
from concourse import mybir

P = 128
ALU = mybir.AluOpType
ACT = mybir.ActivationFunctionType
F32 = mybir.dt.float32
F32R = mybir.dt.float32r
I32 = mybir.dt.int32
BF16 = mybir.dt.bfloat16
AX_X = mybir.AxisListType.X

EPS = 1e-5
TILES = 4
BLK = TILES * P


def first(n):
    return isinstance(n, int) and n == 0


def attention(nc, x, ctxT, g_xattn, Wq, Wk, Wv, Wo, bo, x1_dram, xn2_dram):
    B, Nq, D = x.shape
    DC, KEYS = ctxT.shape[1:]
    INNER = Wq.shape[1]
    PAIRS = INNER // P
    DH = P // 2
    SCALE = float(DH) ** -0.5
    NC = D // P
    KP = DC // 2
    PK = 2 * KEYS
    NB = B * Nq // BLK
    KA = (PK - P) // 2
    CH = [(0, KA), (KA, P), (KA + P, KA)]
    MID = KEYS - KA
    assert MID == DH and PAIRS == 8 and NC == 2 and Nq == 2 * BLK

    with ExitStack() as ctx:
        def sb(name, shape, dt=F32):
            return ctx.enter_context(nc.sbuf_tensor(name, shape, dt))

        def sem(name):
            return ctx.enter_context(nc.semaphore(name))

        wq = [sb(f"wq_{s}", [P, NC, INNER], F32R) for s in ("hi", "lo")]
        wk = [sb(f"wk_{s}", [KP, 2, INNER], F32R) for s in ("hi", "lo")]
        wv = [sb(f"wv_{s}", [KP, 2, INNER], F32R) for s in ("hi", "lo")]
        wo = [sb(f"wo_{s}", [P, PAIRS, D], F32R) for s in ("hi", "lo")]
        cx = [sb(f"cx_{s}", [KP, 2, KEYS + P], F32R) for s in ("hi", "lo")]
        cx_raw = sb("cx_raw", [KP, 2, KEYS + P])
        kst = [sb(f"kst_{s}", [P, PAIRS, PK], F32R) for s in ("hi", "lo")]
        VW = 3 * DH + P
        vst = [sb(f"vst_{s}", [P, PAIRS, VW], F32R) for s in ("hi", "lo")]
        qT = [sb(f"qT_{s}", [P, 4, BLK], F32R) for s in ("hi", "lo")]
        prob = sb("prob", [P, 3, TILES, PK])
        pT = [sb(f"pT_{s}", [P, 3, BLK], F32R) for s in ("hi", "lo")]
        oT = [sb(f"oT_{s}", [P, PAIRS, BLK], F32R) for s in ("hi", "lo")]
        xw = sb("xw", [P, 3, TILES, D])
        xn = xw[:, 2]
        xT = [sb(f"xT_{s}", [P, NC, BLK], F32R) for s in ("hi", "lo")]
        ident = sb("ident", [P, P])
        tbo = sb("tbo", [P, D])
        gate = sb("gate", [P, 1])
        tg = sb("tg", [P, 1])
        nmax = sb("nmax", [P, 3, TILES, 2])
        den = sb("den", [P, 3, TILES, 2])
        rden = sb("rden", [P, 3, TILES, 2])
        st = [sb(f"st{i}", [P, TILES, 6]) for i in range(2)]
        mv = [sb(f"mv{i}", [P, TILES, 2]) for i in range(2)]
        sc = [sb(f"sc{i}", [P, 5, TILES]) for i in range(2)]

        ps = ctx.enter_context(nc.psum_tensor("ps", [P, 8, 512], F32))
        BT, BQ, BV = 4, 6, 7

        V_PARTS = [(slice(0, KA), slice(0, DH)), (slice(0, DH), slice(3 * DH, 4 * DH)),
                   (slice(DH, P), slice(4 * DH, 5 * DH)), (slice(0, KA), slice(2 * DH, 3 * DH))]

        stage0 = prob[:, :].rearrange("p a t k -> p (a t k)")[:, 0:NC * INNER]
        stage1 = xw[:, 1:3].rearrange("p a t c -> p (a t c)")
        half = xw[:, 1].rearrange("p t c -> p (t c)")
        WEIGHTS = [(Wk, wk, KP, 2, stage0), (Wv, wv, KP, 2, stage1), (Wq, wq, P, NC, stage0)]
        for i in range(2):
            m = PAIRS // 2
            WEIGHTS.append((Wo[i * m * P:(i + 1) * m * P, :], [w[:, i * m:(i + 1) * m] for w in wo], P, m, half))
        w_in = [sem(f"w{i}_in") for i in range(5)]
        ident0 = sem("ident0"); ident_done = sem("ident_done"); zeroed = sem("zeroed")
        w_hi = sem("w_hi"); w_lo = sem("w_lo")
        gate_in = sem("gate_in"); tg_done = sem("tg_done"); tbo_done = sem("tbo_done")
        cx_in = sem("cx_in"); cx_hi = sem("cx_hi"); cx_lo = sem("cx_lo")
        kv_done = sem("kv_done"); kv_hi = sem("kv_hi"); kv_lo = sem("kv_lo")
        x_in = sem("x_in"); ln1 = sem("ln1"); xn_done = sem("xn_done"); xb_done = sem("xb_done")
        xt_done = sem("xt_done"); xt_hi = sem("xt_hi"); xt_lo = sem("xt_lo")
        q_done = sem("q_done"); q_hi = sem("q_hi"); q_lo = sem("q_lo")
        s_done = sem("s_done"); max_done = sem("max_done"); exp_done = sem("exp_done")
        rden_done = sem("rden_done"); p_done = sem("p_done")
        t_done = sem("t_done"); pt_hi = sem("pt_hi"); pt_lo = sem("pt_lo")
        pv_done = sem("pv_done"); o_hi = sem("o_hi"); o_lo = sem("o_lo")
        wo_done = sem("wo_done"); x1_done = sem("x1_done"); ln2 = sem("ln2"); xn2_done = sem("xn2_done")
        x1_out = sem("x1_out"); xn2_out = sem("xn2_out")
        chain = sem("chain"); pool_go = sem("pool_go"); dve_go = sem("dve_go")

        xb = x.rearrange("b (k t p) c -> (b k) p t c", t=TILES, p=P)
        x1b = x1_dram.rearrange("(n t p) c -> n p t c", t=TILES, p=P)
        xn2b = xn2_dram.rearrange("(n t p) c -> n p t c", t=TILES, p=P)
        cxb = ctxT.rearrange("b (k p) s -> b p k s", p=KP)

        block = ctx.enter_context(nc.Block())

        @block.sync
        def _(sp):
            def load_ctx(b):
                sp.wait_ge(cx_lo, b + 1)
                sp.dma_start(cx_raw[:, :, 0:KEYS], cxb[b]).then_inc(cx_in, 16)
                sp.dma_start(cx_raw[:, :, KEYS:KEYS + MID], cxb[b, :, :, KA:KEYS]).then_inc(cx_in, 16)
                sp.dma_start(cx_raw[:, :, KEYS + MID:KEYS + P], cxb[b, :, :, 0:MID]).then_inc(cx_in, 16)

            def load_weight(i):
                w, _, p, m, stage = WEIGHTS[i]
                sp.dma_start(stage[0:p].rearrange("p (k n) -> p k n", k=m),
                             w.rearrange("(k p) n -> p k n", p=p)).then_inc(w_in[i], 16)

            sp.sem_inc(cx_lo, 1)
            load_weight(0)
            load_ctx(0)
            sp.dma_start(xw[:, 0], xb[0]).then_inc(x_in, 16)
            sp.dma_start(gate[:, :], g_xattn.rearrange("(a b) -> a b", a=1).broadcast_to([P, 1])).then_inc(gate_in, 16)
            sp.dma_start(tbo[:, :], bo.rearrange("(a b) -> a b", a=1).broadcast_to([P, D])).then_inc(gate_in, 16)
            load_weight(1)
            for i, before in ((2, 1), (3, 2), (4, 4)):
                sp.wait_ge(w_lo, before)
                load_weight(i)
            sp.wait_ge(w_lo, 5)

            def block_io(n, k, more):
                if more:
                    sp.wait_ge(x1_out, 16 * n + 1)
                    sp.dma_start(xw[:, 1 - k], xb[n + 1]).then_inc(x_in, 16)
                sp.wait_ge(x1_done, 4 * n + 8)
                sp.dma_start(x1b[n], xw[:, k]).then_inc(x1_out, 16)
                sp.wait_ge(xn2_done, n + 2)
                sp.dma_start(xn2b[n], xn).then_inc(xn2_out, 16)

            sp.sem_inc(x1_out, 1)
            with sp.Fori(0, B - 1) as b:
                block_io(2 * b, 0, True)
                load_ctx(b + 1)
                block_io(2 * b + 1, 1, True)
            block_io(NB - 2, 0, True)
            block_io(NB - 1, 1, False)
            sp.wait_ge(x1_out, 16 * NB + 1)
            sp.wait_ge(xn2_out, 16 * NB + 1)

        @block.gpsimd
        def _(pool):
            pool.sem_inc(xn2_out, 1)
            pool.sem_inc(xn_done, 1)
            pool.sem_inc(xn2_done, 1)
            pool.memset(ident[:, :], 0.0).then_inc(ident0, 1)
            pool.wait_ge(ident0, 1)
            pool.affine_select(out=ident[:, :], in_=ident[:, :], compare_op=ALU.not_equal, fill=1.0,
                               base=0, pattern=[[-1, P]], channel_multiplier=1).then_inc(ident_done, 1)
            for s in range(2):
                pool.memset(kst[s][:, :, :].bitcast(F32), 0.0).then_inc(zeroed, 1)
                pool.memset(vst[s][:, :, :].bitcast(F32), 0.0).then_inc(zeroed, 1)

            def apply_ln1(n, k, stored):
                pool.wait_ge(ln1, n + 1)
                if stored:
                    pool.wait_ge(xn2_out, 16 * stored[0] + 1)
                pool.sem_inc(pool_go, 1)
                for t in range(TILES):
                    pool.tensor_scalar(xn[:, t, :], xw[:, k, t, :], sc[0][:, 3, t:t + 1], sc[0][:, 4, t:t + 1],
                                       ALU.mult, ALU.add).then_inc(xn_done, 1)
                pool.wait_ge(xn_done, 4 * n + 5)
                pool.tensor_tensor(xw[:, k], xw[:, k], tbo[:, :].unsqueeze(1).broadcast_to([P, TILES, D]),
                                   ALU.add).then_inc(xb_done, 1)

            def apply_ln2(n, k, last):
                pool.wait_ge(ln2, n + 1)
                pool.wait_ge(xn2_out, 16 * n + 1)
                pool.wait_ge(xt_done, 2 * n + (2 if last else 4))
                pool.sem_inc(pool_go, 1)
                for t in range(TILES):
                    i = pool.tensor_scalar(xn[:, t, :], xw[:, k, t, :], sc[1][:, 3, t:t + 1], sc[1][:, 4, t:t + 1],
                                           ALU.mult, ALU.add)
                i.then_inc(xn2_done, 1)

            def normalise(n, p):
                pool.wait_ge(rden_done, 8 * n + p + 1)
                pool.tensor_tensor(prob[:, p % 3].rearrange("p t (h k) -> p (t h) k", h=2),
                                   prob[:, p % 3].rearrange("p t (h k) -> p (t h) k", h=2),
                                   rden[:, p % 3].rearrange("p t h -> p (t h)").unsqueeze(2)
                                   .broadcast_to([P, 2 * TILES, KEYS]), ALU.mult).then_inc(p_done, 1)

            pool.wait_ge(tbo_done, 1)
            pool.wait_ge(w_lo, 2)
            apply_ln1(0, 0, None)
            normalise(0, 0)
            normalise(0, 1)

            def blk(n, k, last):
                for p in range(2, PAIRS):
                    normalise(n, p)
                    if p == 4 and not last:
                        apply_ln1(n + 1, 1 - k, [n])
                if not last:
                    normalise(n + 1, 0)
                    normalise(n + 1, 1)
                apply_ln2(n, k, last)

            with pool.Fori(0, B - 1) as b:
                blk(2 * b, 0, False)
                blk(2 * b + 1, 1, False)
            blk(NB - 2, 0, False)
            blk(NB - 1, 1, True)

        @block.scalar
        def _(act):
            act.sem_inc(exp_done, 4)

            def weight_high(i):
                _, w, p, m, stage = WEIGHTS[i]
                act.wait_ge(w_in[i], 16)
                act.copy(w[0][:, :, :].rearrange("p k n -> p (k n)"), stage[0:p]).then_inc(w_hi, 1)

            def xt_high(n, c):
                act.wait_ge(xt_done, 2 * n + c + 1)
                act.copy(xT[0][:, c, :], ps[:, BQ, :]).then_inc(xt_hi, 1)

            def q_high(n, p):
                act.wait_ge(q_done, 8 * n + p + 1)
                act.copy(qT[0][:, p % 4, :], ps[:, BQ, :]).then_inc(q_hi, 1)

            def exps(n, p, t):
                act.wait_ge(max_done, 4 * (8 * n + p) + t + 1)
                if t == 0:
                    act.wait_ge(t_done, 3 * (8 * n + max(p - 2, 0)) + (1 if p == 0 else 4))
                for h in range(2):
                    i = act.activation(prob[:, p % 3, t, h * KEYS:(h + 1) * KEYS], ps[:, t, h * KEYS:(h + 1) * KEYS],
                                       ACT.Exp, bias=nmax[:, p % 3, t, h:h + 1],
                                       accum_out=den[:, p % 3, t, h:h + 1])
                i.then_inc(exp_done, 1)

            def pt_high(n, p, c):
                act.wait_ge(t_done, 3 * (8 * n + p) + c + 5)
                act.copy(pT[0][0:CH[c][1], c, :], ps[0:CH[c][1], BT + (3 * p + c) % 2, :]).then_inc(pt_hi, 1)

            def o_high(n, p):
                act.wait_ge(pv_done, 8 * n + p + 1)
                act.copy(oT[0][:, p, :], ps[:, BV, :]).then_inc(o_hi, 1)

            def cx_high(b):
                act.wait_ge(kv_done, 8 * b + 1)
                act.wait_ge(cx_in, 48 * b + 48)
                act.copy(cx[0][:, :, :], cx_raw[:, :, :]).then_inc(cx_hi, 1)

            def k_high(b, j):
                act.wait_ge(kv_done, 8 * b + j + 2)
                for h in range(2):
                    r = slice(h * DH, (h + 1) * DH)
                    i = act.activation(kst[0][r, 2 * j:2 * j + 2, h * KEYS:(h + 1) * KEYS],
                                       ps[r, j, 0:PK].rearrange("p (a k) -> p a k", a=2), ACT.Copy, scale=SCALE)
                i.then_inc(kv_hi, 1)

            def v_high(b, j):
                r, c = V_PARTS[j]
                act.wait_ge(kv_done, 8 * b + j + 6)
                act.copy(vst[0][r, :, c], ps[r, BT + j, :].rearrange("p (a d) -> p a d", d=DH)).then_inc(kv_hi, 1)

            def step(n, b, k, p, last):
                change = k == 1 and not last
                ahead = (n, p + 2) if p < 6 else (n + 1, 0) if p == 7 and not last else None
                if p < 7:
                    exps(n, p + 1, 3)
                pt_high(n, p, 0)
                if p == 5 and not last:
                    xt_high(n + 1, 1)
                if ahead:
                    exps(*ahead, 0)
                if p == 6 and change:
                    k_high(b + 1, 0)
                pt_high(n, p, 1)
                if p >= 1:
                    o_high(n, p - 1)
                if ahead:
                    exps(*ahead, 1)
                if p == 6 and change:
                    k_high(b + 1, 1)
                if p < 4:
                    q_high(n, p + 4)
                if p > 4 and not last:
                    q_high(n + 1, p - 5)
                pt_high(n, p, 2)
                if ahead:
                    exps(*ahead, 2)
                if p == 4 and not last:
                    xt_high(n + 1, 0)
                if p == 4 and change:
                    cx_high(b + 1)
                if p == 6 and change:
                    k_high(b + 1, 2)
                    k_high(b + 1, 3)

            def blk(n, b, k, last):
                for p in range(1, PAIRS):
                    step(n, b, k, p, last)
                if last:
                    o_high(n, 7)
                    return
                exps(n + 1, 0, 3)
                o_high(n, 7)
                exps(n + 1, 1, 0)
                q_high(n + 1, 3)
                exps(n + 1, 1, 1)
                exps(n + 1, 1, 2)
                if k == 1:
                    for j in range(4):
                        v_high(b + 1, j)
                step(n + 1, b + k, 1 - k, 0, False)

            weight_high(0)
            cx_high(0)
            act.wait_ge(gate_in, 32)
            act.activation(tg[:, :], gate[:, :], ACT.Tanh).then_inc(tg_done, 1)
            weight_high(1)
            act.wait_ge(zeroed, 4)
            for j in range(4):
                k_high(0, j)
            weight_high(2)
            xt_high(0, 0)
            v_high(0, 0)
            xt_high(0, 1)
            v_high(0, 1)
            for p in range(4):
                q_high(0, p)
                exps(0, p // 2, 2 * (p % 2))
                if p < 3:
                    exps(0, p // 2, 2 * (p % 2) + 1)
            v_high(0, 2)
            v_high(0, 3)
            weight_high(3)
            weight_high(4)
            step(0, 0, 0, 0, False)

            with act.Fori(0, B - 1) as b:
                blk(2 * b, b, 0, False)
                blk(2 * b + 1, b, 1, False)
            blk(NB - 2, B - 1, 0, False)
            blk(NB - 1, B - 1, 1, True)

        @block.vector
        def _(dve):


            def low(out, src, hi, done):
                dve.tensor_tensor(out, src, hi.bitcast(F32), ALU.subtract).then_inc(done, 1)

            dve.sem_inc(x1_done, 4)
            dve.sem_inc(o_lo, 1)
            dve.sem_inc(pt_lo, 2)

            def weight_low(i):
                _, w, p, m, stage = WEIGHTS[i]
                dve.wait_ge(w_hi, i + 1)
                low(w[1][:, :, :].rearrange("p k n -> p (k n)"), stage[0:p],
                    w[0][:, :, :].rearrange("p k n -> p (k n)"), w_lo)

            NEWTON = 3
            STAT = 4 + 3 * NEWTON

            def rstd(which, base, done):
                v, m, s = mv[which][:, :, 1], mv[which][:, :, 0], sc[which]
                dve.wait_ge(chain, base)
                dve.tensor_scalar(s[:, 0, :], v, EPS, None, ALU.add).then_inc(chain, 1)
                dve.wait_ge(chain, base + 1)
                dve.tensor_scalar(s[:, 1, :].bitcast(I32), s[:, 0, :].bitcast(I32), -0.5, float(0x5f3759df),
                                  ALU.mult, ALU.add).then_inc(chain, 1)
                for i in range(NEWTON):
                    out = s[:, 1 if i < NEWTON - 1 else 3, :]
                    dve.wait_ge(chain, base + 3 * i + 2)
                    dve.tensor_tensor(s[:, 2, :], s[:, 1, :], s[:, 1, :], ALU.mult).then_inc(chain, 1)
                    dve.wait_ge(chain, base + 3 * i + 3)
                    dve.scalar_tensor_tensor(s[:, 2, :], s[:, 2, :], -0.5, s[:, 0, :], ALU.mult, ALU.mult)\
                       .then_inc(chain, 1)
                    dve.wait_ge(chain, base + 3 * i + 4)
                    dve.scalar_tensor_tensor(out, s[:, 2, :], 1.5, s[:, 1, :], ALU.add, ALU.mult).then_inc(chain, 1)
                dve.wait_ge(chain, base + 3 * NEWTON + 2)
                dve.scalar_tensor_tensor(s[:, 4, :], m, -1.0, s[:, 3, :], ALU.mult, ALU.mult).then_inc(done, 1)

            def x_stats(n, k, t):
                if t == 0:
                    dve.wait_ge(x_in, 16 * n + 16)
                    dve.wait_ge(xn_done, 4 * n + 1)
                i = dve.bn_stats(st[0][:, t, :], xw[:, k, t, :])
                if t == TILES - 1:
                    i.then_inc(chain, 1)

            def x_scales(n):
                dve.wait_ge(chain, 2 * STAT * n + 1)
                dve.sem_inc(dve_go, 1)
                for t in range(TILES):
                    i = dve.bn_aggr(mv[0][:, t, :], st[0][:, t, :])
                i.then_inc(chain, 1)
                rstd(0, 2 * STAT * n + 2, ln1)

            def x1_stats(n, k, t):
                if t == 0:
                    dve.wait_ge(xn2_done, n + 1)
                    dve.wait_ge(x1_done, 4 * n + 8)
                i = dve.bn_stats(st[1][:, t, :], xw[:, k, t, :])
                if t == TILES - 1:
                    i.then_inc(chain, 1)

            def x1_scales(n):
                dve.wait_ge(chain, 2 * STAT * n + 3 * STAT + 1)
                dve.sem_inc(dve_go, 1)
                for t in range(TILES):
                    i = dve.bn_aggr(mv[1][:, t, :], st[1][:, t, :])
                i.then_inc(chain, 1)
                rstd(1, 2 * STAT * n + 3 * STAT + 2, ln2)

            def q_low(n, p):
                dve.wait_ge(q_hi, 8 * n + p + 1)
                low(qT[1][:, p % 4, :], ps[:, BQ, :], qT[0][:, p % 4, :], q_lo)

            def xt_low(n, c):
                dve.wait_ge(xt_hi, 2 * n + c + 1)
                low(xT[1][:, c, :], ps[:, BQ, :], xT[0][:, c, :], xt_lo)

            def maxima(n, p, t):
                dve.wait_ge(s_done, 4 * (8 * n + p) + t + 1)
                dve.tensor_reduce(nmax[:, p % 3, t, :], ps[:, t, 0:PK].rearrange("p (h k) -> p h k", h=2),
                                  AX_X, ALU.max, negate=True).then_inc(max_done, 1)

            def recip(n, p):
                dve.wait_ge(exp_done, 4 * (8 * n + p) + 8)
                dve.reciprocal(rden[:, p % 3], den[:, p % 3]).then_inc(rden_done, 1)

            def pt_low(n, p, c):
                dve.wait_ge(pt_hi, 3 * (8 * n + p) + c + 1)
                r = slice(0, CH[c][1])
                low(pT[1][r, c, :], ps[r, BT + (3 * p + c) % 2, :], pT[0][r, c, :], pt_lo)

            def o_low(n, p):
                dve.wait_ge(o_hi, 8 * n + p + 1)
                low(oT[1][:, p, :], ps[:, BV, :], oT[0][:, p, :], o_lo)

            def cx_low(b):
                dve.wait_ge(cx_hi, b + 1)
                low(cx[1][:, :, :], cx_raw[:, :, :], cx[0][:, :, :], cx_lo)

            def k_low(b, j):
                dve.wait_ge(kv_hi, 8 * b + j + 1)
                for h in range(2):
                    r = slice(h * DH, (h + 1) * DH)
                    part = kst[0][r, 2 * j:2 * j + 2, h * KEYS:(h + 1) * KEYS]
                    i = dve.scalar_tensor_tensor(kst[1][r, 2 * j:2 * j + 2, h * KEYS:(h + 1) * KEYS],
                                                 ps[r, j, 0:PK].rearrange("p (a k) -> p a k", a=2),
                                                 SCALE, part.bitcast(F32), ALU.mult, ALU.subtract)
                i.then_inc(kv_lo, 1)

            def v_low(b, j):
                r, c = V_PARTS[j]
                dve.wait_ge(kv_hi, 8 * b + j + 5)
                low(vst[1][r, :, c], ps[r, BT + j, :].rearrange("p (a d) -> p a d", d=DH), vst[0][r, :, c], kv_lo)

            def residual(n, k, t):
                if t == 0:
                    dve.wait_ge(xb_done, n + 1)
                dve.wait_ge(wo_done, 4 * n + t + 1)
                dve.scalar_tensor_tensor(xw[:, k, t, :], ps[:, BT + t, 0:D], tg[:, 0:1], xw[:, k, t, :],
                                         ALU.mult, ALU.add).then_inc(x1_done, 1)

            def step(n, b, k, p, last):
                change = k == 1 and not last
                ahead = (n, p + 2) if p < 6 else (n + 1, 0) if p == 7 and not last else None

                def between(t):
                    if p == 0 and not first(n):
                        x1_stats(n - 1, 1 - k, t)
                    if p == 3 and not last:
                        x_stats(n + 1, 1 - k, t)

                if ahead:
                    maxima(*ahead, 0)
                pt_low(n, p, 0)
                if p == 5 and not last:
                    xt_low(n + 1, 1)
                if p < 7:
                    recip(n, p + 1)
                between(0)
                if p == 6 and change:
                    k_low(b + 1, 0)
                if ahead:
                    maxima(*ahead, 1)
                pt_low(n, p, 1)
                between(1)
                if p >= 1:
                    o_low(n, p - 1)
                if ahead:
                    maxima(*ahead, 2)
                if p == 6 and change:
                    k_low(b + 1, 1)
                if p < 4:
                    q_low(n, p + 4)
                if p > 4 and not last:
                    q_low(n + 1, p - 5)
                between(2)
                pt_low(n, p, 2)
                if ahead:
                    maxima(*ahead, 3)
                between(3)
                if p == 4 and not last:
                    xt_low(n + 1, 0)
                if p == 4 and change:
                    cx_low(b + 1)
                if p == 6 and change:
                    k_low(b + 1, 2)
                    k_low(b + 1, 3)
                if p == 0 and not first(n):
                    x1_scales(n - 1)
                if p == 3 and not last:
                    x_scales(n + 1)

            def blk(n, b, k, last):
                for p in range(1, PAIRS):
                    step(n, b, k, p, last)
                if last:
                    o_low(n, 7)
                    for t in range(TILES):
                        residual(n, k, t)
                    dve.sem_inc(chain, STAT)
                    for t in range(TILES):
                        x1_stats(n, k, t)
                    x1_scales(n)
                    return
                maxima(n + 1, 1, 0)
                recip(n + 1, 0)
                o_low(n, 7)
                residual(n, k, 0)
                q_low(n + 1, 3)
                for t in range(1, TILES):
                    maxima(n + 1, 1, t)
                    residual(n, k, t)
                if k == 1:
                    for j in range(4):
                        v_low(b + 1, j)
                step(n + 1, b + k, 1 - k, 0, False)

            weight_low(0)
            cx_low(0)
            for t in range(TILES):
                x_stats(0, 0, t)
            x_scales(0)
            dve.sem_inc(chain, STAT)
            dve.wait_ge(tg_done, 1)
            dve.tensor_scalar(tbo[:, :], tbo[:, :], tg[:, 0:1], None, ALU.mult).then_inc(tbo_done, 1)
            weight_low(1)
            dve.wait_ge(zeroed, 4)
            for j in range(4):
                k_low(0, j)
            weight_low(2)
            xt_low(0, 0)
            v_low(0, 0)
            xt_low(0, 1)
            v_low(0, 1)
            for p in range(4):
                q_low(0, p)
                if p == 2:
                    recip(0, 0)
                maxima(0, p // 2, 2 * (p % 2))
                maxima(0, p // 2, 2 * (p % 2) + 1)
            v_low(0, 2)
            v_low(0, 3)
            weight_low(3)
            weight_low(4)
            step(0, 0, 0, 0, False)

            with dve.Fori(0, B - 1) as b:
                blk(2 * b, b, 0, False)
                blk(2 * b + 1, b, 1, False)
            blk(NB - 2, B - 1, 0, False)
            blk(NB - 1, B - 1, 1, True)

        @block.tensor
        def _(pe):
            def mm3(out, parts, first, last):
                n = 3 * len(parts)
                i = 0
                for a, b in parts:
                    for u, v in ((a[0], b[0]), (a[0], b[1]), (a[1], b[0])):
                        r = pe.matmul(out, u, v, start=first and i == 0, stop=last and i == n - 1)
                        i += 1
                return r

            def cut(pair, *key):
                return [w[key] for w in pair]

            ALLP = slice(None)

            def transposes(n, c):
                if c == 0:
                    if not first(n):
                        pe.wait_ge(q_lo, 8 * n)
                    pe.wait_ge(xn_done, 4 * n + 5)
                else:
                    pe.wait_ge(xt_lo, 2 * n + 1)
                for t in range(TILES):
                    i = pe.transpose(ps[:, BQ, t * P:(t + 1) * P], xn[:, t, c * P:(c + 1) * P], ident[:, :])
                i.then_inc(xt_done, 1)

            def project_q(n, b, k, p):
                if p == 0:
                    pe.wait_ge(xt_lo, 2 * n + 2)
                elif p == 4:
                    pe.wait_ge(x1_done, 4 * n + 3)
                    if k == 0:
                        pe.wait_ge(kv_lo, 8 * b + 7)
                else:
                    pe.wait_ge(q_lo, 8 * n + p)
                mm3(ps[:, BQ, :], [(cut(wq, ALLP, c, slice(p * P, (p + 1) * P)), cut(xT, ALLP, c, ALLP))
                                   for c in range(NC)], True, True).then_inc(q_done, 1)

            def scores(n, b, k, p, t):
                if t == 0:
                    pe.wait_ge(q_lo, 8 * n + p + 1)
                if p == 0 and k == 0:
                    pe.wait_ge(kv_lo, 8 * b + t + 1)
                pe.wait_ge(exp_done, 4 * (8 * n + p) + t + 1)
                mm3(ps[:, t, 0:PK], [(cut(qT, ALLP, p % 4, slice(t * P, (t + 1) * P)), cut(kst, ALLP, p, ALLP))],
                    True, True).then_inc(s_done, 1)

            def transpose_p(n, b, k, p, c):
                c0, m = CH[c]
                if c == 0:
                    pe.wait_ge(p_done, 8 * n + p + 1)
                if p == 0 and c < 2:
                    pe.wait_ge(x1_done, 4 * n + c + 1)
                    if k == 0:
                        pe.wait_ge(kv_lo, 8 * b + c + 5)
                pe.wait_ge(pt_lo, 3 * (8 * n + p) + c + 1)
                for t in range(TILES):
                    i = pe.transpose(ps[0:m, BT + (3 * p + c) % 2, t * P:(t + 1) * P],
                                     prob[:, p % 3, t, c0:c0 + m], ident[:, :])
                i.then_inc(t_done, 1)

            def values(n, b, k, p, c):
                m = CH[c][1]
                if c == 0:
                    pe.wait_ge(o_lo, 8 * n + p + 1)
                if p == 0 and c == 0:
                    pe.wait_ge(x1_done, 4 * n + 4)
                    if k == 0:
                        pe.wait_ge(kv_lo, 8 * b + 8)
                pe.wait_ge(pt_lo, 3 * (8 * n + p) + c + 3)
                cols = (slice(0, P), slice(3 * DH, 3 * DH + P), slice(DH, DH + P))[c]
                i = mm3(ps[:, BV, :], [(cut(vst, slice(0, m), p, cols), cut(pT, slice(0, m), c, ALLP))],
                        c == 0, c == 2)
                if c == 2:
                    i.then_inc(pv_done, 1)

            def out_proj(n, t, last):
                if t == 2 and not last:
                    pe.wait_ge(q_lo, 8 * n + 12)
                for p in range(PAIRS):
                    if t == 0 and p >= PAIRS - 2:
                        pe.wait_ge(o_lo, 8 * n + p + 2)
                    i = mm3(ps[:, BT + t, 0:D], [(cut(oT, ALLP, p, slice(t * P, (t + 1) * P)), cut(wo, ALLP, p, ALLP))],
                            p == 0, p == PAIRS - 1)
                i.then_inc(wo_done, 1)

            def project_k(b, j, n):
                if n is not None:
                    pe.wait_ge(exp_done, 4 * (8 * n + PAIRS) + j + 1)
                if j == 0:
                    pe.wait_ge(cx_lo, b + 2)
                for a in range(2):
                    p = 2 * j + a
                    i = mm3(ps[:, j, a * KEYS:(a + 1) * KEYS],
                            [(cut(wk, ALLP, c, slice(p * P, (p + 1) * P)), cut(cx, ALLP, c, slice(0, KEYS)))
                             for c in range(2)], True, True)
                i.then_inc(kv_done, 1)

            def project_v(b, j, n):
                if n is not None:
                    pe.wait_ge(x1_done, 4 * n + j + 5)
                s = (slice(0, KA), slice(KEYS, KEYS + P), slice(KEYS, KEYS + P), slice(MID, KEYS))[j]
                m, odd = s.stop - s.start, j // 2
                rhs = [[w[:, c, :].rearrange("p (a two d) -> p two a d", two=2, d=DH)[:, odd] for w in wv]
                       for c in range(2)]
                mm3(ps[0:m, BT + j, :].rearrange("p (a d) -> p a d", d=DH),
                    [(cut(cx, ALLP, c, s), rhs[c]) for c in range(2)], True, True).then_inc(kv_done, 1)

            def step(n, b, k, p, last):
                change = k == 1 and not last
                here, nxt = (n, b, k), (n + 1, b + k, 1 - k)
                ahead = (*here, p + 2) if p < 6 else (*nxt, 0) if p == 7 and not last else None
                if ahead:
                    scores(*ahead, 0)
                if p == 6 and change:
                    project_k(b + 1, 0, n)
                transpose_p(*here, p, 0)
                if p == 5 and not last:
                    transposes(n + 1, 1)
                if p >= 1:
                    values(*here, p - 1, 1)
                if ahead:
                    scores(*ahead, 1)
                if p == 6 and change:
                    project_k(b + 1, 1, n)
                transpose_p(*here, p, 1)
                if p >= 1:
                    values(*here, p - 1, 2)
                if ahead:
                    scores(*ahead, 2)
                if p == 6 and change:
                    project_k(b + 1, 2, n)
                if p < 4:
                    project_q(*here, p + 4)
                if p > 4 and not last:
                    project_q(*nxt, p - 5)
                transpose_p(*here, p, 2)
                if ahead:
                    scores(*ahead, 3)
                if p == 6 and change:
                    project_k(b + 1, 3, n)
                if p == 4 and not last:
                    transposes(n + 1, 0)
                values(*here, p, 0)

            def blk(n, b, k, last):
                nxt = (n + 1, b + k, 1 - k)
                for p in range(1, PAIRS):
                    step(n, b, k, p, last)
                values(n, b, k, 7, 1)
                if not last:
                    scores(*nxt, 1, 0)
                values(n, b, k, 7, 2)
                out_proj(n, 0, last)
                if not last:
                    project_q(*nxt, 3)
                for t in range(1, TILES):
                    if not last:
                        scores(*nxt, 1, t)
                    out_proj(n, t, last)
                if last:
                    return
                if k == 1:
                    for j in range(4):
                        project_v(b + 1, j, n)
                step(*nxt, 0, False)

            pe.sem_inc(kv_done, 1)
            pe.sem_inc(t_done, 4)
            pe.wait_ge(w_lo, 1)
            for j in range(4):
                project_k(0, j, None)
            pe.wait_ge(ident_done, 1)
            transposes(0, 0)
            pe.wait_ge(w_lo, 2)
            project_v(0, 0, None)
            transposes(0, 1)
            project_v(0, 1, None)
            pe.wait_ge(w_lo, 3)
            for p in range(4):
                project_q(0, 0, 0, p)
                scores(0, 0, 0, p // 2, 2 * (p % 2))
                scores(0, 0, 0, p // 2, 2 * (p % 2) + 1)
            pe.wait_ge(q_lo, 4)
            project_v(0, 2, None)
            project_v(0, 3, None)
            step(0, 0, 0, 0, False)

            with pe.Fori(0, B - 1) as b:
                blk(2 * b, b, 0, False)
                blk(2 * b + 1, b, 1, False)
            blk(NB - 2, B - 1, 0, False)
            blk(NB - 1, B - 1, 1, True)


def feed_forward(nc, comb, x1_dram, g_ffn, gateT, upT, downT, routerT, gate_sT, up_sT, down_sT, out):
    T, D2 = comb.shape
    D = D2 // 2
    E, _, H = gateT.shape
    NC, HC = D // P, H // P
    NT = T // P
    NB = T // BLK
    ST = NT + E - 1
    SC = ST + 3
    EW = 3 * H * NC
    OOB = float(2 * T)
    assert HC * D == NC * H and NC == 2 and NT * E <= 256 and SC % 2 == 0

    with ExitStack() as outer:
        W = outer.enter_context(nc.sbuf_tensor("W", [P, E * EW], F32))
        Wv = W[:, :].rearrange("p (e w) -> p e w", e=E)
        ident = outer.enter_context(nc.sbuf_tensor("ident2", [P, P], F32))
        tg = outer.enter_context(nc.sbuf_tensor("tg2", [P, 1], F32))
        slot_token = outer.enter_context(nc.sbuf_tensor("slot_token", [P, SC], I32))
        tile_expert = outer.enter_context(nc.sbuf_tensor("tile_expert", [P, SC], I32))
        shared_and_route(nc, comb, x1_dram, g_ffn, gateT, upT, downT, routerT, gate_sT, up_sT, down_sT,
                         Wv, ident, tg, slot_token, tile_expert, OOB)
        routed_experts(nc, comb, W, ident, tg, slot_token, tile_expert, out, E, EW, H, T, ST)


def shared_and_route(nc, comb, x1_dram, g_ffn, gateT, upT, downT, routerT, gate_sT, up_sT, down_sT,
                     Wv, ident, tg, slot_token, tile_expert, OOB):
    T, D = comb.shape[0], comb.shape[1] // 2
    E, _, H = gateT.shape
    NC, HC, NT, NB = D // P, H // P, T // P, T // BLK
    SC = slot_token.shape[1]
    with ExitStack() as ctx:
        def sb(name, shape, dt=F32):
            return ctx.enter_context(nc.sbuf_tensor(name, shape, dt))

        def sem(name):
            return ctx.enter_context(nc.semaphore(name))

        xT = sb("xT_all", [P, NC, T])
        wg = [sb(f"wg_{s}", [P, NC, H], F32R) for s in ("hi", "lo")]
        wu = [sb(f"wu_{s}", [P, NC, H], F32R) for s in ("hi", "lo")]
        wd = [sb(f"wd_{s}", [P, HC, D], F32R) for s in ("hi", "lo")]
        xs = [sb(f"xs_{s}", [P, 2, NC, BLK], F32R) for s in ("hi", "lo")]
        hT = [sb(f"hT_{s}", [P, HC, BLK], F32R) for s in ("hi", "lo")]
        work = sb("work", [P, 4096])
        xl = work[:, 0:2048].rearrange("p (a t c) -> p a t c", a=2, t=TILES)
        row1 = work[:, 0:2048].bitcast(BF16).rearrange("p (i r) -> p i r", i=NT)
        col1 = work[:, 2048:2048 + NT * SC // 2].bitcast(BF16).rearrange("p (i a) -> p i a", i=NT)
        colv = work[:, 2048 + NT * SC // 2:2048 + 3 * NT * SC // 2].bitcast(BF16).rearrange("p (i w) -> p i w", i=NT)
        base = work[:, 0:2048].rearrange("p (a t c) -> p a t c", a=2, t=TILES)
        sg = work[:, 2048:3072].rearrange("p (a c) -> p a c", a=2)
        hf = work[:, 3072:4096].rearrange("p (a c) -> p a c", a=2)
        stage = Wv[:, E - 1, :]
        rT = sb("rT", [P, NC, E])
        rTs = [sb(f"rT_{s}", [P, NC, E], F32R) for s in ("hi", "lo")]
        gate = sb("gate2", [P, 1])
        before = sb("before", [P, P], BF16)
        ones = sb("ones", [P, P], BF16)
        count = sb("count", [P, P])
        upto = sb("upto", [P, E, E])
        token1 = sb("token1", [P, 1])
        desc = sb("desc", [P, E])
        c128 = sb("c128", [P, NT])
        top = sb("top", [P, NT])
        pick = sb("pick", [P, NT, E])
        onehot = sb("onehot", [P, NT + 1, E], BF16)
        many = sb("many", [P, E])
        cmp = work[:, 0:SC * E].rearrange("p (a e) -> p a e", e=E)
        cmpn = work[:, 512:512 + E * NT].rearrange("p (e i) -> p e i", e=E)
        tiles_of = sb("tiles_of", [P, E])
        prod = sb("prod", [P, E, E])
        end = sb("end", [P, E])
        first = sb("first", [P, E])
        slot = sb("slot", [P, NT])
        sloti = sb("sloti", [P, 3, NT], I32)
        slotf = sb("slotf", [P, 2, NT])
        tab = sb("tab", [P, 4, SC])
        et = sb("et", [P, SC])

        ps = ctx.enter_context(nc.psum_tensor("ps2", [P, 8, 512], F32))
        LOG, RANK, TAB = 6, 7, 5
        sh_in = sem("sh_in"); rt_in = sem("rt_in"); rt_lo = sem("rt_lo"); g_in = sem("g_in"); consts = sem("consts")
        sh_hi = sem("sh_hi"); sh_lo = sem("sh_lo"); w_in = sem("w_in")
        xl_in = [sem(f"xl_in{k}") for k in range(2)]; xt_ps = sem("xt_ps"); x_sum = sem("x_sum")
        logits = sem("logits"); onehot_done = sem("onehot_done"); rank_done = sem("rank_done")
        place_done = sem("place_done"); table_done = sem("table_done"); tg_done = sem("tg2_done")
        link_s = sem("link2"); xs_hi = sem("xs_hi"); xs_lo = sem("xs_lo")
        gu_done = sem("gu_done"); silu_done = sem("silu_done"); h_done = sem("h_done")
        h_hi = sem("h_hi"); h_lo = sem("h_lo"); y_done = sem("y_done"); base_done = sem("base_done")
        x1_in = [sem(f"x1_in{k}") for k in range(2)]; base_out = [sem(f"base_out{k}") for k in range(2)]; go = sem("go2"); routed = sem("routed")

        xn2b = comb[:, 0:D].rearrange("(n t p) c -> n p t c", t=TILES, p=P)
        baseb = comb[:, D:2 * D].rearrange("(n t p) c -> n p t c", t=TILES, p=P)
        x1b = x1_dram.rearrange("(n t p) c -> n p t c", t=TILES, p=P)
        block = ctx.enter_context(nc.Block())

        @block.sync
        def _(sp):
            sp.dma_start(rT[:, :, :], routerT.rearrange("(k p) e -> p k e", p=P)).then_inc(rt_in, 16)
            sp.dma_start(gate[:, :], g_ffn.rearrange("(a b) -> a b", a=1).broadcast_to([P, 1])).then_inc(g_in, 16)
            sp.dma_start(xl[:, 0], xn2b[0]).then_inc(xl_in[0], 16)
            sp.dma_start(xl[:, 1], xn2b[1]).then_inc(xl_in[1], 16)
            for j, w in enumerate((gate_sT, up_sT, down_sT)):
                sp.dma_start(stage[:, j * 1024:(j + 1) * 1024].rearrange("p (k n) -> p k n", n=w.shape[1]),
                             w.rearrange("(k p) n -> p k n", p=P)).then_inc(sh_in, 16)
            with sp.Fori(0, NB // 2 - 1) as i:
                for k in range(2):
                    sp.wait_ge(xt_ps, 4 * i + 2 * k + 2)
                    sp.dma_start(xl[:, k], xn2b[2 * i + k + 2]).then_inc(xl_in[k], 16)

            def base_io(i, k, more):
                sp.wait_ge(base_done, 8 * i + 4 * k + 8)
                sp.dma_start(baseb[2 * i + k], base[:, k]).then_inc(base_out[k], 16)
                if more:
                    sp.wait_ge(base_out[k], 16 * i + 16)
                    sp.dma_start(base[:, k], x1b[2 * i + k + 2]).then_inc(x1_in[k], 16)

            sp.wait_ge(table_done, 1)
            for k in range(2):
                sp.dma_start(base[:, k], x1b[k]).then_inc(x1_in[k], 16)
            with sp.Fori(0, NB // 2 - 1) as i:
                base_io(i, 0, True)
                base_io(i, 1, True)
            for k in range(2):
                base_io(NB // 2 - 1, k, False)
            for k in range(2):
                sp.wait_ge(base_out[k], 16 * (NB // 2))

        @block.gpsimd
        def _(pool):
            pool.sem_inc(x_sum, 2)
            pool.sem_inc(h_lo, 2)
            pool.memset(ident[:, :], 0.0).then_inc(go, 1)
            pool.memset(before[:, :], 1.0).then_inc(go, 1)
            pool.memset(upto[:, :, :], 1.0).then_inc(go, 1)
            pool.memset(ones[:, :], 1.0).then_inc(consts, 1)
            pool.memset(onehot[:, :, :], 0.0).then_inc(consts, 1)
            pool.iota(count[:, :], pattern=[[1, P]], base=0, channel_multiplier=0,
                      allow_small_or_imprecise_dtypes=True).then_inc(consts, 1)
            pool.iota(token1[:, :], pattern=[[0, 1]], base=1, channel_multiplier=1,
                      allow_small_or_imprecise_dtypes=True).then_inc(consts, 1)
            pool.wait_ge(go, 3)
            pool.affine_select(out=ident[:, :], in_=ident[:, :], compare_op=ALU.not_equal, fill=1.0,
                               base=0, pattern=[[-1, P]], channel_multiplier=1).then_inc(consts, 1)
            pool.affine_select(out=before[:, :], in_=before[:, :], compare_op=ALU.is_gt, fill=0.0,
                               base=0, pattern=[[1, P]], channel_multiplier=-1).then_inc(consts, 1)
            pool.affine_select(out=upto[:, :, :], in_=upto[:, :, :], compare_op=ALU.is_ge, fill=0.0,
                               base=0, pattern=[[1, E], [-1, E]], channel_multiplier=0).then_inc(consts, 1)
            def load_expert(e):
                for j, w in enumerate((gateT, upT)):
                    pool.dma_start(Wv[:, e, 0:2 * NC * H].rearrange("p (k j h) -> p k j h", k=NC, j=2)[:, :, j, :],
                                   w[e].rearrange("(k p) h -> p k h", p=P)).then_inc(w_in, 16)
                pool.dma_start(Wv[:, e, 2 * NC * H:3 * NC * H].rearrange("p (k c) -> p k c", k=HC),
                               downT[e].rearrange("(k p) c -> p k c", p=P)).then_inc(w_in, 16)

            for e in range(E - 1):
                load_expert(e)

            with pool.Fori(0, NB // 2) as i:
                for k in range(2):
                    pool.wait_ge(xs_lo, 4 * i + 2 * k + 2)
                    pool.tensor_tensor(xT[:, :, bass.ds(i * (2 * BLK) + k * BLK, BLK)], xs[0][:, k].bitcast(F32),
                                       xs[1][:, k].bitcast(F32), ALU.add).then_inc(x_sum, 1)

            pool.wait_ge(sh_lo, 3)
            load_expert(E - 1)

            def h_low(n, j):
                pool.wait_ge(h_hi, 4 * n + j + 1)
                pool.tensor_tensor(hT[1][:, j, :], hf[:, j % 2, :], hT[0][:, j, :].bitcast(F32),
                                   ALU.subtract).then_inc(h_lo, 1)

            with pool.Fori(0, NB) as n:
                for j in range(HC):
                    h_low(n, j)
            pool.wait_ge(w_in, 16 * 3 * E)

        @block.scalar
        def _(act):
            act.wait_ge(g_in, 16)
            act.activation(tg[:, :], gate[:, :], ACT.Tanh).then_inc(tg_done, 1)

            with act.Fori(0, NB // 2) as i:
                for k in range(2):
                    act.wait_ge(x_sum, 2 * i + k + 1)
                    for c in range(NC):
                        act.wait_ge(xt_ps, 4 * i + 2 * k + c + 1)
                        act.copy(xs[0][:, k, c, :], ps[:, 2 * k + c, :]).then_inc(xs_hi, 1)

            for j, w in enumerate((wg, wu, wd)):
                act.wait_ge(sh_in, 48)
                act.copy(w[0][:, :, :].rearrange("p k n -> p (k n)"), stage[:, j * 1024:(j + 1) * 1024])\
                   .then_inc(sh_hi, 1)

            def x_high(n, k):
                act.copy(xs[0][:, k], xT[:, :, bass.ds(n * BLK, BLK)]).then_inc(xs_hi, 1)

            def silu(n, j):
                act.wait_ge(gu_done, 4 * n + j + 1)
                act.activation(sg[:, j % 2, :], ps[:, 2 * (j % 2), :], ACT.Silu).then_inc(silu_done, 1)

            def high(n, j):
                act.wait_ge(h_done, 4 * n + j + 1)
                act.copy(hT[0][:, j, :], hf[:, j % 2, :]).then_inc(h_hi, 1)

            act.wait_ge(x_sum, NB + 2)
            act.wait_ge(logits, 1)
            x_high(0, 0)
            act.wait_ge(table_done, 1)
            for j in range(2):
                silu(0, j)
                high(0, j)

            def blk(n, k, last):
                silu(n, 2)
                high(n, 2)
                if not last:
                    x_high(n + 1, 1 - k)
                silu(n, 3)
                high(n, 3)
                if not last:
                    for j in range(2):
                        silu(n + 1, j)
                        high(n + 1, j)

            with act.Fori(0, NB // 2 - 1) as i:
                blk(2 * i, 0, False)
                blk(2 * i + 1, 1, False)
            blk(NB - 2, 0, False)
            blk(NB - 1, 1, True)

        @block.vector
        def _(dve):
            links = [0]

            def link(i):
                links[0] += 1
                i.then_inc(link_s, 1)
                dve.wait_ge(link_s, links[0])

            dve.sem_inc(base_done, 4)
            dve.wait_ge(rt_in, 16)
            link(dve.tensor_copy(rTs[0][:, :, :], rT[:, :, :]))
            dve.tensor_tensor(rTs[1][:, :, :], rT[:, :, :], rTs[0][:, :, :].bitcast(F32), ALU.subtract)\
               .then_inc(rt_lo, 1)
            with dve.Fori(0, NB // 2) as i:
                for k in range(2):
                    for c in range(NC):
                        dve.wait_ge(xs_hi, 4 * i + 2 * k + c + 1)
                        dve.tensor_tensor(xs[1][:, k, c, :], ps[:, 2 * k + c, :], xs[0][:, k, c, :].bitcast(F32),
                                          ALU.subtract).then_inc(xs_lo, 1)
            for j, w in enumerate((wg, wu, wd)):
                dve.wait_ge(sh_hi, j + 1)
                dve.tensor_tensor(w[1][:, :, :].rearrange("p k n -> p (k n)"), stage[:, j * 1024:(j + 1) * 1024],
                                  w[0][:, :, :].rearrange("p k n -> p (k n)").bitcast(F32),
                                  ALU.subtract).then_inc(sh_lo, 1)

            def x_low(n, k):
                dve.wait_ge(xs_hi, n + 2 * NB + 1)
                dve.tensor_tensor(xs[1][:, k], xT[:, :, bass.ds(n * BLK, BLK)], xs[0][:, k].bitcast(F32),
                                  ALU.subtract).then_inc(xs_lo, 1)

            x_low(0, 0)
            dve.wait_ge(consts, 7)
            link(dve.tensor_scalar(desc[:, :], count[:, 0:E], -1.0, float(E), ALU.mult, ALU.add))
            link(dve.tensor_scalar(c128[:, :], count[:, 0:NT], float(P), None, ALU.mult))
            dve.wait_ge(logits, 1)
            lg = ps[:, LOG, 0:NT * E].rearrange("p (i e) -> p i e", e=E)

            def bc(ap, axis, shape):
                return ap.unsqueeze(axis).broadcast_to(shape)

            link(dve.tensor_reduce(top[:, :], lg, AX_X, ALU.max))
            link(dve.tensor_tensor(pick[:, :, :], lg, bc(top[:, :], 2, [P, NT, E]), ALU.is_equal))
            link(dve.tensor_tensor(pick[:, :, :], pick[:, :, :], bc(desc[:, :], 1, [P, NT, E]), ALU.mult))
            link(dve.tensor_reduce(top[:, :], pick[:, :, :], AX_X, ALU.max))
            dve.tensor_tensor(onehot[:, 0:NT, :], pick[:, :, :], bc(top[:, :], 2, [P, NT, E]), ALU.is_equal)\
               .then_inc(onehot_done, 1)
            dve.wait_ge(rank_done, 1)
            rank = ps[:, RANK, 0:NT * E].rearrange("p (i e) -> p i e", e=E)
            link(dve.tensor_copy(many[:, :], ps[:, RANK, NT * E:NT * E + E]))
            link(dve.tensor_tensor(cmpn[:, :, :], bc(c128[:, :], 1, [P, E, NT]), bc(many[:, :], 2, [P, E, NT]),
                                   ALU.is_lt))
            link(dve.tensor_reduce(tiles_of[:, :], cmpn[:, :, :], AX_X, ALU.add))
            link(dve.tensor_tensor(prod[:, :, :], upto[:, :, :], bc(tiles_of[:, :], 1, [P, E, E]), ALU.mult))
            link(dve.tensor_reduce(end[:, :], prod[:, :, :], AX_X, ALU.add))
            link(dve.tensor_tensor(first[:, :], end[:, :], tiles_of[:, :], ALU.subtract))
            link(dve.tensor_tensor(cmp[:, :, :], bc(count[:, 0:SC], 2, [P, SC, E]), bc(end[:, :], 1, [P, SC, E]),
                                   ALU.is_ge))
            link(dve.tensor_reduce(et[:, :], cmp[:, :, :], AX_X, ALU.add))
            dve.tensor_scalar(tile_expert[:, :], et[:, :], float(E - 1), None, ALU.min).then_inc(routed, 1)
            link(dve.scalar_tensor_tensor(pick[:, :, :], bc(first[:, :], 1, [P, NT, E]), float(P), rank,
                                          ALU.mult, ALU.add))
            link(dve.tensor_tensor(pick[:, :, :], pick[:, :, :], onehot[:, 0:NT, :], ALU.mult))
            link(dve.tensor_reduce(slot[:, :], pick[:, :, :], AX_X, ALU.add))
            link(dve.tensor_copy(sloti[:, 0, :], slot[:, :]))
            link(dve.tensor_scalar(sloti[:, 1, :], sloti[:, 0, :], P - 1, None, ALU.bitwise_and))
            link(dve.tensor_scalar(sloti[:, 2, :], sloti[:, 0, :], 7, None, ALU.logical_shift_right))
            link(dve.tensor_copy(slotf[:, :, :], sloti[:, 1:3, :]))
            dve.tensor_tensor(row1, bc(count[:, :], 1, [P, NT, P]), bc(slotf[:, 0, :], 2, [P, NT, P]),
                              ALU.is_equal).then_inc(place_done, 1)
            link(dve.tensor_tensor(col1, bc(count[:, 0:SC], 1, [P, NT, SC]), bc(slotf[:, 1, :], 2, [P, NT, SC]),
                                   ALU.is_equal))
            dve.tensor_scalar(colv[:, :, 0:SC], col1, token1[:, 0:1], None, ALU.mult).then_inc(place_done, 1)
            dve.tensor_tensor(colv[:, :, SC:2 * SC], col1, bc(count[:, 0:NT], 2, [P, NT, SC]), ALU.mult)\
               .then_inc(place_done, 1)
            dve.wait_ge(table_done, 1)
            link(dve.tensor_copy(tab[:, 0, :], ps[:, TAB, 0:SC]))
            link(dve.scalar_tensor_tensor(tab[:, 1, :], ps[:, TAB, SC:2 * SC], float(P), tab[:, 0, :],
                                          ALU.mult, ALU.add))
            link(dve.tensor_scalar(tab[:, 2, :], tab[:, 0, :], 0.0, OOB, ALU.is_equal, ALU.mult))
            dve.scalar_tensor_tensor(slot_token[:, :], tab[:, 1, :], -1.0, tab[:, 2, :], ALU.add, ALU.add)\
               .then_inc(routed, 1)
            dve.wait_ge(routed, 2)

            def gated(n, j):
                dve.wait_ge(h_lo, 4 * n + j + 1)
                dve.wait_ge(silu_done, 4 * n + j + 1)
                dve.tensor_tensor(hf[:, j % 2, :], ps[:, 2 * (j % 2) + 1, :], sg[:, j % 2, :],
                                  ALU.mult).then_inc(h_done, 1)

            def add_base(n, i, k):
                dve.wait_ge(x1_in[k], 16 * i + 16)
                for t in range(TILES):
                    dve.wait_ge(y_done, 4 * n + t + 1)
                    dve.scalar_tensor_tensor(base[:, k, t, :], ps[:, 4 + t, 0:D], tg[:, 0:1], base[:, k, t, :],
                                             ALU.mult, ALU.add).then_inc(base_done, 1)

            dve.wait_ge(tg_done, 1)
            for j in range(2):
                gated(0, j)

            def blk(i, k, last):
                n = 2 * i + k
                gated(n, 2)
                if not last:
                    x_low(n + 1, 1 - k)
                gated(n, 3)
                if not last:
                    gated(n + 1, 0)
                add_base(n, i, k)
                if not last:
                    gated(n + 1, 1)

            with dve.Fori(0, NB // 2 - 1) as i:
                blk(i, 0, False)
                blk(i, 1, False)
            blk(NB // 2 - 1, 0, False)
            blk(NB // 2 - 1, 1, True)

        @block.tensor
        def _(pe):
            def mm3(out, parts, first, last):
                n = 3 * len(parts)
                i = 0
                for a, b in parts:
                    for u, v in ((a[0], b[0]), (a[0], b[1]), (a[1], b[0])):
                        r = pe.matmul(out, u, v, start=first and i == 0, stop=last and i == n - 1)
                        i += 1
                return r

            def transposes(i, k):
                pe.wait_ge(xl_in[k], 16 * i + 16)
                for c in range(NC):
                    for t in range(TILES):
                        r = pe.transpose(ps[:, 2 * k + c, t * P:(t + 1) * P], xl[:, k, t, c * P:(c + 1) * P],
                                         ident[:, :])
                    r.then_inc(xt_ps, 1)

            def block_logits(i, k):
                pe.wait_ge(xs_lo, 4 * i + 2 * k + 2)
                for t in range(TILES):
                    r = mm3(ps[:, LOG, bass.ds(i * (2 * TILES * E) + (k * TILES + t) * E, E)],
                            [([w[:, k, c, t * P:(t + 1) * P] for w in xs], [w[:, c, :] for w in rTs])
                             for c in range(NC)], True, True)
                return r

            def gate_up(n, k, j):
                if j == 0:
                    pe.wait_ge(xs_lo, 2 * NB + n + 1)
                for m, w in enumerate((wg, wu)):
                    r = mm3(ps[:, 2 * (j % 2) + m, :],
                            [([v[:, c, j * P:(j + 1) * P] for v in w], [v[:, k, c, :] for v in xs])
                             for c in range(NC)], True, True)
                r.then_inc(gu_done, 1)

            def down(n, j):
                pe.wait_ge(h_lo, 4 * n + j + 3)
                for t in range(TILES):
                    if j == 0:
                        pe.wait_ge(base_done, 4 * n + t + 1)
                    r = mm3(ps[:, 4 + t, 0:D], [([v[:, j, t * P:(t + 1) * P] for v in hT], [v[:, j, :] for v in wd])],
                            j == 0, j == HC - 1)
                    if j == HC - 1:
                        r.then_inc(y_done, 1)

            pe.wait_ge(consts, 7)
            pe.wait_ge(rt_lo, 1)
            transposes(0, 0)
            with pe.Fori(0, NB // 2 - 1) as i:
                transposes(i, 1)
                block_logits(i, 0)
                transposes(i + 1, 0)
                block_logits(i, 1)
            transposes(NB // 2 - 1, 1)
            block_logits(NB // 2 - 1, 0)
            block_logits(NB // 2 - 1, 1).then_inc(logits, 1)

            pe.wait_ge(sh_lo, 3)
            gate_up(0, 0, 0)
            pe.wait_ge(onehot_done, 1)
            pe.matmul(ps[:, RANK, 0:(NT + 1) * E], before[:, :], onehot[:, :, :].rearrange("p i e -> p (i e)"),
                      start=True, stop=False)
            for i in range(NT):
                r = pe.matmul(ps[:, RANK, (i + 1) * E:(NT + 1) * E].rearrange("p (i e) -> p i e", e=E), ones[:, :],
                              onehot[:, i, :].unsqueeze(1).broadcast_to([P, NT - i, E]),
                              start=False, stop=i == NT - 1)
            r.then_inc(rank_done, 1)
            gate_up(0, 0, 1)
            pe.wait_ge(place_done, 3)
            for i in range(NT):
                r = pe.matmul(ps[:, TAB, 0:2 * SC], row1[:, i, :], colv[:, i, :], start=i == 0, stop=i == NT - 1)
            r.then_inc(table_done, 1)

            def blk(n, k, last):
                down(n, 0)
                pe.wait_ge(h_done, 4 * n + 1)
                gate_up(n, k, 2)
                down(n, 1)
                pe.wait_ge(h_done, 4 * n + 2)
                gate_up(n, k, 3)
                down(n, 2)
                if not last:
                    pe.wait_ge(h_done, 4 * n + 3)
                    gate_up(n + 1, 1 - k, 0)
                down(n, 3)
                if not last:
                    pe.wait_ge(h_done, 4 * n + 4)
                    gate_up(n + 1, 1 - k, 1)

            with pe.Fori(0, NB // 2 - 1) as i:
                blk(2 * i, 0, False)
                blk(2 * i + 1, 1, False)
            blk(NB - 2, 0, False)
            blk(NB - 1, 1, True)


def routed_experts(nc, comb, W, ident, tg, slot_token, tile_expert, out, E, EW, H, T, ST):
    D = comb.shape[1] // 2
    NC, HC = D // P, H // P
    RING = LOOP = 4
    assert (ST - 3) % LOOP == 0
    with ExitStack() as ctx:
        def sb(name, shape, dt=F32):
            return ctx.enter_context(nc.sbuf_tensor(name, shape, dt))

        def sem(name):
            return ctx.enter_context(nc.semaphore(name))

        rows = [sb(f"rows{i}", [P, 2 * D]) for i in range(RING)]
        gidx = [sb(f"gidx{i}", [P, 1], I32) for i in range(2)]
        sidx = [sb(f"sidx{i}", [P, 1], I32) for i in range(2)]
        xT = sb("xT3", [P, 2, NC * P])
        sg = sb("sg3", [P, 2, H])
        h = sb("h3", [P, 2, H])
        hT = sb("hT3", [P, 2, HC * P])
        og = [sb(f"og{i}", [P, D]) for i in range(2)]
        ps = ctx.enter_context(nc.psum_tensor("ps3", [P, 8, 512], F32))
        XB, HB, YB = 4, 5, 6
        cleared = sem("cleared")
        g_idx = sem("g_idx"); s_idx = sem("s_idx"); issue = sem("issue")
        rows_in = [sem(f"rows_in{i}") for i in range(RING)]
        out_sent = [sem(f"out_sent{i}") for i in range(2)]
        xt_ps = sem("xt3_ps"); xt_sb = sem("xt3_sb"); gate_done = sem("gate3"); up_done = sem("up3"); silu_done = sem("silu3")
        h_done = sem("h3_done"); ht_ps = sem("ht3_ps"); ht_sb = sem("ht3_sb"); y_done = sem("y3")
        og_done = sem("og3")
        block = ctx.enter_context(nc.Block())

        def steps(eng, step):
            step(0, 1)
            step(0, 2)
            with eng.Fori(0, (ST - 3) // LOOP) as j:
                for r in range(3, 3 + LOOP):
                    step(j, r)

        @block.gpsimd
        def _(pool):
            last_token = pool.to_reg(T - 1)


            def gather(j, r):
                i = j * LOOP + r
                col = i if isinstance(i, int) else pool.snap(i)
                if r >= RING:
                    pool.wait_ge(og_done, i - 3)
                if r >= 2:
                    pool.wait_ge(rows_in[(r - 2) % RING], 16 * (j * (LOOP // RING) + (r - 2) // RING + 1))
                    pool.sem_inc(issue, 1)
                pool.tensor_copy(gidx[r % 2][:, :], slot_token[:, bass.ds(col, 1)]).then_inc(g_idx, 1)
                pool.wait_ge(g_idx, i + 1)
                pool.sem_inc(issue, 1)
                pool.indirect_dma_start(rows[r % RING][:, :], None, comb,
                                        bass.IndirectOffsetOnAxis(gidx[r % 2][:, 0:1], 0),
                                        bounds_check=last_token, oob_is_err=False).then_inc(rows_in[r % RING], 16)

            def scatter(j, r):
                i = j * LOOP + r
                col = i if isinstance(i, int) else pool.snap(i)
                if r >= 2:
                    pool.wait_ge(out_sent[r % 2], 16 * (j * (LOOP // 2) + r // 2))
                    pool.sem_inc(issue, 1)
                pool.tensor_copy(sidx[r % 2][:, :], slot_token[:, bass.ds(col, 1)]).then_inc(s_idx, 1)
                pool.wait_ge(s_idx, i + 1)
                pool.wait_ge(og_done, i + 1)
                pool.sem_inc(issue, 1)
                pool.indirect_dma_start(out, bass.IndirectOffsetOnAxis(sidx[r % 2][:, 0:1], 0), og[r % 2][:, :],
                                        None, bounds_check=last_token, oob_is_err=False)\
                    .then_inc(out_sent[r % 2], 16)

            for i in range(RING):
                pool.memset(rows[i][:, :], 0.0).then_inc(cleared, 1)
            pool.wait_ge(cleared, RING)
            for i in range(3):
                gather(0, i)

            def step(j, r):
                gather(j, r + 2)
                scatter(j, r - 1)

            steps(pool, step)
            scatter((ST - 3) // LOOP, 2)
            for k in range(2):
                pool.wait_ge(out_sent[k], 16 * ((ST + 1 - k) // 2))

        @block.scalar
        def _(act):
            def rows_out(j, r):
                act.wait_ge(xt_ps, j * LOOP + r + 1)
                act.copy(xT[:, r % 2, :], ps[:, XB, 0:NC * P]).then_inc(xt_sb, 1)

            def silu(j, r):
                i = j * LOOP + r
                act.wait_ge(gate_done, i + 1)
                if r >= 2:
                    act.wait_ge(h_done, i - 1)
                act.activation(sg[:, r % 2, :], ps[:, 2 * (r % 2), :], ACT.Silu).then_inc(silu_done, 1)

            def step(j, r):
                silu(j, r)
                rows_out(j, r + 1)

            rows_out(0, 0)
            step(0, 0)
            steps(act, step)

        @block.vector
        def _(dve):
            def step(j, r):
                i = j * LOOP + r - 1
                r = r - 1
                dve.wait_ge(silu_done, i + 1)
                dve.wait_ge(up_done, i + 1)
                dve.tensor_tensor(h[:, r % 2, :], ps[:, 2 * (r % 2) + 1, :], sg[:, r % 2, :], ALU.mult)\
                   .then_inc(h_done, 1)
                dve.wait_ge(ht_ps, i + 1)
                dve.tensor_copy(hT[:, r % 2, :], ps[:, HB, :]).then_inc(ht_sb, 1)
                if r >= 2:
                    dve.wait_ge(out_sent[r % 2], 16 * (j * (LOOP // 2) + r // 2))
                dve.wait_ge(y_done, i + 1)
                dve.scalar_tensor_tensor(og[r % 2][:, :], ps[:, YB + r % 2, 0:D], tg[:, 0:1],
                                         rows[r % RING][:, D:2 * D], ALU.mult, ALU.add).then_inc(og_done, 1)

            steps(dve, step)
            step((ST - 3) // LOOP, 3)

        @block.tensor
        def _(pe):
            def transposes(j, r):
                i = j * LOOP + r
                pe.wait_ge(rows_in[r % RING], 16 * (j * (LOOP // RING) + r // RING + 1))
                if r >= 1:
                    pe.wait_ge(xt_sb, i)
                for c in range(NC):
                    k = pe.transpose(ps[:, XB, c * P:(c + 1) * P], rows[r % RING][:, c * P:(c + 1) * P], ident[:, :])
                k.then_inc(xt_ps, 1)

            def expert_at(i):
                e = pe.value_load(tile_expert[0:1, bass.ds(i, 1)], min_val=0, max_val=E - 1)
                return pe.snap(e * EW)

            def product(j, r, m, at, done):
                for c in range(NC):
                    k = pe.matmul(ps[:, 2 * (r % 2) + m, :], xT[:, r % 2, c * P:(c + 1) * P],
                                  W[:, bass.ds(at + (2 * c + m) * H, H)], start=c == 0, stop=c == NC - 1)
                k.then_inc(done, 1)

            def h_transposes(j, r):
                i = j * LOOP + r
                pe.wait_ge(h_done, i + 1)
                if r >= 1:
                    pe.wait_ge(ht_sb, i)
                for c in range(HC):
                    k = pe.transpose(ps[:, HB, c * P:(c + 1) * P], h[:, r % 2, c * P:(c + 1) * P], ident[:, :])
                k.then_inc(ht_ps, 1)

            def down(j, r):
                i = j * LOOP + r
                at = expert_at(i)
                pe.wait_ge(ht_sb, i + 1)
                if r >= 2:
                    pe.wait_ge(og_done, i - 1)
                for c in range(HC):
                    k = pe.matmul(ps[:, YB + r % 2, 0:D], hT[:, r % 2, c * P:(c + 1) * P],
                                  W[:, bass.ds(at + 2 * NC * H + c * D, D)], start=c == 0, stop=c == HC - 1)
                k.then_inc(y_done, 1)

            def step(j, r):
                i = j * LOOP + r
                at = expert_at(i)
                pe.wait_ge(xt_sb, i + 1)
                if r >= 2:
                    pe.wait_ge(h_done, i - 1)
                product(j, r, 0, at, gate_done)
                transposes(j, r + 1)
                if r >= 1:
                    h_transposes(j, r - 1)
                product(j, r, 1, at, up_done)
                if r >= 1:
                    down(j, r - 1)

            transposes(0, 0)
            step(0, 0)
            steps(pe, step)
            h_transposes((ST - 3) // LOOP, 2)
            down((ST - 3) // LOOP, 2)


def program(nc, ins, out, tokens, dim):
    comb = nc.dram_tensor("comb_dram", (tokens, 2 * dim), F32).ap()
    x1 = nc.dram_tensor("x1_dram", (tokens, dim), F32).ap()
    attention(nc, ins['x'], ins['ctx_768'], ins['g_xattn'], ins['L0_xattn_Wq'], ins['L0_xattn_Wk'],
              ins['L0_xattn_Wv'], ins['L0_xattn_Wo'], ins['L0_xattn_bo'], x1, comb[:, 0:dim])
    feed_forward(nc, comb, x1, ins['g_ffn'], ins['L0_ffn_gate'], ins['L0_ffn_up'], ins['L0_ffn_down'],
                 ins['L0_ffn_router'], ins['L0_ffn_w_gate_s'], ins['L0_ffn_w_up_s'], ins['L0_ffn_w_down_s'], out)


_INS = {
    'x': None, 'ctx_768': (0, 2, 1), 'g_xattn': None, 'g_ffn': None,
    'L0_xattn_Wq': None, 'L0_xattn_Wk': None, 'L0_xattn_Wv': None, 'L0_xattn_Wo': None, 'L0_xattn_bo': None,
    'L0_ffn_up': (0, 2, 1), 'L0_ffn_gate': (0, 2, 1), 'L0_ffn_down': (0, 2, 1), 'L0_ffn_router': (1, 0),
    'L0_ffn_w_up_s': (1, 0), 'L0_ffn_w_gate_s': (1, 0), 'L0_ffn_w_down_s': (1, 0),
}


def kernel(**inputs):
    import numpy as _np
    import concourse.bacc as _bacc
    from concourse import mybir as _mybir
    from concourse.bass_utils import run_bass_kernel_spmd as _run

    nc = _bacc.Bacc("TRN2", target_bir_lowering=False, num_devices=1)
    arrays, args = {}, {}
    for name, order in _INS.items():
        a = _np.asarray(inputs[name])
        a = _np.ascontiguousarray(a if order is None else a.transpose(order))
        arrays[f"in_{name}_dram"] = a
        args[name] = nc.dram_tensor(f"in_{name}_dram", a.shape, _mybir.dt.from_np(a.dtype),
                                    kind="ExternalInput").ap()
    shape = inputs['x'].shape
    tokens, dim = shape[0] * shape[1], shape[2]
    out = nc.dram_tensor("out_0_dram", (tokens, dim), _mybir.dt.float32, kind="ExternalOutput").ap()
    program(nc, args, out, tokens, dim)
    r = _run(nc, [arrays], core_ids=[0])
    return r.results[0]["out_0_dram"].reshape(shape)
```

```python
from contextlib import ExitStack

import concourse.bass as bass
from concourse import mybir

P = 128
ALU = mybir.AluOpType
ACT = mybir.ActivationFunctionType
F32 = mybir.dt.float32
F32R = mybir.dt.float32r
I32 = mybir.dt.int32
BF16 = mybir.dt.bfloat16
AX_X = mybir.AxisListType.X

EPS = 1e-5
TILES = 4
BLK = TILES * P


def is_first(n):
    return isinstance(n, int) and n == 0


def attention(nc, x, ctxT, g_xattn, Wq, Wk, Wv, Wo, bo, x1_dram, xn2_dram):
    B, Nq, D = x.shape
    DC, KEYS = ctxT.shape[1:]
    INNER = Wq.shape[1]
    PAIRS = INNER // P
    DH = P // 2
    SCALE = float(DH) ** -0.5
    NC = D // P
    KP = DC // 2
    PK = 2 * KEYS
    NB = B * Nq // BLK
    KA = (PK - P) // 2
    CH = [(0, KA), (KA, P), (KA + P, KA)]
    MID = KEYS - KA
    assert MID == DH and PAIRS == 8 and NC == 2 and Nq == 2 * BLK

    with ExitStack() as ctx:
        def sb(name, shape, dt=F32):
            return ctx.enter_context(nc.sbuf_tensor(name, shape, dt))

        def sem(name):
            return ctx.enter_context(nc.semaphore(name))

        wq = [sb(f"wq_{s}", [P, NC, INNER], F32R) for s in ("hi", "lo")]
        wk = [sb(f"wk_{s}", [KP, 2, INNER], F32R) for s in ("hi", "lo")]
        wv = [sb(f"wv_{s}", [KP, 2, INNER], F32R) for s in ("hi", "lo")]
        wo = [sb(f"wo_{s}", [P, PAIRS, D], F32R) for s in ("hi", "lo")]
        cx = [sb(f"cx_{s}", [KP, 2, KEYS + P], F32R) for s in ("hi", "lo")]
        cx_raw = sb("cx_raw", [KP, 2, KEYS + P])
        kst = [sb(f"kst_{s}", [P, PAIRS, PK], F32R) for s in ("hi", "lo")]
        VW = 3 * DH + P
        vst = [sb(f"vst_{s}", [P, PAIRS, VW], F32R) for s in ("hi", "lo")]
        qT = [sb(f"qT_{s}", [P, 4, BLK], F32R) for s in ("hi", "lo")]
        prob = sb("prob", [P, 3, TILES, PK])
        pT = [sb(f"pT_{s}", [P, 3, BLK], F32R) for s in ("hi", "lo")]
        oT = [sb(f"oT_{s}", [P, PAIRS, BLK], F32R) for s in ("hi", "lo")]
        xw = sb("xw", [P, 3, TILES, D])
        xn = xw[:, 2]
        xT = [sb(f"xT_{s}", [P, NC, BLK], F32R) for s in ("hi", "lo")]
        ident = sb("ident", [P, P])
        tbo = sb("tbo", [P, D])
        gate = sb("gate", [P, 1])
        tg = sb("tg", [P, 1])
        nmax = sb("nmax", [P, 3, TILES, 2])
        den = sb("den", [P, 3, TILES, 2])
        rden = sb("rden", [P, 3, TILES, 2])
        st = [sb(f"st{i}", [P, TILES, 6]) for i in range(2)]
        mv = [sb(f"mv{i}", [P, TILES, 2]) for i in range(2)]
        sc = [sb(f"sc{i}", [P, 5, TILES]) for i in range(2)]

        ps = ctx.enter_context(nc.psum_tensor("ps", [P, 8, 512], F32))
        BT, BQ, BV = 4, 6, 7

        V_PARTS = [(slice(0, KA), slice(0, DH)), (slice(0, DH), slice(3 * DH, 4 * DH)),
                   (slice(DH, P), slice(4 * DH, 5 * DH)), (slice(0, KA), slice(2 * DH, 3 * DH))]
        V_BANKS = [BT, BT + 1, BV, BQ]

        stage0 = prob[:, :].rearrange("p a t k -> p (a t k)")[:, 0:NC * INNER]
        stage1 = xw[:, 1:3].rearrange("p a t c -> p (a t c)")
        half = xw[:, 1].rearrange("p t c -> p (t c)")
        WEIGHTS = [(Wk, wk, KP, 2, stage0), (Wv, wv, KP, 2, stage1), (Wq, wq, P, NC, stage0)]
        for i in range(2):
            m = PAIRS // 2
            WEIGHTS.append((Wo[i * m * P:(i + 1) * m * P, :], [w[:, i * m:(i + 1) * m] for w in wo], P, m, half))
        w_in = [sem(f"w{i}_in") for i in range(5)]
        ident0 = sem("ident0"); ident_done = sem("ident_done"); zeroed = sem("zeroed")
        w_hi = sem("w_hi"); w_lo = sem("w_lo")
        gate_in = sem("gate_in"); tg_done = sem("tg_done"); tbo_done = sem("tbo_done")
        cx_in = sem("cx_in"); cx_hi = sem("cx_hi"); cx_lo = sem("cx_lo")
        kv_done = sem("kv_done"); kv_hi = sem("kv_hi"); kv_lo = sem("kv_lo")
        x_in = sem("x_in"); ln1 = sem("ln1"); xn_done = sem("xn_done"); xb_done = sem("xb_done")
        xt_done = sem("xt_done"); xt_hi = sem("xt_hi"); xt_lo = sem("xt_lo")
        q_done = sem("q_done"); q_hi = sem("q_hi"); q_lo = sem("q_lo")
        s_done = sem("s_done"); max_done = sem("max_done"); exp_done = sem("exp_done")
        rden_done = sem("rden_done"); p_done = sem("p_done")
        t_done = sem("t_done"); pt_hi = sem("pt_hi"); pt_lo = sem("pt_lo")
        pv_done = sem("pv_done"); o_hi = sem("o_hi"); o_lo = sem("o_lo")
        wo_done = sem("wo_done"); x1_done = sem("x1_done"); ln2 = sem("ln2"); xn2_done = sem("xn2_done")
        x1_out = sem("x1_out"); xn2_out = sem("xn2_out")
        chain = sem("chain"); pool_go = sem("pool_go"); dve_go = sem("dve_go")

        xb = x.rearrange("b (k t p) c -> (b k) p t c", t=TILES, p=P)
        x1b = x1_dram.rearrange("(n t p) c -> n p t c", t=TILES, p=P)
        xn2b = xn2_dram.rearrange("(n t p) c -> n p t c", t=TILES, p=P)
        cxb = ctxT.rearrange("b (k p) s -> b p k s", p=KP)

        block = ctx.enter_context(nc.Block())

        @block.sync
        def _(sp):
            def load_ctx(b):
                sp.wait_ge(cx_lo, b + 1)
                sp.dma_start(cx_raw[:, :, 0:KEYS], cxb[b]).then_inc(cx_in, 16)
                sp.dma_start(cx_raw[:, :, KEYS:KEYS + MID], cxb[b, :, :, KA:KEYS]).then_inc(cx_in, 16)
                sp.dma_start(cx_raw[:, :, KEYS + MID:KEYS + P], cxb[b, :, :, 0:MID]).then_inc(cx_in, 16)

            def load_weight(i):
                w, _, p, m, stage = WEIGHTS[i]
                sp.dma_start(stage[0:p].rearrange("p (k n) -> p k n", k=m),
                             w.rearrange("(k p) n -> p k n", p=p)).then_inc(w_in[i], 16)

            sp.sem_inc(cx_lo, 1)
            load_weight(0)
            load_ctx(0)
            sp.dma_start(xw[:, 0], xb[0]).then_inc(x_in, 16)
            sp.dma_start(gate[:, :], g_xattn.rearrange("(a b) -> a b", a=1).broadcast_to([P, 1])).then_inc(gate_in, 16)
            sp.dma_start(tbo[:, :], bo.rearrange("(a b) -> a b", a=1).broadcast_to([P, D])).then_inc(gate_in, 16)
            load_weight(1)
            for i, before in ((2, 1), (3, 2), (4, 4)):
                sp.wait_ge(w_lo, before)
                load_weight(i)
            sp.wait_ge(w_lo, 5)

            def block_io(n, k, more):
                if more:
                    sp.wait_ge(x1_out, 16 * n + 1)
                    sp.dma_start(xw[:, 1 - k], xb[n + 1]).then_inc(x_in, 16)
                sp.wait_ge(x1_done, 4 * n + 8)
                sp.dma_start(x1b[n], xw[:, k]).then_inc(x1_out, 16)
                sp.wait_ge(xn2_done, n + 2)
                sp.dma_start(xn2b[n], xn).then_inc(xn2_out, 16)

            sp.sem_inc(x1_out, 1)
            with sp.Fori(0, B - 1) as b:
                block_io(2 * b, 0, True)
                load_ctx(b + 1)
                block_io(2 * b + 1, 1, True)
            block_io(NB - 2, 0, True)
            block_io(NB - 1, 1, False)
            sp.wait_ge(x1_out, 16 * NB + 1)
            sp.wait_ge(xn2_out, 16 * NB + 1)

        @block.gpsimd
        def _(pool):
            pool.sem_inc(xn2_out, 1)
            pool.sem_inc(xn_done, 1)
            pool.sem_inc(xn2_done, 1)
            pool.memset(ident[:, :], 0.0).then_inc(ident0, 1)
            pool.wait_ge(ident0, 1)
            pool.affine_select(out=ident[:, :], in_=ident[:, :], compare_op=ALU.not_equal, fill=1.0,
                               base=0, pattern=[[-1, P]], channel_multiplier=1).then_inc(ident_done, 1)
            for s in range(2):
                pool.memset(kst[s][:, :, :].bitcast(F32), 0.0).then_inc(zeroed, 1)
                pool.memset(vst[s][:, :, :].bitcast(F32), 0.0).then_inc(zeroed, 1)

            def apply_ln1(n, k):
                pool.wait_ge(ln1, n + 1)
                if not is_first(n):
                    pool.wait_ge(xn2_out, 16 * (n - 1) + 1)
                pool.sem_inc(pool_go, 1)
                for t in range(TILES):
                    pool.tensor_scalar(xn[:, t, :], xw[:, k, t, :], sc[0][:, 3, t:t + 1], sc[0][:, 4, t:t + 1],
                                       ALU.mult, ALU.add).then_inc(xn_done, 1)

            def add_bias(n, k):
                pool.wait_ge(xn_done, 4 * n + 5)
                pool.tensor_tensor(xw[:, k], xw[:, k], tbo[:, :].unsqueeze(1).broadcast_to([P, TILES, D]),
                                   ALU.add).then_inc(xb_done, 1)

            def apply_ln2(n, k, last):
                pool.wait_ge(ln2, n + 1)
                pool.wait_ge(xn2_out, 16 * n + 1)
                pool.wait_ge(xt_done, 2 * n + (2 if last else 4))
                pool.sem_inc(pool_go, 1)
                for t in range(TILES):
                    i = pool.tensor_scalar(xn[:, t, :], xw[:, k, t, :], sc[1][:, 3, t:t + 1], sc[1][:, 4, t:t + 1],
                                           ALU.mult, ALU.add)
                i.then_inc(xn2_done, 1)

            def normalise(n, p):
                pool.wait_ge(rden_done, 8 * n + p + 1)
                pool.tensor_tensor(prob[:, p % 3].rearrange("p t (h k) -> p (t h) k", h=2),
                                   prob[:, p % 3].rearrange("p t (h k) -> p (t h) k", h=2),
                                   rden[:, p % 3].rearrange("p t h -> p (t h)").unsqueeze(2)
                                   .broadcast_to([P, 2 * TILES, KEYS]), ALU.mult).then_inc(p_done, 1)

            pool.wait_ge(tbo_done, 1)
            pool.wait_ge(w_lo, 2)
            apply_ln1(0, 0)
            normalise(0, 0)
            add_bias(0, 0)
            normalise(0, 1)
            normalise(0, 2)

            def blk(n, k, last):
                for p in range(3, PAIRS):
                    normalise(n, p)
                    if p == 5 and not last:
                        apply_ln1(n + 1, 1 - k)
                    if p == 6 and not last:
                        add_bias(n + 1, 1 - k)
                if not last:
                    for p in range(3):
                        normalise(n + 1, p)
                apply_ln2(n, k, last)

            with pool.Fori(0, B - 1) as b:
                blk(2 * b, 0, False)
                blk(2 * b + 1, 1, False)
            blk(NB - 2, 0, False)
            blk(NB - 1, 1, True)

        @block.scalar
        def _(act):
            act.sem_inc(exp_done, 4)

            def weight_high(i):
                _, w, p, m, stage = WEIGHTS[i]
                act.wait_ge(w_in[i], 16)
                act.copy(w[0][:, :, :].rearrange("p k n -> p (k n)"), stage[0:p]).then_inc(w_hi, 1)

            def xt_high(n, c):
                act.wait_ge(xt_done, 2 * n + c + 1)
                act.copy(xT[0][:, c, :], ps[:, BQ, :]).then_inc(xt_hi, 1)

            def q_high(n, p):
                act.wait_ge(q_done, 8 * n + p + 1)
                act.copy(qT[0][:, p % 4, :], ps[:, BQ, :]).then_inc(q_hi, 1)

            def exps(n, p, t):
                act.wait_ge(max_done, 4 * (8 * n + p) + t + 1)
                if t == 0:
                    act.wait_ge(t_done, 3 * (8 * n + max(p - 2, 0)) + (1 if p == 0 else 4))
                for h in range(2):
                    i = act.activation(prob[:, p % 3, t, h * KEYS:(h + 1) * KEYS], ps[:, t, h * KEYS:(h + 1) * KEYS],
                                       ACT.Exp, bias=nmax[:, p % 3, t, h:h + 1],
                                       accum_out=den[:, p % 3, t, h:h + 1])
                i.then_inc(exp_done, 1)

            def pt_high(n, p, c):
                act.wait_ge(t_done, 3 * (8 * n + p) + c + 5)
                act.copy(pT[0][0:CH[c][1], c, :], ps[0:CH[c][1], BT + (3 * p + c) % 2, :]).then_inc(pt_hi, 1)

            def o_high(n, p):
                act.wait_ge(pv_done, 8 * n + p + 1)
                act.copy(oT[0][:, p, :], ps[:, BV, :]).then_inc(o_hi, 1)

            def cx_high(b):
                act.wait_ge(kv_done, 8 * b + 1)
                act.wait_ge(cx_in, 48 * b + 48)
                act.copy(cx[0][:, :, :], cx_raw[:, :, :]).then_inc(cx_hi, 1)

            def k_high(b, j):
                act.wait_ge(kv_done, 8 * b + j + 2)
                for h in range(2):
                    r = slice(h * DH, (h + 1) * DH)
                    i = act.activation(kst[0][r, 2 * j:2 * j + 2, h * KEYS:(h + 1) * KEYS],
                                       ps[r, j, 0:PK].rearrange("p (a k) -> p a k", a=2), ACT.Copy, scale=SCALE)
                i.then_inc(kv_hi, 1)

            def v_high(b, j):
                r, c = V_PARTS[j]
                act.wait_ge(kv_done, 8 * b + j + 6)
                act.copy(vst[0][r, :, c], ps[r, V_BANKS[j], :].rearrange("p (a d) -> p a d", d=DH)).then_inc(kv_hi, 1)

            def step(n, b, k, p, last):
                change = k == 1 and not last
                ahead = (n, p + 2) if p < 6 else (n + 1, 0) if p == 7 and not last else None
                if p < 7:
                    exps(n, p + 1, 3)
                pt_high(n, p, 0)
                if p == 6 and not last:
                    xt_high(n + 1, 1)
                if ahead:
                    exps(*ahead, 0)
                if p == 6 and change:
                    k_high(b + 1, 0)
                if p >= 1:
                    o_high(n, p - 1)
                pt_high(n, p, 1)
                if ahead:
                    exps(*ahead, 1)
                if p == 6 and change:
                    k_high(b + 1, 1)
                if p < 4:
                    q_high(n, p + 4)
                if p > 5 and not last:
                    q_high(n + 1, p - 6)
                pt_high(n, p, 2)
                if ahead:
                    exps(*ahead, 2)
                if p == 5 and not last:
                    xt_high(n + 1, 0)
                if p == 4 and change:
                    cx_high(b + 1)
                if p == 6 and change:
                    k_high(b + 1, 2)
                    k_high(b + 1, 3)

            def blk(n, b, k, last):
                for p in range(2, PAIRS):
                    step(n, b, k, p, last)
                if last:
                    o_high(n, 7)
                    return
                exps(n + 1, 0, 3)
                o_high(n, 7)
                exps(n + 1, 1, 0)
                q_high(n + 1, 2)
                exps(n + 1, 1, 1)
                q_high(n + 1, 3)
                exps(n + 1, 1, 2)
                if k == 1:
                    for j in range(4):
                        v_high(b + 1, j)
                for p in range(2):
                    step(n + 1, b + k, 1 - k, p, False)

            weight_high(0)
            cx_high(0)
            act.wait_ge(gate_in, 32)
            act.activation(tg[:, :], gate[:, :], ACT.Tanh).then_inc(tg_done, 1)
            weight_high(1)
            act.wait_ge(zeroed, 4)
            for j in range(4):
                k_high(0, j)
            weight_high(2)
            xt_high(0, 0)
            v_high(0, 0)
            xt_high(0, 1)
            v_high(0, 1)
            q_high(0, 0)
            v_high(0, 2)
            q_high(0, 1)
            for t in range(3):
                exps(0, 0, t)
            q_high(0, 2)
            exps(0, 0, 3)
            exps(0, 1, 0)
            q_high(0, 3)
            exps(0, 1, 1)
            exps(0, 1, 2)
            v_high(0, 3)
            weight_high(3)
            step(0, 0, 0, 0, False)
            weight_high(4)
            step(0, 0, 0, 1, False)

            with act.Fori(0, B - 1) as b:
                blk(2 * b, b, 0, False)
                blk(2 * b + 1, b, 1, False)
            blk(NB - 2, B - 1, 0, False)
            blk(NB - 1, B - 1, 1, True)

        @block.vector
        def _(dve):
            def low(out, src, hi, done):
                dve.tensor_tensor(out, src, hi.bitcast(F32), ALU.subtract).then_inc(done, 1)

            dve.sem_inc(x1_done, 4)
            dve.sem_inc(o_lo, 1)
            dve.sem_inc(pt_lo, 2)

            def weight_low(i):
                _, w, p, m, stage = WEIGHTS[i]
                dve.wait_ge(w_hi, i + 1)
                low(w[1][:, :, :].rearrange("p k n -> p (k n)"), stage[0:p],
                    w[0][:, :, :].rearrange("p k n -> p (k n)"), w_lo)

            NEWTON = 3
            STAT = 4 + 3 * NEWTON

            LINKS = 3 * NEWTON + 4

            def scale_link(which, base, i, done):
                v, m, s = mv[which][:, :, 1], mv[which][:, :, 0], sc[which]
                dve.wait_ge(chain, base + i + 1)
                step_, kind = divmod(i - 3, 3)
                if i == 0:
                    dve.sem_inc(dve_go, 1)
                    for t in range(TILES):
                        r = dve.bn_aggr(mv[which][:, t, :], st[which][:, t, :])
                elif i == 1:
                    r = dve.tensor_scalar(s[:, 0, :], v, EPS, None, ALU.add)
                elif i == 2:
                    r = dve.tensor_scalar(s[:, 1, :].bitcast(I32), s[:, 0, :].bitcast(I32), -0.5, float(0x5f3759df),
                                          ALU.mult, ALU.add)
                elif i == LINKS - 1:
                    r = dve.scalar_tensor_tensor(s[:, 4, :], m, -1.0, s[:, 3, :], ALU.mult, ALU.mult)
                elif kind == 0:
                    r = dve.tensor_tensor(s[:, 2, :], s[:, 1, :], s[:, 1, :], ALU.mult)
                elif kind == 1:
                    r = dve.scalar_tensor_tensor(s[:, 2, :], s[:, 2, :], -0.5, s[:, 0, :], ALU.mult, ALU.mult)
                else:
                    out = s[:, 1 if step_ < NEWTON - 1 else 3, :]
                    r = dve.scalar_tensor_tensor(out, s[:, 2, :], 1.5, s[:, 1, :], ALU.add, ALU.mult)
                r.then_inc(done if i == LINKS - 1 else chain, 1)

            def x_stats(n, k, t):
                if t == 0:
                    dve.wait_ge(x_in, 16 * n + 16)
                    dve.wait_ge(xn_done, 4 * n + 1)
                i = dve.bn_stats(st[0][:, t, :], xw[:, k, t, :])
                if t == TILES - 1:
                    i.then_inc(chain, 1)

            def x_link(n, i):
                scale_link(0, 2 * STAT * n, i, ln1)

            def x1_stats(n, k, t):
                if t == 0:
                    dve.wait_ge(xn2_done, n + 1)
                dve.wait_ge(x1_done, 4 * n + t + 5)
                i = dve.bn_stats(st[1][:, t, :], xw[:, k, t, :])
                if t == TILES - 1:
                    i.then_inc(chain, 1)

            def x1_link(n, i):
                scale_link(1, 2 * STAT * n + 3 * STAT, i, ln2)

            def q_low(n, p):
                dve.wait_ge(q_hi, 8 * n + p + 1)
                low(qT[1][:, p % 4, :], ps[:, BQ, :], qT[0][:, p % 4, :], q_lo)

            def xt_low(n, c):
                dve.wait_ge(xt_hi, 2 * n + c + 1)
                low(xT[1][:, c, :], ps[:, BQ, :], xT[0][:, c, :], xt_lo)

            def maxima(n, p, t):
                dve.wait_ge(s_done, 4 * (8 * n + p) + t + 1)
                dve.tensor_reduce(nmax[:, p % 3, t, :], ps[:, t, 0:PK].rearrange("p (h k) -> p h k", h=2),
                                  AX_X, ALU.max, negate=True).then_inc(max_done, 1)

            def recip(n, p):
                dve.wait_ge(exp_done, 4 * (8 * n + p) + 8)
                dve.reciprocal(rden[:, p % 3], den[:, p % 3]).then_inc(rden_done, 1)

            def pt_low(n, p, c):
                dve.wait_ge(pt_hi, 3 * (8 * n + p) + c + 1)
                r = slice(0, CH[c][1])
                low(pT[1][r, c, :], ps[r, BT + (3 * p + c) % 2, :], pT[0][r, c, :], pt_lo)

            def o_low(n, p):
                dve.wait_ge(o_hi, 8 * n + p + 1)
                low(oT[1][:, p, :], ps[:, BV, :], oT[0][:, p, :], o_lo)

            def cx_low(b):
                dve.wait_ge(cx_hi, b + 1)
                low(cx[1][:, :, :], cx_raw[:, :, :], cx[0][:, :, :], cx_lo)

            def k_low(b, j):
                dve.wait_ge(kv_hi, 8 * b + j + 1)
                for h in range(2):
                    r = slice(h * DH, (h + 1) * DH)
                    part = kst[0][r, 2 * j:2 * j + 2, h * KEYS:(h + 1) * KEYS]
                    i = dve.scalar_tensor_tensor(kst[1][r, 2 * j:2 * j + 2, h * KEYS:(h + 1) * KEYS],
                                                 ps[r, j, 0:PK].rearrange("p (a k) -> p a k", a=2),
                                                 SCALE, part.bitcast(F32), ALU.mult, ALU.subtract)
                i.then_inc(kv_lo, 1)

            def v_low(b, j):
                r, c = V_PARTS[j]
                dve.wait_ge(kv_hi, 8 * b + j + 5)
                low(vst[1][r, :, c], ps[r, V_BANKS[j], :].rearrange("p (a d) -> p a d", d=DH), vst[0][r, :, c], kv_lo)

            def residual(n, k, t):
                if t == 0:
                    dve.wait_ge(xb_done, n + 1)
                dve.wait_ge(wo_done, 4 * n + t + 1)
                dve.scalar_tensor_tensor(xw[:, k, t, :], ps[:, BT + t, 0:D], tg[:, 0:1], xw[:, k, t, :],
                                         ALU.mult, ALU.add).then_inc(x1_done, 1)

            def step(n, b, k, p, last):
                change = k == 1 and not last
                ahead = (n, p + 2) if p < 6 else (n + 1, 0) if p == 7 and not last else None

                def between(t):
                    if p == 0 and not is_first(n) and t < TILES:
                        x1_stats(n - 1, 1 - k, t)
                    if p == 1 and not is_first(n):
                        for i in range(t * LINKS // 5, (t + 1) * LINKS // 5):
                            x1_link(n - 1, i)
                    if p == 3 and not last and t in (1, 3):
                        x_stats(n + 1, 1 - k, t // 2)
                    if p == 4 and not last and t == 0:
                        x_stats(n + 1, 1 - k, 2)
                        x_stats(n + 1, 1 - k, 3)
                    if p == 4 and not last and t > 0:
                        for i in range((t - 1) * LINKS // 4, t * LINKS // 4):
                            x_link(n + 1, i)

                if ahead:
                    maxima(*ahead, 0)
                if p < 7:
                    recip(n, p + 1)
                between(0)
                pt_low(n, p, 0)
                if p == 6 and not last:
                    xt_low(n + 1, 1)
                between(1)
                if p == 6 and change:
                    k_low(b + 1, 0)
                if p == 4:
                    o_low(n, p - 1)
                if ahead:
                    maxima(*ahead, 1)
                if p >= 1 and p != 4:
                    o_low(n, p - 1)
                pt_low(n, p, 1)
                between(2)
                if ahead:
                    maxima(*ahead, 2)
                if p == 6 and change:
                    k_low(b + 1, 1)
                if p < 4:
                    q_low(n, p + 4)
                if p > 5 and not last:
                    q_low(n + 1, p - 6)
                pt_low(n, p, 2)
                between(3)
                if ahead:
                    maxima(*ahead, 3)
                between(4)
                if p == 5 and not last:
                    xt_low(n + 1, 0)
                if p == 4 and change:
                    cx_low(b + 1)
                if p == 6 and change:
                    k_low(b + 1, 2)
                    k_low(b + 1, 3)

            def blk(n, b, k, last):
                for p in range(2, PAIRS):
                    step(n, b, k, p, last)
                if last:
                    o_low(n, 7)
                    dve.sem_inc(chain, STAT)
                    residual(n, k, 0)
                    for t in range(1, TILES):
                        residual(n, k, t)
                        x1_stats(n, k, t - 1)
                    x1_stats(n, k, TILES - 1)
                    for i in range(LINKS):
                        x1_link(n, i)
                    return
                maxima(n + 1, 1, 0)
                recip(n + 1, 0)
                o_low(n, 7)
                q_low(n + 1, 2)
                residual(n, k, 0)
                maxima(n + 1, 1, 1)
                q_low(n + 1, 3)
                residual(n, k, 1)
                maxima(n + 1, 1, 2)
                residual(n, k, 2)
                maxima(n + 1, 1, 3)
                residual(n, k, 3)
                if k == 1:
                    for j in range(4):
                        v_low(b + 1, j)
                for p in range(2):
                    step(n + 1, b + k, 1 - k, p, False)

            weight_low(0)
            cx_low(0)
            for t in range(TILES):
                x_stats(0, 0, t)
            for i in range(LINKS):
                x_link(0, i)
            dve.sem_inc(chain, STAT)
            dve.wait_ge(tg_done, 1)
            dve.tensor_scalar(tbo[:, :], tbo[:, :], tg[:, 0:1], None, ALU.mult).then_inc(tbo_done, 1)
            weight_low(1)
            dve.wait_ge(zeroed, 4)
            for j in range(4):
                k_low(0, j)
            weight_low(2)
            xt_low(0, 0)
            v_low(0, 0)
            xt_low(0, 1)
            v_low(0, 1)
            q_low(0, 0)
            v_low(0, 2)
            q_low(0, 1)
            for t in range(TILES):
                maxima(0, 0, t)
            q_low(0, 2)
            maxima(0, 1, 0)
            recip(0, 0)
            maxima(0, 1, 1)
            q_low(0, 3)
            maxima(0, 1, 2)
            maxima(0, 1, 3)
            v_low(0, 3)
            weight_low(3)
            step(0, 0, 0, 0, False)
            weight_low(4)
            step(0, 0, 0, 1, False)

            with dve.Fori(0, B - 1) as b:
                blk(2 * b, b, 0, False)
                blk(2 * b + 1, b, 1, False)
            blk(NB - 2, B - 1, 0, False)
            blk(NB - 1, B - 1, 1, True)

        @block.tensor
        def _(pe):
            def mm3(out, parts, first, last):
                n = 3 * len(parts)
                i = 0
                for a, b in parts:
                    for u, v in ((a[0], b[0]), (a[0], b[1]), (a[1], b[0])):
                        r = pe.matmul(out, u, v, start=first and i == 0, stop=last and i == n - 1)
                        i += 1
                return r

            def cut(pair, *key):
                return [w[key] for w in pair]

            ALLP = slice(None)

            def transposes(n, c):
                if c == 0:
                    if not is_first(n):
                        pe.wait_ge(q_lo, 8 * n)
                    pe.wait_ge(xn_done, 4 * n + 5)
                else:
                    pe.wait_ge(xt_lo, 2 * n + 1)
                for t in range(TILES):
                    i = pe.transpose(ps[:, BQ, t * P:(t + 1) * P], xn[:, t, c * P:(c + 1) * P], ident[:, :])
                i.then_inc(xt_done, 1)

            def project_q(n, b, k, p):
                if p == 0:
                    pe.wait_ge(xt_lo, 2 * n + 2)
                elif p == 4:
                    pe.wait_ge(x1_done, 4 * n + 3)
                    if k == 0:
                        pe.wait_ge(kv_lo, 8 * b + 8)
                else:
                    pe.wait_ge(q_lo, 8 * n + p)
                mm3(ps[:, BQ, :], [(cut(wq, ALLP, c, slice(p * P, (p + 1) * P)), cut(xT, ALLP, c, ALLP))
                                   for c in range(NC)], True, True).then_inc(q_done, 1)

            def scores(n, b, k, p, t):
                if t == 0:
                    pe.wait_ge(q_lo, 8 * n + p + 1)
                if p == 0 and k == 0:
                    pe.wait_ge(kv_lo, 8 * b + t + 1)
                pe.wait_ge(exp_done, 4 * (8 * n + p) + t + 1)
                mm3(ps[:, t, 0:PK], [(cut(qT, ALLP, p % 4, slice(t * P, (t + 1) * P)), cut(kst, ALLP, p, ALLP))],
                    True, True).then_inc(s_done, 1)

            def transpose_p(n, b, k, p, c):
                c0, m = CH[c]
                if c == 0:
                    pe.wait_ge(p_done, 8 * n + p + 1)
                if p == 0 and c < 2:
                    pe.wait_ge(x1_done, 4 * n + c + 1)
                    if k == 0:
                        pe.wait_ge(kv_lo, 8 * b + c + 5)
                pe.wait_ge(pt_lo, 3 * (8 * n + p) + c + 1)
                for t in range(TILES):
                    i = pe.transpose(ps[0:m, BT + (3 * p + c) % 2, t * P:(t + 1) * P],
                                     prob[:, p % 3, t, c0:c0 + m], ident[:, :])
                i.then_inc(t_done, 1)

            def values(n, b, k, p, c):
                m = CH[c][1]
                if c == 0:
                    pe.wait_ge(o_lo, 8 * n + p + 1)
                if p == 0 and c == 0:
                    pe.wait_ge(x1_done, 4 * n + 4)
                    if k == 0:
                        pe.wait_ge(kv_lo, 8 * b + 8)
                pe.wait_ge(pt_lo, 3 * (8 * n + p) + c + 3)
                cols = (slice(0, P), slice(3 * DH, 3 * DH + P), slice(DH, DH + P))[c]
                i = mm3(ps[:, BV, :], [(cut(vst, slice(0, m), p, cols), cut(pT, slice(0, m), c, ALLP))],
                        c == 0, c == 2)
                if c == 2:
                    i.then_inc(pv_done, 1)

            def out_proj(n, t, last):
                if t == 2 and not last:
                    pe.wait_ge(q_lo, 8 * n + 12)
                for p in range(PAIRS):
                    if t == 0 and p >= PAIRS - 2:
                        pe.wait_ge(o_lo, 8 * n + p + 2)
                    i = mm3(ps[:, BT + t, 0:D], [(cut(oT, ALLP, p, slice(t * P, (t + 1) * P)), cut(wo, ALLP, p, ALLP))],
                            p == 0, p == PAIRS - 1)
                i.then_inc(wo_done, 1)

            def project_k(b, j, n):
                if n is not None:
                    pe.wait_ge(exp_done, 4 * (8 * n + PAIRS) + j + 1)
                if j == 0:
                    pe.wait_ge(cx_lo, b + 2)
                for a in range(2):
                    p = 2 * j + a
                    i = mm3(ps[:, j, a * KEYS:(a + 1) * KEYS],
                            [(cut(wk, ALLP, c, slice(p * P, (p + 1) * P)), cut(cx, ALLP, c, slice(0, KEYS)))
                             for c in range(2)], True, True)
                i.then_inc(kv_done, 1)

            def project_v(b, j, n):
                if n is not None:
                    pe.wait_ge(x1_done, 4 * n + V_BANKS[j] - BT + 5)
                s = (slice(0, KA), slice(KEYS, KEYS + P), slice(KEYS, KEYS + P), slice(MID, KEYS))[j]
                m, odd = s.stop - s.start, j // 2
                rhs = [[w[:, c, :].rearrange("p (a two d) -> p two a d", two=2, d=DH)[:, odd] for w in wv]
                       for c in range(2)]
                mm3(ps[0:m, V_BANKS[j], :].rearrange("p (a d) -> p a d", d=DH),
                    [(cut(cx, ALLP, c, s), rhs[c]) for c in range(2)], True, True).then_inc(kv_done, 1)

            def step(n, b, k, p, last):
                change = k == 1 and not last
                here, nxt = (n, b, k), (n + 1, b + k, 1 - k)
                ahead = (*here, p + 2) if p < 6 else (*nxt, 0) if p == 7 and not last else None
                if ahead:
                    scores(*ahead, 0)
                if p == 6 and change:
                    project_k(b + 1, 0, n)
                transpose_p(*here, p, 0)
                if p == 6 and not last:
                    transposes(n + 1, 1)
                early = p == 4
                if p >= 1:
                    values(*here, p - 1, 1)
                if early:
                    values(*here, p - 1, 2)
                if ahead:
                    scores(*ahead, 1)
                if p == 6 and change:
                    project_k(b + 1, 1, n)
                if p >= 1 and not early:
                    values(*here, p - 1, 2)
                transpose_p(*here, p, 1)
                if ahead:
                    scores(*ahead, 2)
                if p == 6 and change:
                    project_k(b + 1, 2, n)
                if p < 4:
                    project_q(*here, p + 4)
                if p > 5 and not last:
                    project_q(*nxt, p - 6)
                transpose_p(*here, p, 2)
                if ahead:
                    scores(*ahead, 3)
                if p == 6 and change:
                    project_k(b + 1, 3, n)
                if p == 5 and not last:
                    transposes(n + 1, 0)
                values(*here, p, 0)

            def blk(n, b, k, last):
                nxt = (n + 1, b + k, 1 - k)
                for p in range(2, PAIRS):
                    step(n, b, k, p, last)
                values(n, b, k, 7, 1)
                if not last:
                    scores(*nxt, 1, 0)
                values(n, b, k, 7, 2)
                if not last:
                    project_q(*nxt, 2)
                out_proj(n, 0, last)
                for t in range(1, TILES):
                    if not last:
                        scores(*nxt, 1, t)
                    if t == 1 and not last:
                        project_q(*nxt, 3)
                    out_proj(n, t, last)
                if last:
                    return
                if k == 1:
                    for j in range(4):
                        project_v(b + 1, j, n)
                for p in range(2):
                    step(*nxt, p, False)

            pe.sem_inc(kv_done, 1)
            pe.sem_inc(t_done, 4)
            pe.wait_ge(w_lo, 1)
            for j in range(4):
                project_k(0, j, None)
            pe.wait_ge(ident_done, 1)
            transposes(0, 0)
            pe.wait_ge(w_lo, 2)
            project_v(0, 0, None)
            transposes(0, 1)
            project_v(0, 1, None)
            pe.wait_ge(w_lo, 3)
            project_q(0, 0, 0, 0)
            project_v(0, 2, None)
            project_q(0, 0, 0, 1)
            for t in range(TILES):
                scores(0, 0, 0, 0, t)
            for p in (2, 3):
                project_q(0, 0, 0, p)
                scores(0, 0, 0, 1, 2 * p - 4)
                scores(0, 0, 0, 1, 2 * p - 3)
            pe.wait_ge(q_lo, 4)
            project_v(0, 3, None)
            for p in range(2):
                step(0, 0, 0, p, False)

            with pe.Fori(0, B - 1) as b:
                blk(2 * b, b, 0, False)
                blk(2 * b + 1, b, 1, False)
            blk(NB - 2, B - 1, 0, False)
            blk(NB - 1, B - 1, 1, True)


def feed_forward(nc, comb, x1_dram, g_ffn, gateT, upT, downT, routerT, gate_sT, up_sT, down_sT, out):
    T, D2 = comb.shape
    D = D2 // 2
    E, _, H = gateT.shape
    NC, HC = D // P, H // P
    NT = T // P
    NB = T // BLK
    ST = NT + E - 1
    SC = ST + 3
    EW = 3 * H * NC
    OOB = float(2 * T)
    assert HC * D == NC * H and NC == 2 and NT * E <= 256 and SC % 2 == 0

    with ExitStack() as outer:
        W = outer.enter_context(nc.sbuf_tensor("W", [P, E * EW], F32))
        Wv = W[:, :].rearrange("p (e w) -> p e w", e=E)
        ident = outer.enter_context(nc.sbuf_tensor("ident2", [P, P], F32))
        tg = outer.enter_context(nc.sbuf_tensor("tg2", [P, 1], F32))
        slot_token = outer.enter_context(nc.sbuf_tensor("slot_token", [P, SC], I32))
        tile_expert = outer.enter_context(nc.sbuf_tensor("tile_expert", [P, SC], I32))
        shared_and_route(nc, comb, x1_dram, g_ffn, gateT, upT, downT, routerT, gate_sT, up_sT, down_sT,
                         Wv, ident, tg, slot_token, tile_expert, OOB)
        routed_experts(nc, comb, W, ident, tg, slot_token, tile_expert, out, E, EW, H, T, ST)


def shared_and_route(nc, comb, x1_dram, g_ffn, gateT, upT, downT, routerT, gate_sT, up_sT, down_sT,
                     Wv, ident, tg, slot_token, tile_expert, OOB):
    T, D = comb.shape[0], comb.shape[1] // 2
    E, _, H = gateT.shape
    NC, HC, NT, NB = D // P, H // P, T // P, T // BLK
    SC = slot_token.shape[1]
    with ExitStack() as ctx:
        def sb(name, shape, dt=F32):
            return ctx.enter_context(nc.sbuf_tensor(name, shape, dt))

        def sem(name):
            return ctx.enter_context(nc.semaphore(name))

        xT = sb("xT_all", [P, NC, T])
        wg = [sb(f"wg_{s}", [P, NC, H], F32R) for s in ("hi", "lo")]
        wu = [sb(f"wu_{s}", [P, NC, H], F32R) for s in ("hi", "lo")]
        wd = [sb(f"wd_{s}", [P, HC, D], F32R) for s in ("hi", "lo")]
        xs = [sb(f"xs_{s}", [P, 2, NC, BLK], F32R) for s in ("hi", "lo")]
        hT = [sb(f"hT_{s}", [P, HC, BLK], F32R) for s in ("hi", "lo")]
        work = sb("work", [P, 4096])
        xl = work[:, 0:2048].rearrange("p (a t c) -> p a t c", a=2, t=TILES)
        hot = Wv[:, E - 2:E, :].rearrange("p e w -> p (e w)")
        HOT = [0, NT * P // 2, (NT * P + NT * SC) // 2, (NT * P + 3 * NT * SC) // 2]
        row1 = hot[:, HOT[0]:HOT[1]].bitcast(BF16).rearrange("p (i r) -> p i r", i=NT)
        col1 = hot[:, HOT[1]:HOT[2]].bitcast(BF16).rearrange("p (i a) -> p i a", i=NT)
        colv = hot[:, HOT[2]:HOT[3]].bitcast(BF16).rearrange("p (i w) -> p i w", i=NT)
        base = work[:, 0:2048].rearrange("p (a t c) -> p a t c", a=2, t=TILES)
        sg = work[:, 2048:3072].rearrange("p (a c) -> p a c", a=2)
        hf = work[:, 3072:4096].rearrange("p (a c) -> p a c", a=2)
        stage = Wv[:, E - 1, :]
        rT = sb("rT", [P, NC, E])
        rTs = [sb(f"rT_{s}", [P, NC, E], F32R) for s in ("hi", "lo")]
        gate = sb("gate2", [P, 1])
        before = sb("before", [P, P], BF16)
        ones = sb("ones", [P, P], BF16)
        count = sb("count", [P, P])
        upto = sb("upto", [P, E, E])
        token1 = sb("token1", [P, 1])
        desc = sb("desc", [P, E])
        c128 = sb("c128", [P, NT])
        top = sb("top", [P, NT])
        pick = sb("pick", [P, NT, E])
        onehot = sb("onehot", [P, NT + 1, E], BF16)
        lt = hot[0:E, 0:2 * BLK].rearrange("e (a c) -> e a c", a=2)
        cmp = hot[:, HOT[3]:HOT[3] + SC * E].rearrange("p (a e) -> p a e", e=E)
        cmpn = hot[:, HOT[3] + SC * E:HOT[3] + (SC + NT) * E].rearrange("p (e i) -> p e i", e=E)
        ranks = sb("ranks", [P, (NT + 1) * E])
        tiles_of = sb("tiles_of", [P, E])
        prod = sb("prod", [P, E, E])
        end = sb("end", [P, E])
        first = sb("first", [P, E])
        slot = sb("slot", [P, NT])
        sloti = sb("sloti", [P, 3, NT], I32)
        slotf = sb("slotf", [P, 2, NT])
        tab = sb("tab", [P, 4, SC])
        et = sb("et", [P, SC])

        ps = ctx.enter_context(nc.psum_tensor("ps2", [P, 8, 512], F32))
        LT, LOG, RANK, TAB = 4, 6, 7, 0
        sh_in = sem("sh_in"); rt_in = sem("rt_in"); rt_lo = sem("rt_lo"); g_in = sem("g_in"); consts = sem("consts")
        sh_hi = sem("sh_hi"); sh_lo = sem("sh_lo"); w_in = sem("w_in"); w_in_last = sem("w_in_last")
        xl_in = [sem(f"xl_in{k}") for k in range(2)]; xt_ps = sem("xt_ps")
        x_kept = [sem(f"x_kept{c}") for c in range(NC)]
        logits = sem("logits"); onehot_done = sem("onehot_done"); rank_done = sem("rank_done")
        lt_ps = sem("lt_ps"); lt_sb = sem("lt_sb"); rank_read = sem("rank_read"); table_read = sem("table_read")
        place_done = sem("place_done"); table_done = sem("table_done"); tg_done = sem("tg2_done")
        link_s = sem("link2"); xs_hi = sem("xs_hi"); xs_lo = sem("xs_lo")
        gu_done = sem("gu_done"); silu_done = sem("silu_done"); h_done = sem("h_done")
        h_hi = sem("h_hi"); h_lo = sem("h_lo"); y_done = sem("y_done"); base_done = sem("base_done")
        x1_in = [sem(f"x1_in{k}") for k in range(2)]
        base_out = [sem(f"base_out{k}") for k in range(2)]; go = sem("go2"); routed = sem("routed")

        xn2b = comb[:, 0:D].rearrange("(n t p) c -> n p t c", t=TILES, p=P)
        baseb = comb[:, D:2 * D].rearrange("(n t p) c -> n p t c", t=TILES, p=P)
        x1b = x1_dram.rearrange("(n t p) c -> n p t c", t=TILES, p=P)
        block = ctx.enter_context(nc.Block())

        def load_expert(eng, e, w_in):
            for j, w in enumerate((gateT, upT)):
                eng.dma_start(Wv[:, e, 0:2 * NC * H].rearrange("p (k j h) -> p k j h", k=NC, j=2)[:, :, j, :],
                              w[e].rearrange("(k p) h -> p k h", p=P)).then_inc(w_in, 16)
            eng.dma_start(Wv[:, e, 2 * NC * H:3 * NC * H].rearrange("p (k c) -> p k c", k=HC),
                          downT[e].rearrange("(k p) c -> p k c", p=P)).then_inc(w_in, 16)

        @block.sync
        def _(sp):
            sp.dma_start(xl[:, 0], xn2b[0]).then_inc(xl_in[0], 16)
            sp.dma_start(rT[:, :, :], routerT.rearrange("(k p) e -> p k e", p=P)).then_inc(rt_in, 16)
            sp.dma_start(xl[:, 1], xn2b[1]).then_inc(xl_in[1], 16)
            sp.dma_start(gate[:, :], g_ffn.rearrange("(a b) -> a b", a=1).broadcast_to([P, 1])).then_inc(g_in, 16)
            for j, w in enumerate((gate_sT, up_sT, down_sT)):
                sp.dma_start(stage[:, j * 1024:(j + 1) * 1024].rearrange("p (k n) -> p k n", n=w.shape[1]),
                             w.rearrange("(k p) n -> p k n", p=P)).then_inc(sh_in, 16)
            with sp.Fori(0, NB // 2 - 1) as i:
                for k in range(2):
                    sp.wait_ge(xt_ps, 4 * i + 2 * k + 2)
                    sp.dma_start(xl[:, k], xn2b[2 * i + k + 2]).then_inc(xl_in[k], 16)

            def base_io(i, k, more):
                sp.wait_ge(base_done, 8 * i + 4 * k + 8)
                sp.dma_start(baseb[2 * i + k], base[:, k]).then_inc(base_out[k], 16)
                if more:
                    sp.wait_ge(base_out[k], 16 * i + 16)
                    sp.dma_start(base[:, k], x1b[2 * i + k + 2]).then_inc(x1_in[k], 16)

            sp.wait_ge(xt_ps, 2 * NB)
            for k in range(2):
                sp.dma_start(base[:, k], x1b[k]).then_inc(x1_in[k], 16)
            sp.wait_ge(table_done, 1)
            for e in (E - 2, E - 1):
                load_expert(sp, e, w_in_last)
            with sp.Fori(0, NB // 2 - 1) as i:
                base_io(i, 0, True)
                base_io(i, 1, True)
            for k in range(2):
                base_io(NB // 2 - 1, k, False)
            for k in range(2):
                sp.wait_ge(base_out[k], 16 * (NB // 2))

        @block.gpsimd
        def _(pool):
            pool.sem_inc(h_lo, 2)
            pool.memset(ident[:, :], 0.0).then_inc(go, 1)
            pool.memset(before[:, :], 1.0).then_inc(go, 1)
            pool.memset(upto[:, :, :], 1.0).then_inc(go, 1)
            pool.memset(ones[:, :], 1.0).then_inc(consts, 1)
            pool.memset(onehot[:, :, :], 0.0).then_inc(consts, 1)
            pool.iota(count[:, :], pattern=[[1, P]], base=0, channel_multiplier=0,
                      allow_small_or_imprecise_dtypes=True).then_inc(consts, 1)
            pool.iota(token1[:, :], pattern=[[0, 1]], base=1, channel_multiplier=1,
                      allow_small_or_imprecise_dtypes=True).then_inc(consts, 1)
            pool.wait_ge(go, 3)
            pool.affine_select(out=ident[:, :], in_=ident[:, :], compare_op=ALU.not_equal, fill=1.0,
                               base=0, pattern=[[-1, P]], channel_multiplier=1).then_inc(consts, 1)
            pool.affine_select(out=before[:, :], in_=before[:, :], compare_op=ALU.is_gt, fill=0.0,
                               base=0, pattern=[[1, P]], channel_multiplier=-1).then_inc(consts, 1)
            pool.affine_select(out=upto[:, :, :], in_=upto[:, :, :], compare_op=ALU.is_ge, fill=0.0,
                               base=0, pattern=[[1, E], [-1, E]], channel_multiplier=0).then_inc(consts, 1)
            pool.wait_ge(xl_in[1], 16 * (NB // 2))
            for e in range(E - 2):
                load_expert(pool, e, w_in)

            def h_low(n, j):
                pool.wait_ge(h_hi, 4 * n + j + 1)
                pool.tensor_tensor(hT[1][:, j, :], hf[:, j % 2, :], hT[0][:, j, :].bitcast(F32),
                                   ALU.subtract).then_inc(h_lo, 1)

            with pool.Fori(0, NB) as n:
                for j in range(HC):
                    h_low(n, j)
            pool.wait_ge(w_in, 16 * 3 * (E - 2))
            pool.wait_ge(w_in_last, 16 * 3 * 2)

        @block.scalar
        def _(act):
            act.wait_ge(g_in, 16)
            act.activation(tg[:, :], gate[:, :], ACT.Tanh).then_inc(tg_done, 1)

            def rows_high(i, k):
                for c in range(NC):
                    act.wait_ge(xt_ps, 4 * i + 2 * k + c + 1)
                    if c == 0:
                        act.copy(xT[:, 0, bass.ds(i * (2 * BLK) + k * BLK, BLK)], ps[:, 2 * k, :])\
                           .then_inc(x_kept[0], 1)
                    act.copy(xs[0][:, k, c, :], ps[:, 2 * k + c, :]).then_inc(xs_hi, 1)

            def weight_high(j):
                w = (wg, wu, wd)[j]
                act.wait_ge(sh_in, 48)
                act.copy(w[0][:, :, :].rearrange("p k n -> p (k n)"), stage[:, j * 1024:(j + 1) * 1024])\
                   .then_inc(sh_hi, 1)

            def logits_out(i, k):
                act.wait_ge(lt_ps, 2 * i + k + 1)
                act.copy(lt[:, k, :], ps[0:E, LT + k, :]).then_inc(lt_sb, 1)

            def x_high(n, k):
                act.copy(xs[0][:, k], xT[:, :, bass.ds(n * BLK, BLK)]).then_inc(xs_hi, 1)

            rows_high(0, 0)
            with act.Fori(0, NB // 2 - 1) as i:
                rows_high(i, 1)
                logits_out(i, 0)
                rows_high(i + 1, 0)
                logits_out(i, 1)
            rows_high(NB // 2 - 1, 1)
            logits_out(NB // 2 - 1, 0)
            for c in range(NC):
                act.wait_ge(x_kept[c], NB)
            x_high(0, 0)
            weight_high(0)
            logits_out(NB // 2 - 1, 1)
            weight_high(1)

            def silu(n, j):
                act.wait_ge(gu_done, 4 * n + j + 1)
                act.activation(sg[:, j % 2, :], ps[:, 2 * (j % 2), :], ACT.Silu).then_inc(silu_done, 1)

            def high(n, j):
                act.wait_ge(h_done, 4 * n + j + 1)
                act.copy(hT[0][:, j, :], hf[:, j % 2, :]).then_inc(h_hi, 1)

            weight_high(2)
            for j in range(2):
                silu(0, j)
                high(0, j)

            def blk(n, k, last):
                silu(n, 2)
                high(n, 2)
                if not last:
                    x_high(n + 1, 1 - k)
                silu(n, 3)
                high(n, 3)
                if not last:
                    for j in range(2):
                        silu(n + 1, j)
                        high(n + 1, j)

            blk(0, 0, False)
            blk(1, 1, False)
            with act.Fori(1, NB // 2 - 1) as i:
                blk(2 * i, 0, False)
                blk(2 * i + 1, 1, False)
            blk(NB - 2, 0, False)
            blk(NB - 1, 1, True)

        @block.vector
        def _(dve):
            links = [0]

            def link(i):
                links[0] += 1
                i.then_inc(link_s, 1)
                dve.wait_ge(link_s, links[0])

            dve.sem_inc(base_done, 4)
            dve.wait_ge(rt_in, 16)
            link(dve.tensor_copy(rTs[0][:, :, :], rT[:, :, :]))
            dve.tensor_tensor(rTs[1][:, :, :], rT[:, :, :], rTs[0][:, :, :].bitcast(F32), ALU.subtract)\
               .then_inc(rt_lo, 1)
            def rows_low(i, k):
                for c in range(NC):
                    dve.wait_ge(xs_hi, 4 * i + 2 * k + c + 1)
                    dve.tensor_tensor(xs[1][:, k, c, :], ps[:, 2 * k + c, :], xs[0][:, k, c, :].bitcast(F32),
                                      ALU.subtract).then_inc(xs_lo, 1)
                dve.tensor_copy(xT[:, 1, bass.ds(i * (2 * BLK) + k * BLK, BLK)], ps[:, 2 * k + 1, :])\
                   .then_inc(x_kept[1], 1)

            def weight_low(j):
                w = (wg, wu, wd)[j]
                dve.wait_ge(sh_hi, j + 1)
                dve.tensor_tensor(w[1][:, :, :].rearrange("p k n -> p (k n)"), stage[:, j * 1024:(j + 1) * 1024],
                                  w[0][:, :, :].rearrange("p k n -> p (k n)").bitcast(F32),
                                  ALU.subtract).then_inc(sh_lo, 1)

            def x_low(n, k):
                dve.wait_ge(xs_hi, n + 2 * NB + 1)
                dve.tensor_tensor(xs[1][:, k], xT[:, :, bass.ds(n * BLK, BLK)], xs[0][:, k].bitcast(F32),
                                  ALU.subtract).then_inc(xs_lo, 1)

            rows_low(0, 0)
            with dve.Fori(0, NB // 2 - 1) as i:
                rows_low(i, 1)
                rows_low(i + 1, 0)
            rows_low(NB // 2 - 1, 1)
            dve.wait_ge(x_kept[1], NB)
            x_low(0, 0)
            for j in range(2):
                weight_low(j)

            def gated(n, j):
                dve.wait_ge(h_lo, 4 * n + j + 1)
                dve.wait_ge(silu_done, 4 * n + j + 1)
                dve.tensor_tensor(hf[:, j % 2, :], ps[:, 2 * (j % 2) + 1, :], sg[:, j % 2, :],
                                  ALU.mult).then_inc(h_done, 1)

            def add_base(n, i, k):
                dve.wait_ge(x1_in[k], 16 * i + 16)
                for t in range(TILES):
                    dve.wait_ge(y_done, 4 * n + t + 1)
                    dve.scalar_tensor_tensor(base[:, k, t, :], ps[:, 4 + t, 0:D], tg[:, 0:1], base[:, k, t, :],
                                             ALU.mult, ALU.add).then_inc(base_done, 1)

            dve.wait_ge(consts, 7)
            link(dve.tensor_scalar(desc[:, :], count[:, 0:E], -1.0, float(E), ALU.mult, ALU.add))
            link(dve.tensor_scalar(c128[:, :], count[:, 0:NT], float(P), None, ALU.mult))
            dve.wait_ge(logits, 1)
            lg = ps[:, LOG, 0:NT * E].rearrange("p (i e) -> p i e", e=E)

            def bc(ap, axis, shape):
                return ap.unsqueeze(axis).broadcast_to(shape)

            link(dve.tensor_reduce(top[:, :], lg, AX_X, ALU.max))
            link(dve.tensor_tensor(pick[:, :, :], lg, bc(top[:, :], 2, [P, NT, E]), ALU.is_equal))
            link(dve.tensor_tensor(pick[:, :, :], pick[:, :, :], bc(desc[:, :], 1, [P, NT, E]), ALU.mult))
            link(dve.tensor_reduce(top[:, :], pick[:, :, :], AX_X, ALU.max))
            dve.tensor_tensor(onehot[:, 0:NT, :], pick[:, :, :], bc(top[:, :], 2, [P, NT, E]), ALU.is_equal)\
               .then_inc(onehot_done, 1)
            weight_low(2)
            dve.wait_ge(tg_done, 1)
            gated(0, 0)
            dve.wait_ge(rank_done, 1)
            dve.tensor_copy(ranks[:, :], ps[:, RANK, 0:(NT + 1) * E]).then_inc(rank_read, 1)
            gated(0, 1)
            dve.wait_ge(rank_read, 1)
            rank = ranks[:, 0:NT * E].rearrange("p (i e) -> p i e", e=E)
            many = ranks[:, NT * E:(NT + 1) * E]
            link(dve.tensor_tensor(cmpn[:, :, :], bc(c128[:, :], 1, [P, E, NT]), bc(many, 2, [P, E, NT]),
                                   ALU.is_lt))
            link(dve.tensor_reduce(tiles_of[:, :], cmpn[:, :, :], AX_X, ALU.add))
            link(dve.tensor_tensor(prod[:, :, :], upto[:, :, :], bc(tiles_of[:, :], 1, [P, E, E]), ALU.mult))
            link(dve.tensor_reduce(end[:, :], prod[:, :, :], AX_X, ALU.add))
            link(dve.tensor_tensor(first[:, :], end[:, :], tiles_of[:, :], ALU.subtract))
            link(dve.tensor_tensor(cmp[:, :, :], bc(count[:, 0:SC], 2, [P, SC, E]), bc(end[:, :], 1, [P, SC, E]),
                                   ALU.is_ge))
            link(dve.tensor_reduce(et[:, :], cmp[:, :, :], AX_X, ALU.add))
            dve.tensor_scalar(tile_expert[:, :], et[:, :], float(E - 1), None, ALU.min).then_inc(routed, 1)
            gated(0, 2)
            x_low(1, 1)
            link(dve.scalar_tensor_tensor(pick[:, :, :], bc(first[:, :], 1, [P, NT, E]), float(P), rank,
                                          ALU.mult, ALU.add))
            link(dve.tensor_tensor(pick[:, :, :], pick[:, :, :], onehot[:, 0:NT, :], ALU.mult))
            link(dve.tensor_reduce(slot[:, :], pick[:, :, :], AX_X, ALU.add))
            link(dve.tensor_copy(sloti[:, 0, :], slot[:, :]))
            link(dve.tensor_scalar(sloti[:, 1, :], sloti[:, 0, :], P - 1, None, ALU.bitwise_and))
            link(dve.tensor_scalar(sloti[:, 2, :], sloti[:, 0, :], 7, None, ALU.logical_shift_right))
            link(dve.tensor_copy(slotf[:, :, :], sloti[:, 1:3, :]))
            gated(0, 3)
            half = NT // 2
            for i in (0, half):
                dve.tensor_tensor(row1[:, i:i + half, :], bc(count[:, :], 1, [P, half, P]),
                                  bc(slotf[:, 0, i:i + half], 2, [P, half, P]), ALU.is_equal).then_inc(place_done, 1)
                if i == 0:
                    gated(1, 0)
            add_base(0, 0, 0)
            gated(1, 1)
            link(dve.tensor_tensor(col1, bc(count[:, 0:SC], 1, [P, NT, SC]), bc(slotf[:, 1, :], 2, [P, NT, SC]),
                                   ALU.is_equal))
            dve.tensor_scalar(colv[:, :, 0:SC], col1, token1[:, 0:1], None, ALU.mult).then_inc(place_done, 1)
            gated(1, 2)
            x_low(2, 0)
            dve.tensor_tensor(colv[:, :, SC:2 * SC], col1, bc(count[:, 0:NT], 2, [P, NT, SC]), ALU.mult)\
               .then_inc(place_done, 1)
            gated(1, 3)
            dve.wait_ge(table_done, 1)
            link(dve.tensor_copy(tab[:, 0, :], ps[:, TAB, 0:SC]))
            dve.scalar_tensor_tensor(tab[:, 1, :], ps[:, TAB, SC:2 * SC], float(P), tab[:, 0, :],
                                     ALU.mult, ALU.add).then_inc(table_read, 1)
            dve.wait_ge(table_read, 1)
            link(dve.tensor_scalar(tab[:, 2, :], tab[:, 0, :], 0.0, OOB, ALU.is_equal, ALU.mult))
            dve.scalar_tensor_tensor(slot_token[:, :], tab[:, 1, :], -1.0, tab[:, 2, :], ALU.add, ALU.add)\
               .then_inc(routed, 1)
            dve.wait_ge(routed, 2)
            gated(2, 0)
            add_base(1, 0, 1)
            gated(2, 1)

            def blk(i, k, last):
                n = 2 * i + k
                gated(n, 2)
                if not last:
                    x_low(n + 1, 1 - k)
                gated(n, 3)
                if not last:
                    gated(n + 1, 0)
                add_base(n, i, k)
                if not last:
                    gated(n + 1, 1)

            with dve.Fori(1, NB // 2 - 1) as i:
                blk(i, 0, False)
                blk(i, 1, False)
            blk(NB // 2 - 1, 0, False)
            blk(NB // 2 - 1, 1, True)

        @block.tensor
        def _(pe):
            def mm3(out, parts, first, last):
                n = 3 * len(parts)
                i = 0
                for a, b in parts:
                    for u, v in ((a[0], b[0]), (a[0], b[1]), (a[1], b[0])):
                        r = pe.matmul(out, u, v, start=first and i == 0, stop=last and i == n - 1)
                        i += 1
                return r

            def transposes(i, k):
                pe.wait_ge(xl_in[k], 16 * i + 16)
                for c in range(NC):
                    for t in range(TILES):
                        r = pe.transpose(ps[:, 2 * k + c, t * P:(t + 1) * P], xl[:, k, t, c * P:(c + 1) * P],
                                         ident[:, :])
                    r.then_inc(xt_ps, 1)

            def block_logits(i, k):
                pe.wait_ge(xs_lo, 4 * i + 2 * k + 2)
                pe.wait_ge(x_kept[1], 2 * i + k + 1)
                mm3(ps[0:E, LT + k, :], [([w[:, c, :] for w in rTs], [w[:, k, c, :] for w in xs])
                                         for c in range(NC)], True, True).then_inc(lt_ps, 1)

            def logit_rows(i, k):
                pe.wait_ge(lt_sb, 2 * i + k + 1)
                for t in range(TILES):
                    r = pe.matmul(ps[:, LOG, bass.ds(i * (2 * TILES * E) + (k * TILES + t) * E, E)],
                                  lt[:, k, t * P:(t + 1) * P], ident[0:E, 0:E], start=True, stop=True)
                return r

            def gate_up(n, k, j):
                if j == 0:
                    pe.wait_ge(xs_lo, 2 * NB + n + 1)
                for m, w in enumerate((wg, wu)):
                    r = mm3(ps[:, 2 * (j % 2) + m, :],
                            [([v[:, c, j * P:(j + 1) * P] for v in w], [v[:, k, c, :] for v in xs])
                             for c in range(NC)], True, True)
                r.then_inc(gu_done, 1)

            def down(n, j):
                pe.wait_ge(h_lo, 4 * n + j + 3)
                for t in range(TILES):
                    if j == 0:
                        pe.wait_ge(base_done, 4 * n + t + 1)
                    r = mm3(ps[:, 4 + t, 0:D], [([v[:, j, t * P:(t + 1) * P] for v in hT], [v[:, j, :] for v in wd])],
                            j == 0, j == HC - 1)
                    if j == HC - 1:
                        r.then_inc(y_done, 1)

            pe.wait_ge(consts, 7)
            pe.wait_ge(rt_lo, 1)
            transposes(0, 0)
            with pe.Fori(0, NB // 2 - 1) as i:
                transposes(i, 1)
                block_logits(i, 0)
                transposes(i + 1, 0)
                block_logits(i, 1)
                for k in range(2):
                    logit_rows(i, k)
            transposes(NB // 2 - 1, 1)
            for k in range(2):
                block_logits(NB // 2 - 1, k)
            logit_rows(NB // 2 - 1, 0)
            logit_rows(NB // 2 - 1, 1).then_inc(logits, 1)

            pe.wait_ge(sh_lo, 2)
            gate_up(0, 0, 0)
            pe.wait_ge(onehot_done, 1)
            pe.matmul(ps[:, RANK, 0:(NT + 1) * E], before[:, :], onehot[:, :, :].rearrange("p i e -> p (i e)"),
                      start=True, stop=False)
            for i in range(NT):
                r = pe.matmul(ps[:, RANK, (i + 1) * E:(NT + 1) * E].rearrange("p (i e) -> p i e", e=E), ones[:, :],
                              onehot[:, i, :].unsqueeze(1).broadcast_to([P, NT - i, E]),
                              start=False, stop=i == NT - 1)
            r.then_inc(rank_done, 1)
            gate_up(0, 0, 1)
            pe.wait_ge(sh_lo, 3)
            pe.wait_ge(rank_read, 1)

            def slot_table():
                pe.wait_ge(place_done, 4)
                for i in range(NT):
                    r = pe.matmul(ps[:, TAB, 0:2 * SC], row1[:, i, :], colv[:, i, :], start=i == 0,
                                  stop=i == NT - 1)
                r.then_inc(table_done, 1)
                pe.wait_ge(table_read, 1)

            def blk(n, k, last, table=False):
                down(n, 0)
                pe.wait_ge(h_done, 4 * n + 1)
                gate_up(n, k, 2)
                down(n, 1)
                pe.wait_ge(h_done, 4 * n + 2)
                gate_up(n, k, 3)
                down(n, 2)
                if not last:
                    pe.wait_ge(h_done, 4 * n + 3)
                    if table:
                        slot_table()
                    gate_up(n + 1, 1 - k, 0)
                down(n, 3)
                if not last:
                    pe.wait_ge(h_done, 4 * n + 4)
                    gate_up(n + 1, 1 - k, 1)

            blk(0, 0, False)
            blk(1, 1, False, table=True)
            with pe.Fori(1, NB // 2 - 1) as i:
                blk(2 * i, 0, False)
                blk(2 * i + 1, 1, False)
            blk(NB - 2, 0, False)
            blk(NB - 1, 1, True)


def routed_experts(nc, comb, W, ident, tg, slot_token, tile_expert, out, E, EW, H, T, ST):
    D = comb.shape[1] // 2
    NC, HC = D // P, H // P
    RING = LOOP = 4
    GU = NC * H
    assert (ST - 3) % LOOP == 0 and HC * D == GU
    with ExitStack() as ctx:
        def sb(name, shape, dt=F32):
            return ctx.enter_context(nc.sbuf_tensor(name, shape, dt))

        def sem(name):
            return ctx.enter_context(nc.semaphore(name))

        rows = [sb(f"rows{i}", [P, 2 * D]) for i in range(RING)]
        gidx = [sb(f"gidx{i}", [P, 1], I32) for i in range(2)]
        sidx = [sb(f"sidx{i}", [P, 1], I32) for i in range(2)]
        w3 = [sb(f"w3_{s}", [P, 2, 2, GU], F32R) for s in ("hi", "lo")]
        wd3 = [sb(f"wd3_{s}", [P, LOOP, GU], F32R) for s in ("hi", "lo")]
        xT = [sb(f"xT3_{s}", [P, 2, NC * P], F32R) for s in ("hi", "lo")]
        sg = sb("sg3", [P, 2, H])
        h = sb("h3", [P, H])
        hT = [sb(f"hT3_{s}", [P, HC * P], F32R) for s in ("hi", "lo")]
        og = [sb(f"og{i}", [P, D]) for i in range(2)]
        ps = ctx.enter_context(nc.psum_tensor("ps3", [P, 8, 512], F32))
        XB, HB, YB = 4, 5, 6
        cleared = sem("cleared")
        g_idx = sem("g_idx"); s_idx = sem("s_idx")
        issue = sem("issue")
        rows_in = [sem(f"rows_in{i}") for i in range(RING)]
        out_sent = [sem(f"out_sent{i}") for i in range(2)]
        w3_hi = [sem(f"w3_hi{m}") for m in range(3)]; w3_lo = [sem(f"w3_lo{m}") for m in range(3)]
        xt_ps = sem("xt3_ps"); xt_hi = sem("xt3_hi"); xt_lo = sem("xt3_lo")
        gate_done = sem("gate3"); up_done = sem("up3"); silu_done = sem("silu3"); h_done = sem("h3_done")
        ht_ps = sem("ht3_ps"); ht_hi = sem("ht3_hi"); ht_lo = sem("ht3_lo"); y_done = sem("y3")
        og_done = sem("og3")
        block = ctx.enter_context(nc.Block())

        def steps(eng, step):
            for i in range(1, 3 + LOOP):
                step(0, i)
            with eng.Fori(1, (ST - 3) // LOOP) as j:
                for r in range(3, 3 + LOOP):
                    step(j, r)

        END = ((ST - 3) // LOOP, 2)

        def later(j, r, n):
            return not isinstance(j, int) or j * LOOP + r >= n

        def expert_at(eng, j, r):
            e = eng.value_load(tile_expert[0:1, bass.ds(j * LOOP + r, 1)], min_val=0, max_val=E - 1)
            return eng.snap(e * EW)

        def raw(at, m):
            if m == 2:
                return W[:, bass.ds(at + 2 * GU, GU)]
            return W[:, bass.ds(at, 2 * GU)].rearrange("p (c m h) -> p c m h", c=NC, m=2)[:, :, m, :]

        def part(s, r, m):
            return wd3[s][:, r % LOOP] if m == 2 else w3[s][:, r % 2, m].rearrange("p (c h) -> p c h", c=NC)

        @block.gpsimd
        def _(pool):
            last_token = pool.to_reg(T - 1)

            def gather(j, r):
                i = j * LOOP + r
                if later(j, r, RING):
                    pool.wait_ge(og_done, i - 3)
                pool.wait_ge(g_idx, i + 1)
                pool.sem_inc(issue, 1)
                pool.indirect_dma_start(rows[r % RING][:, :], None, comb,
                                        bass.IndirectOffsetOnAxis(gidx[r % 2][:, 0:1], 0),
                                        bounds_check=last_token, oob_is_err=False).then_inc(rows_in[r % RING], 16)

            def scatter(j, r):
                i = j * LOOP + r
                pool.wait_ge(s_idx, i + 1)
                pool.wait_ge(og_done, i + 1)
                pool.sem_inc(issue, 1)
                pool.indirect_dma_start(out, bass.IndirectOffsetOnAxis(sidx[r % 2][:, 0:1], 0), og[r % 2][:, :],
                                        None, bounds_check=last_token, oob_is_err=False)\
                    .then_inc(out_sent[r % 2], 16)

            def down_low(j, r):
                at = expert_at(pool, j, r)
                pool.wait_ge(w3_hi[2], j * LOOP + r + 1)
                pool.tensor_tensor(part(1, r, 2), raw(at, 2), part(0, r, 2).bitcast(F32),
                                   ALU.subtract).then_inc(w3_lo[2], 1)

            pool.wait_ge(cleared, RING)
            for i in range(3):
                gather(0, i)

            def step(j, r):
                down_low(j, r)
                gather(j, r + 2)
                if later(j, r, 2):
                    scatter(j, r - 2)

            down_low(0, 0)
            steps(pool, step)
            scatter(END[0], END[1] - 1)
            scatter(*END)
            for k in range(2):
                pool.wait_ge(out_sent[k], 16 * ((ST + 1 - k) // 2))

        @block.scalar
        def _(act):
            def gather_index(j, r):
                i = j * LOOP + r
                if later(j, r, 2):
                    act.wait_ge(rows_in[(r - 2) % RING], 16 * (j * (LOOP // RING) + (r - 2) // RING + 1))
                act.copy(gidx[r % 2][:, :], slot_token[:, bass.ds(i, 1)]).then_inc(g_idx, 1)

            def scatter_index(j, r):
                i = j * LOOP + r
                if later(j, r, 2):
                    act.wait_ge(out_sent[r % 2], 16 * (j * (LOOP // 2) + r // 2))
                act.copy(sidx[r % 2][:, :], slot_token[:, bass.ds(i, 1)]).then_inc(s_idx, 1)

            def weights_high(at, j, r, m):
                i = j * LOOP + r
                if m < 2 and later(j, r, 2):
                    act.wait_ge((gate_done, up_done)[m], i - 1)
                if m == 2 and later(j, r, LOOP):
                    act.wait_ge(y_done, i - 3)
                act.copy(part(0, r, m), raw(at, m)).then_inc(w3_hi[m], 1)

            def rows_high(j, r):
                act.wait_ge(xt_ps, j * LOOP + r + 1)
                act.copy(xT[0][:, r % 2, :], ps[:, XB, 0:NC * P]).then_inc(xt_hi, 1)

            def silu(j, r):
                i = j * LOOP + r
                act.wait_ge(gate_done, i + 1)
                if later(j, r, 2):
                    act.wait_ge(h_done, i - 1)
                act.activation(sg[:, r % 2, :], ps[:, 2 * (r % 2), :], ACT.Silu).then_inc(silu_done, 1)

            def h_high(j, r):
                act.wait_ge(ht_ps, j * LOOP + r + 1)
                act.copy(hT[0][:, :], ps[:, HB, :]).then_inc(ht_hi, 1)

            def step(j, r):
                at = expert_at(act, j, r + 1)
                weights_high(at, j, r + 1, 0)
                if later(j, r, 1):
                    gather_index(j, r + 2)
                if later(j, r, 2):
                    scatter_index(j, r - 2)
                if later(j, r, 1):
                    h_high(j, r - 1)
                silu(j, r)
                rows_high(j, r + 1)
                weights_high(at, j, r + 1, 1)
                weights_high(at, j, r + 1, 2)

            for i in range(2):
                gather_index(0, i)
            at = expert_at(act, 0, 0)
            for m in range(3):
                weights_high(at, 0, 0, m)
            gather_index(0, 2)
            rows_high(0, 0)
            step(0, 0)
            steps(act, step)
            scatter_index(END[0], END[1] - 1)
            h_high(*END)
            scatter_index(*END)

        @block.vector
        def _(dve):
            def weights_low(at, j, r, m):
                dve.wait_ge(w3_hi[m], j * LOOP + r + 1)
                dve.tensor_tensor(part(1, r, m), raw(at, m), part(0, r, m).bitcast(F32),
                                  ALU.subtract).then_inc(w3_lo[m], 1)

            def rows_low(j, r):
                dve.wait_ge(xt_hi, j * LOOP + r + 1)
                dve.tensor_tensor(xT[1][:, r % 2, :], ps[:, XB, 0:NC * P], xT[0][:, r % 2, :].bitcast(F32),
                                  ALU.subtract).then_inc(xt_lo, 1)

            def gated(j, r):
                i = j * LOOP + r
                dve.wait_ge(silu_done, i + 1)
                dve.wait_ge(up_done, i + 1)
                dve.tensor_tensor(h[:, :], ps[:, 2 * (r % 2) + 1, :], sg[:, r % 2, :], ALU.mult).then_inc(h_done, 1)

            def h_low(j, r):
                dve.wait_ge(ht_hi, j * LOOP + r + 1)
                dve.tensor_tensor(hT[1][:, :], ps[:, HB, :], hT[0][:, :].bitcast(F32), ALU.subtract)\
                   .then_inc(ht_lo, 1)

            def add(j, r):
                if later(j, r, 2):
                    dve.wait_ge(out_sent[r % 2], 16 * (j * (LOOP // 2) + r // 2))
                dve.wait_ge(y_done, j * LOOP + r + 1)
                dve.scalar_tensor_tensor(og[r % 2][:, :], ps[:, YB + r % 2, 0:D], tg[:, 0:1],
                                         rows[r % RING][:, D:2 * D], ALU.mult, ALU.add).then_inc(og_done, 1)

            def step(j, r):
                at = expert_at(dve, j, r + 1)
                if later(j, r, 2):
                    add(j, r - 2)
                weights_low(at, j, r + 1, 0)
                if later(j, r, 1):
                    h_low(j, r - 1)
                rows_low(j, r + 1)
                gated(j, r)
                weights_low(at, j, r + 1, 1)

            for i in range(RING):
                dve.memset(rows[i][:, :], 0.0).then_inc(cleared, 1)
            at = expert_at(dve, 0, 0)
            for m in range(2):
                weights_low(at, 0, 0, m)
            rows_low(0, 0)
            step(0, 0)
            steps(dve, step)
            add(END[0], END[1] - 1)
            h_low(*END)
            add(*END)

        @block.tensor
        def _(pe):
            def mm3(out, parts):
                n = 3 * len(parts)
                i = 0
                for a, b in parts:
                    for u, v in ((a[0], b[0]), (a[0], b[1]), (a[1], b[0])):
                        k = pe.matmul(out, u, v, start=i == 0, stop=i == n - 1)
                        i += 1
                return k

            def transposes(j, r):
                pe.wait_ge(rows_in[r % RING], 16 * (j * (LOOP // RING) + r // RING + 1))
                if later(j, r, 1):
                    pe.wait_ge(xt_lo, j * LOOP + r)
                for c in range(NC):
                    k = pe.transpose(ps[:, XB, c * P:(c + 1) * P], rows[r % RING][:, c * P:(c + 1) * P], ident[:, :])
                k.then_inc(xt_ps, 1)

            def product(j, r, m, done):
                pe.wait_ge(w3_lo[m], j * LOOP + r + 1)
                mm3(ps[:, 2 * (r % 2) + m, :],
                    [([v[:, r % 2, c * P:(c + 1) * P] for v in xT], [v[:, r % 2, m, c * H:(c + 1) * H] for v in w3])
                     for c in range(NC)]).then_inc(done, 1)

            def h_transposes(j, r):
                i = j * LOOP + r
                pe.wait_ge(h_done, i + 1)
                if later(j, r, 1):
                    pe.wait_ge(ht_lo, i)
                for c in range(HC):
                    k = pe.transpose(ps[:, HB, c * P:(c + 1) * P], h[:, c * P:(c + 1) * P], ident[:, :])
                k.then_inc(ht_ps, 1)

            def down(j, r):
                i = j * LOOP + r
                pe.wait_ge(w3_lo[2], i + 1)
                pe.wait_ge(ht_lo, i + 1)
                if later(j, r, 2):
                    pe.wait_ge(og_done, i - 1)
                mm3(ps[:, YB + r % 2, 0:D],
                    [([v[:, c * P:(c + 1) * P] for v in hT], [v[:, r % LOOP, c * D:(c + 1) * D] for v in wd3])
                     for c in range(HC)]).then_inc(y_done, 1)

            def step(j, r):
                i = j * LOOP + r
                pe.wait_ge(xt_lo, i + 1)
                if later(j, r, 2):
                    pe.wait_ge(h_done, i - 1)
                product(j, r, 0, gate_done)
                if later(j, r, 1):
                    h_transposes(j, r - 1)
                transposes(j, r + 1)
                product(j, r, 1, up_done)
                if later(j, r, 1):
                    down(j, r - 1)

            transposes(0, 0)
            step(0, 0)
            steps(pe, step)
            h_transposes(*END)
            down(*END)


def program(nc, ins, out, tokens, dim):
    comb = nc.dram_tensor("comb_dram", (tokens, 2 * dim), F32).ap()
    x1 = nc.dram_tensor("x1_dram", (tokens, dim), F32).ap()
    attention(nc, ins['x'], ins['ctx_768'], ins['g_xattn'], ins['L0_xattn_Wq'], ins['L0_xattn_Wk'],
              ins['L0_xattn_Wv'], ins['L0_xattn_Wo'], ins['L0_xattn_bo'], x1, comb[:, 0:dim])
    feed_forward(nc, comb, x1, ins['g_ffn'], ins['L0_ffn_gate'], ins['L0_ffn_up'], ins['L0_ffn_down'],
                 ins['L0_ffn_router'], ins['L0_ffn_w_gate_s'], ins['L0_ffn_w_up_s'], ins['L0_ffn_w_down_s'], out)


_INS = {
    'x': None, 'ctx_768': (0, 2, 1), 'g_xattn': None, 'g_ffn': None,
    'L0_xattn_Wq': None, 'L0_xattn_Wk': None, 'L0_xattn_Wv': None, 'L0_xattn_Wo': None, 'L0_xattn_bo': None,
    'L0_ffn_up': (0, 2, 1), 'L0_ffn_gate': (0, 2, 1), 'L0_ffn_down': (0, 2, 1), 'L0_ffn_router': (1, 0),
    'L0_ffn_w_up_s': (1, 0), 'L0_ffn_w_gate_s': (1, 0), 'L0_ffn_w_down_s': (1, 0),
}


def kernel(**inputs):
    import numpy as _np
    import concourse.bacc as _bacc
    from concourse import mybir as _mybir
    from concourse.bass_utils import run_bass_kernel_spmd as _run

    nc = _bacc.Bacc("TRN2", target_bir_lowering=False, num_devices=1)
    arrays, args = {}, {}
    for name, order in _INS.items():
        a = _np.asarray(inputs[name])
        a = _np.ascontiguousarray(a if order is None else a.transpose(order))
        arrays[f"in_{name}_dram"] = a
        args[name] = nc.dram_tensor(f"in_{name}_dram", a.shape, _mybir.dt.from_np(a.dtype),
                                    kind="ExternalInput").ap()
    shape = inputs['x'].shape
    tokens, dim = shape[0] * shape[1], shape[2]
    out = nc.dram_tensor("out_0_dram", (tokens, dim), _mybir.dt.float32, kind="ExternalOutput").ap()
    program(nc, args, out, tokens, dim)
    r = _run(nc, [arrays], core_ids=[0])
    return r.results[0]["out_0_dram"].reshape(shape)
```
